# Optimizing a Trainium2 kernel written in Bass

```python
import numpy as np
import jax
import jax.numpy as jnp

def _softmax(x, axis=-1):
    return jax.nn.softmax(x, axis=axis)

def _gelu(x):
    return jax.nn.gelu(x, approximate=True)

def _silu(x):
    return jax.nn.silu(x)

def _sigmoid(x):
    return jax.nn.sigmoid(x)

def _layernorm(x, axis=-1, eps=1e-05):
    m = jnp.mean(x, axis=axis, keepdims=True)
    v = jnp.var(x, axis=axis, keepdims=True)
    return (x - m) / jnp.sqrt(v + eps)

def _scatter_add(tgt, idx, src, axis=0):
    return tgt.at[idx].add(src)

def _segment_sum(src, seg, n):
    return jax.ops.segment_sum(src, seg, n)
kernel_name = 'mk_prb_d1_jaxref_r8_6c4d2b'

def setup_inputs(seed: int=0):
    np.random.seed(seed)
    _w = jnp.asarray

    def _L0_attn_setup():
        import jax, jax.numpy as jnp
        import numpy as np
        D_MODEL = 128
        N_HEAD = 16
        HEAD_D = D_MODEL // N_HEAD
        D_FF = 512
        LN_EPS = 1e-05
        ATTN_EPS = 1e-06

        def _layer_norm(x, g, b, eps=LN_EPS):
            mu = jnp.mean(x, axis=-1, keepdims=True)
            var = jnp.var(x, axis=-1, keepdims=True)
            return (x - mu) * jax.lax.rsqrt(var + eps) * g + b

        def _linear_attention(x, qkv_w, qkv_b, out_w, out_b):
            B, N, C = x.shape
            qkv = (x @ qkv_w + qkv_b).reshape(B, N, 3, N_HEAD, HEAD_D)
            qkv = jnp.transpose(qkv, (2, 0, 3, 1, 4))
            q, k, v = (qkv[0], qkv[1], qkv[2])
            qf = jax.nn.elu(q) + 1.0
            kf = jax.nn.elu(k) + 1.0
            kv = jnp.einsum('bhnd,bhne->bhde', kf.astype(jnp.float32), v.astype(jnp.float32)).astype(v.dtype)
            y_num = jnp.einsum('bhnd,bhde->bhne', qf, kv)
            z = jnp.sum(kf.astype(jnp.float32), axis=2)
            y_den = jnp.einsum('bhnd,bhd->bhn', qf, z.astype(qf.dtype))
            y_den = jnp.maximum(y_den, ATTN_EPS)[..., None]
            y = (y_num / y_den).transpose(0, 2, 1, 3).reshape(B, N, C)
            return y @ out_w + out_b
        key = jax.random.key(seed)
        ks = jax.random.split(key, 16)
        s = 0.02
        return {'src': jax.random.normal(ks[0], (4, 512, D_MODEL), dtype=jnp.float32), 'qkv_w': jax.random.normal(ks[1], (D_MODEL, 3 * D_MODEL), dtype=jnp.float32) * s, 'qkv_b': jax.random.normal(ks[2], (3 * D_MODEL,), dtype=jnp.float32) * s, 'out_w': jax.random.normal(ks[3], (D_MODEL, D_MODEL), dtype=jnp.float32) * s, 'out_b': jax.random.normal(ks[4], (D_MODEL,), dtype=jnp.float32) * s, 'w1': jax.random.normal(ks[5], (D_MODEL, D_FF), dtype=jnp.float32) * s, 'b1': jax.random.normal(ks[6], (D_FF,), dtype=jnp.float32) * s, 'w2': jax.random.normal(ks[7], (D_FF, D_MODEL), dtype=jnp.float32) * s, 'b2': jax.random.normal(ks[8], (D_MODEL,), dtype=jnp.float32) * s, 'g1': jnp.ones((D_MODEL,), dtype=jnp.float32), 'be1': jnp.zeros((D_MODEL,), dtype=jnp.float32), 'g2': jnp.ones((D_MODEL,), dtype=jnp.float32), 'be2': jnp.zeros((D_MODEL,), dtype=jnp.float32)}
    _L0_attn_in = _L0_attn_setup()

    def _L0_ffn_setup():
        import jax, jax.numpy as jnp
        import numpy as np
        ALPHA = 1.702
        LIMIT = 9.0
        TOP_K = 2

        def swiglu(x):
            g, v = (x[..., 0::2], x[..., 1::2])
            g = jnp.clip(g, None, LIMIT)
            v = jnp.clip(v, -LIMIT, LIMIT)
            return g * jax.nn.sigmoid(ALPHA * g) * (v + 1)
        key = jax.random.key(seed)
        ks = jax.random.split(key, 6)
        B, L, D = (2, 256, 128)
        E, F = (8, 256)
        s_gate = 1.0 / np.sqrt(D)
        s1 = 1.0 / np.sqrt(D)
        s2 = 1.0 / np.sqrt(F)
        return {'x': jax.random.normal(ks[0], (B, L, D), dtype=jnp.float32), 'gate_w': jax.random.normal(ks[1], (D, E), dtype=jnp.float32) * s_gate, 'dense_1_w': jax.random.normal(ks[2], (E, 2 * F, D), dtype=jnp.float32) * s1, 'dense_1_b': jnp.zeros((E, 2 * F), dtype=jnp.float32), 'dense_2_w': jax.random.normal(ks[3], (E, D, F), dtype=jnp.float32) * s2, 'dense_2_b': jnp.zeros((E, D), dtype=jnp.float32)}
    _L0_ffn_in = _L0_ffn_setup()
    _d = {'L0_attn_src': _L0_attn_in['src'], 'L0_attn_qkv_w': _L0_attn_in['qkv_w'], 'L0_attn_qkv_b': _L0_attn_in['qkv_b'], 'L0_attn_out_w': _L0_attn_in['out_w'], 'L0_attn_out_b': _L0_attn_in['out_b'], 'L0_attn_w1': _L0_attn_in['w1'], 'L0_attn_b1': _L0_attn_in['b1'], 'L0_attn_w2': _L0_attn_in['w2'], 'L0_attn_b2': _L0_attn_in['b2'], 'L0_attn_g1': _L0_attn_in['g1'], 'L0_attn_be1': _L0_attn_in['be1'], 'L0_attn_g2': _L0_attn_in['g2'], 'L0_attn_be2': _L0_attn_in['be2'], 'L0_ffn_gate_w': _L0_ffn_in['gate_w'], 'L0_ffn_dense_1_w': _L0_ffn_in['dense_1_w'], 'L0_ffn_dense_1_b': _L0_ffn_in['dense_1_b'], 'L0_ffn_dense_2_w': _L0_ffn_in['dense_2_w'], 'L0_ffn_dense_2_b': _L0_ffn_in['dense_2_b']}
    _x0 = _d['L0_attn_src']
    _d['L0_attn_src'] = jax.random.normal(jax.random.fold_in(jax.random.key(seed), 1), (8, 1024, 128), dtype=_x0.dtype)
    del _x0
    return _d

def reference(L0_attn_src, L0_attn_qkv_w, L0_attn_qkv_b, L0_attn_out_w, L0_attn_out_b, L0_attn_w1, L0_attn_b1, L0_attn_w2, L0_attn_b2, L0_attn_g1, L0_attn_be1, L0_attn_g2, L0_attn_be2, L0_ffn_gate_w, L0_ffn_dense_1_w, L0_ffn_dense_1_b, L0_ffn_dense_2_w, L0_ffn_dense_2_b):

    def _L0_attn_ref(src, qkv_w, qkv_b, out_w, out_b, w1, b1, w2, b2, g1, be1, g2, be2):
        import jax, jax.numpy as jnp
        import numpy as np
        D_MODEL = 128
        N_HEAD = 16
        HEAD_D = D_MODEL // N_HEAD
        D_FF = 512
        LN_EPS = 1e-05
        ATTN_EPS = 1e-06

        def _layer_norm(x, g, b, eps=LN_EPS):
            mu = jnp.mean(x, axis=-1, keepdims=True)
            var = jnp.var(x, axis=-1, keepdims=True)
            return (x - mu) * jax.lax.rsqrt(var + eps) * g + b

        def _linear_attention(x, qkv_w, qkv_b, out_w, out_b):
            B, N, C = x.shape
            qkv = (x @ qkv_w + qkv_b).reshape(B, N, 3, N_HEAD, HEAD_D)
            qkv = jnp.transpose(qkv, (2, 0, 3, 1, 4))
            q, k, v = (qkv[0], qkv[1], qkv[2])
            qf = jax.nn.elu(q) + 1.0
            kf = jax.nn.elu(k) + 1.0
            kv = jnp.einsum('bhnd,bhne->bhde', kf.astype(jnp.float32), v.astype(jnp.float32)).astype(v.dtype)
            y_num = jnp.einsum('bhnd,bhde->bhne', qf, kv)
            z = jnp.sum(kf.astype(jnp.float32), axis=2)
            y_den = jnp.einsum('bhnd,bhd->bhn', qf, z.astype(qf.dtype))
            y_den = jnp.maximum(y_den, ATTN_EPS)[..., None]
            y = (y_num / y_den).transpose(0, 2, 1, 3).reshape(B, N, C)
            return y @ out_w + out_b
        attn_out = _linear_attention(_layer_norm(src, g1, be1), qkv_w, qkv_b, out_w, out_b)
        x = src + attn_out
        h = jax.nn.gelu(_layer_norm(x, g2, be2) @ w1 + b1, approximate=False)
        return x + h @ w2 + b2

    def _L0_ffn_ref(x, gate_w, dense_1_w, dense_1_b, dense_2_w, dense_2_b):
        import jax, jax.numpy as jnp
        import numpy as np
        ALPHA = 1.702
        LIMIT = 9.0
        TOP_K = 2

        def swiglu(x):
            g, v = (x[..., 0::2], x[..., 1::2])
            g = jnp.clip(g, None, LIMIT)
            v = jnp.clip(v, -LIMIT, LIMIT)
            return g * jax.nn.sigmoid(ALPHA * g) * (v + 1)
        B, L, D = x.shape
        xf = x.reshape(B * L, D)
        gate = xf @ gate_w
        weights, sel = jax.lax.top_k(gate, k=TOP_K)
        weights = jax.nn.softmax(weights, axis=-1)
        h = jnp.einsum('ecd,td->tec', dense_1_w, xf) + dense_1_b[None]
        h = swiglu(h)
        y = jnp.einsum('edf,tef->ted', dense_2_w, h) + dense_2_b[None]
        y_sel = jnp.take_along_axis(y, sel[:, :, None], axis=1)
        out = jnp.einsum('tkd,tk->td', y_sel, weights)
        return out.reshape(B, L, D)
    x = L0_attn_src
    xn = _layernorm(x, axis=-1)
    x = x + _L0_attn_ref(xn, L0_attn_qkv_w, L0_attn_qkv_b, L0_attn_out_w, L0_attn_out_b, L0_attn_w1, L0_attn_b1, L0_attn_w2, L0_attn_b2, L0_attn_g1, L0_attn_be1, L0_attn_g2, L0_attn_be2) + _L0_ffn_ref(xn, L0_ffn_gate_w, L0_ffn_dense_1_w, L0_ffn_dense_1_b, L0_ffn_dense_2_w, L0_ffn_dense_2_b)
    return x

_drawn_inputs = setup_inputs


def setup_inputs(seed=0):
    import zlib

    import numpy as np

    out = dict(_drawn_inputs(seed))
    spreads = {'L0_attn_g1': (1.0, 0.6),
     'L0_attn_be1': (0.0, 0.8),
     'L0_attn_g2': (1.0, 0.6),
     'L0_attn_be2': (0.0, 2.0),
     'L0_ffn_dense_1_b': (0.0, 0.318),
     'L0_ffn_dense_2_b': (0.0, 0.366)}
    factors = {'L0_attn_qkv_w': 8.0,
     'L0_attn_qkv_b': 8.0,
     'L0_attn_out_w': 8.0,
     'L0_attn_out_b': 5.882,
     'L0_attn_b1': 33.173,
     'L0_attn_b2': 5.709}
    for name, (base, spread) in spreads.items():
        noise = np.random.default_rng([zlib.crc32(name.encode()), seed]).standard_normal(out[name].shape)
        drawn = base * np.exp(spread * noise) if base else spread * noise
        out[name] = jnp.asarray(drawn.astype(out[name].dtype))
    for name, factor in factors.items():
        out[name] = (out[name] * factor).astype(out[name].dtype)
    return out
```

```python
from contextlib import ExitStack

import concourse.bass as bass
from concourse import mybir

P = 128
F32 = mybir.dt.float32
BF16 = mybir.dt.bfloat16
U32 = mybir.dt.uint32
I32 = mybir.dt.int32
ALU = mybir.AluOpType
ACT = mybir.ActivationFunctionType
AX_X = mybir.AxisListType.X
PE_E = mybir.EngineType.PE
DVE_E = mybir.EngineType.DVE

LN_EPS = 1e-5
DEN_EPS = 1e-6
LIMIT = 9.0
BIG = 3.0e38


def free_wait(eng, sem, value):
    if isinstance(value, int) and value <= 0:
        return
    eng.wait_ge(sem, value)


def layer_kernel(nc, x, wqkv, wo, w1, w2, wgate, vecs, brow, ew1, eb1, ew2, eb2, out):
    NBATCH, SEQ, D = x.shape
    NE = wgate.shape[1]
    H2 = eb1.shape[1] * eb1.shape[2]
    FE = H2 // 2
    FF = w1.shape[1]
    NF = FF // P
    HD = 8
    NH = D // HD
    TPB = SEQ // P
    NT = NBATCH * TPB
    TOKENS = NBATCH * SEQ
    GT = 4
    NG = NT // GT
    GB = TPB // GT
    W = D + 4
    LT = TOKENS // P + NE - 1
    LP = LT + 5
    NM = 2 * LT
    UN = 8
    EP = 4
    assert D == P and GB == 2 and NG == 16 and NE == 8

    xs = [nc.dram_tensor(f"expert_rows_{k}", (LT * P, W), F32).ap() for k in range(2)]
    ye = [nc.dram_tensor(f"expert_out_{k}", (TOKENS, D), F32).ap() for k in range(2)]
    x_v = x.rearrange("b (p t) d -> p b t d", t=TPB)
    out_v = out.rearrange("b (p t) d -> p b t d", t=TPB)
    ye_v = [y.rearrange("(b p t) d -> p b t d", b=NBATCH, t=TPB) for y in ye]
    xs_v = [s.rearrange("(j p) w -> p j w", p=P) for s in xs]

    with ExitStack() as ctx:
        def sb(name, shape, dt=F32):
            return ctx.enter_context(nc.sbuf_tensor(name, shape, dt))

        def sem(name):
            return ctx.enter_context(nc.semaphore(name))

        x_all = sb("x_all", [P, NT, D])
        xn_rows = sb("xn_rows", [P, NT, W])
        aT_all = sb("aT_all", [P, NT * P])
        wqkv_raw = sb("wqkv_raw", [P, 3 * D])
        wqkv_s = sb("wqkv_s", [P, 3 * D])
        wo_s = sb("wo_s", [P, D])
        w1_raw = sb("w1_raw", [P, FF])
        w1_s = sb("w1_s", [P, FF])
        w2_s = sb("w2_s", [P, NF, D])
        wg_s = sb("wg_s", [P, NE])
        ew2_s = sb("ew2_s", [P, NE, 2, D])
        eb2_s = sb("eb2_s", [P, NE, D])
        cols = sb("cols", [P, 8])
        G1, BE1, G2, BE2 = range(4)
        BQ, NBQ, BQ1, B1 = 0, 1, 2, 4
        vec_raw = sb("vec_raw", [P, 5 + NF])
        be1_wide = sb("be1_wide", [P, P])
        brow_f = sb("brow_f", [P, 4 * D])
        brow_t = sb("brow_t", [P, 3, 4 * D], BF16)
        bias_kv = sb("bias_kv", [P, 2, 2 * D], BF16)
        bias_o = sb("bias_o", [P, GT, D], BF16)
        bias_2 = sb("bias_2", [P, GT, D], BF16)
        row3 = sb("row3", [P, 3])
        ones_b = sb("ones_b", [P, P], BF16)
        upper_b = sb("upper_b", [P, P], BF16)
        ident = sb("ident", [P, P])
        hmask = sb("hmask", [P, D])
        zmask = sb("zmask", [P, NH])
        pad_row = sb("pad_row", [P, W])
        halfm = sb("halfm", [P, 2 * GT])
        stats = sb("stats", [P, 2, GT, 6])
        mv = sb("mv", [P, 2, GT, 2])
        part = sb("part", [P, 4, GT])
        varg = sb("varg", [P, 2, 2, GT])
        rr = sb("rr", [P, 2, 2, GT])
        nbias = sb("nbias", [P, 2, GT])
        inv_r2 = sb("inv_r2", [P, NT])
        aT_g = sb("aT_g", [P, 2, GT * P])
        rev8 = sb("rev8", [P, NE])
        top = sb("top", [P, 8, NT])
        wts = sb("wts", [P, 2, NT])
        slot_f = sb("slot_f", [P, NT])
        slot_u = sb("slot_u", [P, 2, NT], U32)
        cnt = sb("cnt", [P, 12, NE])
        cnt_i = sb("cnt_i", [P, 2, NE], I32)
        jrow = sb("jrow", [P, LP])
        tile_e = sb("tile_e", [P, LP, NE])
        tile_s = sb("tile_s", [P, LP])
        tile_x = sb("tile_x", [P, EP + 2 * LP], U32)
        stage_rows = sb("stage_rows", [P, TPB, W])
        stage_idx = sb("stage_idx", [P, 2, TPB], U32)

        eq = sb("eq", [P, 2, 512])
        ek = sb("ek", [P, 2, GT, D])
        qf = sb("qf", [P, 2, GT * P])
        kf = sb("kf", [P, 2, GT, D])
        vv = sb("vv", [P, 2, GT, D + 1])
        kvz = sb("kvz", [P, D + NH])
        den = sb("den", [P, 2, GT, NH])
        rden = sb("rden", [P, 2, GT, NH])
        ysb = sb("ysb", [P, 2, GT, D])
        yTs = sb("yTs", [P, 2, GT * P])
        x1 = sb("x1", [P, 2, GT, D])
        newt = sb("newt", [P, 6, GT])
        newt_i = sb("newt_i", [P, GT], I32)
        bb = sb("bb", [P, 2, GT, D])
        bTs = sb("bTs", [P, 2, GT * P])
        hh = sb("hh", [P, NF, GT * P])
        tt = sb("tt", [P, GT, D])

        ctx_ps = ctx.enter_context(nc.psum_tensor("banks", [P, 8, 512], F32))
        banks = ctx_ps

        S = {}

        def s(name):
            if name not in S:
                S[name] = sem(name)
            return S[name]

        w_in = s("w_in")
        wide_in = s("wide_in")
        x_in = [s(f"x_in_{p}") for p in range(2)]
        aT_saved = [s(f"aT_saved_{p}") for p in range(2)]
        aT_in = [s(f"aT_in_{p}") for p in range(2)]
        rows_in = [s(f"rows_in_{u}") for u in range(UN)]
        list_dma = [s(f"list_dma_{k}") for k in range(2)]
        back_dma = [s(f"back_dma_{k}") for k in range(2)]
        y_in = [s(f"y_in_{p}") for p in range(2)]
        out_dma = [s(f"out_dma_{p}") for p in range(2)]

        a_t = bb
        small = [hh[:, i, :] for i in range(4)]
        oneh = [kf[:, k].rearrange("p t d -> p (t d)").rearrange("p (c e) -> p c e", e=NE) for k in range(2)]
        oneh_b = [qf[:, k, 0:NT * NE // 2].bitcast(BF16).rearrange("p (c e) -> p c e", e=NE) for k in range(2)]
        gates = ysb[:, 0].rearrange("p t d -> p (t d)").rearrange("p (c e) -> p c e", e=NE)
        bsp = [bTs[:, 0, :], bTs[:, 1, :], yTs[:, 0, :]]
        brow_c = [x1[:, k].rearrange("p t d -> p (t d)") for k in range(2)]
        ew1_s = aT_all[:, 0:NE * H2].rearrange("p (e f) -> p e f", e=NE)
        eb1_s = aT_all[:, NE * H2:2 * NE * H2].rearrange("p (e f) -> p e f", e=NE)
        xg = [xn_rows[:, u, :] for u in range(UN)]
        xTs = [bTs[:, u, 0:P] for u in range(2)]
        hb = [ek[:, u].rearrange("p t d -> p (t d)") for u in range(2)]
        gm = [qf[:, u, 0:FE] for u in range(2)]
        vm = [kf[:, u].rearrange("p t d -> p (t d)")[:, 0:FE] for u in range(2)]
        sg = [eq[:, u, 0:FE] for u in range(2)]
        hs = [ysb[:, u].rearrange("p t d -> p (t d)")[:, 0:FE] for u in range(2)]
        hTs = [yTs[:, u, 0:FE] for u in range(2)]
        yo = [bb[:, u // 2, u % 2, :] for u in range(4)]
        yc = [[aT_all[:, (2 * p + k) * 1024:(2 * p + k + 1) * 1024].rearrange("p (t d) -> p t d", d=D)
               for k in range(2)] for p in range(2)]

        block = ctx.enter_context(nc.Block())

        @block.sync
        def _(sp):
            def x_group(i, par):
                src = x_v[:, i, par * GT:(par + 1) * GT, :] if isinstance(i, int) else \
                    x_v[:, bass.ds(i, 1), par * GT:(par + 1) * GT, :].rearrange("p b t d -> p (b t) d")
                dst = x_all[:, par * GT:(par + 1) * GT, :] if isinstance(i, int) else \
                    x_all[:, bass.ds(i * TPB + par * GT, GT), :]
                sp.dma_start(dst, src).then_inc(x_in[par], 16)

            for par in range(2):
                x_group(0, par)
            loads = [(wqkv_raw[:, :], wqkv), (wo_s[:, :], wo), (w1_raw[:, :], w1),
                     (w2_s[:, :, :], w2.rearrange("(f p) d -> p f d", p=P)), (wg_s[:, :], wgate),
                     (vec_raw[:, :], vecs), (brow_f[:, :], brow.partition_broadcast(P))]
            for dst, src in loads:
                sp.dma_start(dst, src).then_inc(w_in, 16)
            with sp.Fori(1, NBATCH) as i:
                for par in range(2):
                    sp.wait_ge(x_in[par], i * 16)
                    x_group(i, par)
            for par in range(2):
                sp.wait_ge(aT_saved[par], 16 * NBATCH)
            sp.wait_ge(s("gate_done"), NG)

            def attn_in(b, h):
                free_wait(sp, s("kv_done"), 2 * b + h - 1)
                sp.dma_start(aT_g[:, h, :], aT_all[:, bass.ds(b * (TPB * P) + h * GT * P, GT * P)])\
                    .then_inc(aT_in[h], 16)
            for h in range(2):
                attn_in(0, h)
            with sp.Fori(1, NBATCH) as b:
                for h in range(2):
                    attn_in(b, h)

            for h in range(2):
                sp.wait_ge(aT_in[h], 16 * NBATCH)
            sp.dma_start(ew1_s[:, :, :], ew1.rearrange("p e a f -> p e (a f)")).then_inc(wide_in, 16)
            sp.dma_start(ew2_s[:, :, :, :], ew2.rearrange("p e (c d) -> p e c d", c=2)).then_inc(wide_in, 16)
            sp.dma_start(eb1_s[:, :, :].rearrange("p e f -> p (e f)"),
                         eb1.rearrange("e a f -> (e a f)").partition_broadcast(P)).then_inc(wide_in, 16)
            sp.dma_start(eb2_s[:, :, :].rearrange("p e f -> p (e f)"),
                         eb2.rearrange("e d -> (e d)").partition_broadcast(P)).then_inc(wide_in, 16)

            for k in range(2):
                sp.wait_ge(list_dma[k], 16 * (NT + 1))
            sp.wait_ge(s("res_done"), NG)

            def load_rows(i, u):
                n = i * UN + u
                free_wait(sp, back_dma[u % 2], 16 * (i * (UN // 2) + u // 2 - 3))
                j = i * (UN // 2) + u // 2
                src = xs_v[u % 2][:, j, :] if isinstance(i, int) else \
                    xs_v[u % 2][:, bass.ds(j, 1), :].rearrange("p a w -> p (a w)")
                sp.dma_start(xg[u], src).then_inc(rows_in[u], 16)

            for u in range(UN):
                load_rows(0, u)
            with sp.Fori(1, NM // UN) as i:
                for u in range(UN):
                    load_rows(i, u)
            for u in range(NM % UN):
                load_rows(NM // UN, u)

            for k in range(2):
                sp.wait_ge(back_dma[k], 16 * LT)
            sp.wait_ge(s("d1_done"), NM)

            def load_y(b, p):
                free_wait(sp, s("comb_done"), b - 1)
                for k in range(2):
                    src = ye_v[k][:, b] if isinstance(b, int) else \
                        ye_v[k][:, bass.ds(b, 1)].rearrange("p b t d -> p (b t) d")
                    sp.dma_start(yc[p][k], src).then_inc(y_in[p], 16)
            def store(b, p):
                sp.wait_ge(s("comb_done"), b + 1)
                dst = out_v[:, b] if isinstance(b, int) else \
                    out_v[:, bass.ds(b, 1)].rearrange("p b t d -> p (b t) d")
                src = x_all[:, b * TPB:(b + 1) * TPB, :] if isinstance(b, int) else \
                    x_all[:, bass.ds(b * TPB, TPB), :]
                sp.dma_start(dst, src).then_inc(out_dma[p], 16)
            load_y(0, 0)
            load_y(1, 1)
            with sp.Fori(1, NBATCH // 2) as i:
                for p in range(2):
                    store(2 * i - 2 + p, p)
                    load_y(2 * i + p, p)
            for p in range(2):
                store(NBATCH - 2 + p, p)
            for p in range(2):
                sp.wait_ge(out_dma[p], 16 * (NBATCH // 2))

        @block.gpsimd
        def _(pool):
            g = nc.gpsimd
            g.memset(ones_b[:, :], 1.0).then_inc(s("c_ones"), 1)
            g.memset(upper_b[:, :], 1.0).then_inc(s("c_set"), 1)
            g.memset(ident[:, :], 0.0).then_inc(s("c_set"), 1)
            g.memset(hmask[:, :], 1.0).then_inc(s("c_set"), 1)
            g.memset(zmask[:, :], 1.0).then_inc(s("c_set"), 1)
            g.memset(row3[:, :], 1.0).then_inc(s("c_set"), 1)
            g.memset(halfm[:, :], -0.5).then_inc(s("c_set"), 1)
            g.memset(pad_row[:, :], 0.0).then_inc(s("c_set"), 1)
            g.memset(xn_rows[:, :, D:W], 0.0).then_inc(s("c_set"), 1)
            g.memset(vv[:, :, :, D:D + 1], 1.0).then_inc(s("c_vv"), 1)
            g.memset(tile_x[:, 0:EP], 0).then_inc(s("c_set"), 1)
            pool.wait_ge(s("c_set"), 9)
            g.affine_select(out=ident[:, :], in_=ident[:, :], compare_op=ALU.not_equal, fill=1.0, base=0,
                            pattern=[[-1, P]], channel_multiplier=1).then_inc(s("c_ident"), 1)
            g.iota(pad_row[:, D:D + 1].bitcast(I32), pattern=[[0, 1]], base=2 * TOKENS, channel_multiplier=0)\
                .then_inc(s("c_pad"), 1)
            pool.wait_ge(s("c_pad"), 1)
            for k in range(2):
                pool.dma_start(xs_v[k], pad_row[:, :].rearrange("p (a w) -> p a w", a=1).broadcast_to([P, LT, W]))\
                    .then_inc(list_dma[k], 16)
            g.iota(xn_rows[:, :, D:D + 1].bitcast(I32).rearrange("p (b t) a -> p b (t a)", t=TPB),
                   pattern=[[SEQ, NBATCH], [1, TPB]], base=0, channel_multiplier=TPB).then_inc(s("c_ids"), 1)
            g.affine_select(out=upper_b[:, :], in_=upper_b[:, :], compare_op=ALU.is_gt, fill=0.0, base=0,
                            pattern=[[1, P]], channel_multiplier=-1).then_inc(s("c_upper"), 1)
            hm = hmask[:, :].rearrange("p (h e) -> p h e", e=HD)
            g.affine_select(out=hm, in_=hm, compare_op=ALU.is_ge, fill=0.0, base=0,
                            pattern=[[-HD, NH], [0, HD]], channel_multiplier=1).then_inc(s("c_m1"), 1)
            g.affine_select(out=zmask[:, :], in_=zmask[:, :], compare_op=ALU.is_ge, fill=0.0, base=0,
                            pattern=[[-HD, NH]], channel_multiplier=1).then_inc(s("c_m1"), 1)
            g.affine_select(out=row3[:, :], in_=row3[:, :], compare_op=ALU.is_equal, fill=0.0, base=0,
                            pattern=[[-1, 3]], channel_multiplier=1).then_inc(s("c_row3"), 1)
            pool.wait_ge(s("c_m1"), 2)
            g.affine_select(out=hm, in_=hm, compare_op=ALU.is_ge, fill=0.0, base=HD - 1,
                            pattern=[[HD, NH], [0, HD]], channel_multiplier=-1).then_inc(s("c_mask"), 1)
            g.affine_select(out=zmask[:, :], in_=zmask[:, :], compare_op=ALU.is_ge, fill=0.0, base=HD - 1,
                            pattern=[[HD, NH]], channel_multiplier=-1).then_inc(s("c_mask"), 1)
            g.iota(jrow[:, :], pattern=[[1, LP]], base=0, channel_multiplier=0,
                   allow_small_or_imprecise_dtypes=True).then_inc(s("c_j"), 1)
            g.iota(rev8[:, :], pattern=[[-1, NE]], base=NE, channel_multiplier=0,
                   allow_small_or_imprecise_dtypes=True).then_inc(s("c_j"), 1)

            def roots(g_, par):
                pool.wait_ge(s("varg_ready"), g_ + 1)
                free_wait(pool, s("a_ready"), g_ - 1)
                free_wait(pool, s("inv_done"), g_ - 1)
                g.tensor_tensor(rr[:, par].rearrange("p a t -> p (a t)"),
                                varg[:, par].rearrange("p a t -> p (a t)"), halfm[:, :], ALU.pow)\
                    .then_inc(s("rr_ready"), 1)
            for par in range(2):
                roots(par, par)
            with pool.Fori(1, NG // 2) as i:
                for par in range(2):
                    roots(2 * i + par, par)

            def scatter_batch(b):
                pool.wait_ge(s("stage_ready"), b + 1)
                for t in range(TPB):
                    for k in range(2):
                        pool.wait_ge(list_dma[k], 16 * (b * TPB + t + 1))
                        g.indirect_dma_start(
                            xs[k], bass.IndirectOffsetOnAxis(ap=stage_idx[:, k, t:t + 1], axis=0),
                            stage_rows[:, t, :], None)\
                            .then_inc(list_dma[k], 16)
            for b in range(NBATCH):
                scatter_batch(b)

            def scatter_back(i, u):
                n = i * UN + u
                pool.wait_ge(s("y_ready"), n + 1)
                free_wait(pool, back_dma[u % 2], 16 * (i * (UN // 2) + u // 2))
                g.indirect_dma_start(
                    ye[u % 2], bass.IndirectOffsetOnAxis(ap=xg[u][:, D:D + 1].bitcast(U32), axis=0),
                    yo[u % 4], None, bounds_check=TOKENS - 1, oob_is_err=False).then_inc(back_dma[u % 2], 16)
            for n in range(NM):
                scatter_back(n // UN, n % UN)

        @block.scalar
        def _(act):
            a = nc.scalar
            def norm_a(g_, par):
                act.wait_ge(s("nb_ready"), g_ + 1)
                free_wait(act, s("t_done"), g_ - 1)
                for t in range(GT):
                    c = g_ * GT + t
                    src = x_all[:, c, :] if isinstance(c, int) else \
                        x_all[:, bass.ds(c, 1), :].rearrange("p a d -> p (a d)")
                    last = a.activation(a_t[:, par, t, :], src, ACT.Identity,
                                        bias=nbias[:, par, t:t + 1], scale=rr[:, par, 1, t:t + 1])
                last.then_inc(s("a_ready"), 1)

            def evac_a(i, par):
                g_ = 2 * i + par
                act.wait_ge(s("t_done"), g_ + 1)
                free_wait(act, s("gate_done"), g_ - 1)
                free_wait(act, aT_saved[par], 16 * i)
                a.activation(aT_g[:, par, :], banks[:, par, :], ACT.Copy).then_inc(s("aT_ready"), 1)
                act.wait_ge(s("aT_ready"), g_ + 1)
                act.dma_start(aT_all[:, bass.ds(g_ * (GT * P), GT * P)], aT_g[:, par, :])\
                    .then_inc(aT_saved[par], 16)

            for par in range(2):
                norm_a(par, par)
                evac_a(0, par)
            with act.Fori(1, NG // 2) as i:
                for par in range(2):
                    norm_a(2 * i + par, par)
                    evac_a(i, par)

            act.wait_ge(s("gdiff_ready"), 1)
            a.activation(top[:, 4, :], top[:, 3, :], ACT.Exp).then_inc(s("gexp_ready"), 1)

            def elu_parts(b, h):
                gi = 2 * b + h
                act.wait_ge(s("q_done"), gi + 1)
                act.wait_ge(s("cols_ready"), 1)
                bank = 4 if h == 0 else 5
                free_wait(act, s("qf_ready"), gi - 1)
                a.activation(eq[:, h, :], banks[:, bank, :], ACT.Relu, bias=cols[:, NBQ:NBQ + 1], scale=-1.0)\
                    .then_inc(s("qe1"), 1)
                act.wait_ge(s("qe1"), gi + 1)
                a.activation(eq[:, h, :], eq[:, h, :], ACT.Exp, scale=-1.0).then_inc(s("qe_ready"), 1)
                act.wait_ge(s("kv_done"), gi + 1)
                free_wait(act, s("kf_ready"), gi - 1)
                kv = banks[:, 2 * h:2 * h + 2, :].rearrange("p a (c n) -> p (a c) n", n=2 * D)
                a.activation(ek[:, h], kv[:, :, 0:D], ACT.Relu, scale=-1.0).then_inc(s("ke1"), 1)
                free_wait(act, s("kvacc_done"), b)
                a.activation(vv[:, h, :, 0:D], kv[:, :, D:2 * D], ACT.Copy).then_inc(s("v_ready"), 1)
                act.wait_ge(s("ke1"), gi + 1)
                a.activation(ek[:, h], ek[:, h], ACT.Exp, scale=-1.0).then_inc(s("ke_ready"), 1)

            def evac_t(b, k, dst, done, count, bank, user, ucount):
                act.wait_ge(done, count)
                free_wait(act, user, ucount)
                a.activation(dst, banks[:, bank, :], ACT.Copy).then_inc(s("tev"), 1)

            def gelus(b, h):
                gi = 2 * b + h
                free_wait(act, s("w2_done"), gi)
                for f in range(NF):
                    act.wait_ge(s("w1_done"), gi * NF + f + 1)
                    a.activation(hh[:, f, :], banks[:, 4 if f % 2 == 0 else 0, :], ACT.Gelu,
                                 bias=cols[:, B1 + f:B1 + f + 1]).then_inc(s("gelu_done"), 1)

            def act_batch(b, last):
                for h in range(2):
                    evac_t(b, h, yTs[:, h, :], s("yt_done"), 2 * b + h + 1, 5, s("o_done"), 2 * b + h - 1)
                if not last:
                    for h in range(2):
                        elu_parts(b + 1, h)
                evac_t(b, 2, bTs[:, 0, :], s("bt_done"), 2 * b + 1, 1, s("w1_done"), (2 * b - 1) * NF)
                gelus(b, 0)
                evac_t(b, 3, bTs[:, 1, :], s("bt_done"), 2 * b + 2, 5, s("w1_done"), 2 * b * NF)
                gelus(b, 1)

            for h in range(2):
                elu_parts(0, h)
            act_batch(0, False)
            with act.Fori(1, NBATCH - 1) as b:
                act_batch(b, False)
            act_batch(NBATCH - 1, True)

            def evac_x(n, u):
                act.wait_ge(s("xt_done"), n + 1)
                free_wait(act, s("d1_done"), n - 1)
                a.activation(xTs[u % 2], banks[:, u % 2, 0:P], ACT.Copy).then_inc(s("xT_ready"), 1)

            def evac_h(n, u):
                act.wait_ge(s("ht_done"), n + 1)
                free_wait(act, s("d2_done"), n - 1)
                a.activation(hTs[u % 2], banks[:, 4 + u % 2, 0:FE], ACT.Copy).then_inc(s("hT_ready"), 1)

            def swish(n, u):
                act.wait_ge(s("gm_ready"), n + 1)
                free_wait(act, s("hs_ready"), n - 1)
                a.activation(sg[u % 2], gm[u % 2], ACT.Gelu_apprx_sigmoid).then_inc(s("sg_ready"), 1)

            def act_step(n, u):
                if not isinstance(n, int) or n + 1 < NM:
                    evac_x(n + 1, u + 1)
                if not isinstance(n, int) or n >= 2:
                    evac_h(n - 2, u)
                if not isinstance(n, int) or 0 <= n < NM:
                    swish(n, u)
            act_step(-1, -1)
            for u in range(UN):
                act_step(u, u)
            with act.Fori(1, NM // UN) as i:
                for u in range(UN):
                    act_step(UN * i + u, u)
            for n in range(NM // UN * UN, NM + 2):
                act_step(n, n % UN)

        @block.vector
        def _(dve):
            v = nc.vector

            def mean_var(par, done, g_):
                st = [stats[:, par, :, q] for q in range(6)]
                v.tensor_tensor(part[:, 0, :], st[1], st[4], ALU.subtract)
                v.tensor_tensor(part[:, 1, :], st[2], st[5], ALU.add)
                v.tensor_tensor(part[:, 2, :], st[1], st[4], ALU.add).then_inc(done, 1)
                dve.wait_ge(done, 3 * g_ + 1)
                v.scalar_tensor_tensor(part[:, 3, :], part[:, 0, :], 0.25, part[:, 0, :], ALU.mult, ALU.mult)
                v.tensor_scalar(mv[:, par, :, 0], part[:, 2, :], 0.5, None, ALU.mult).then_inc(done, 1)
                dve.wait_ge(done, 3 * g_ + 2)
                v.scalar_tensor_tensor(mv[:, par, :, 1], part[:, 1, :], 1.0 / D, part[:, 3, :],
                                       ALU.mult, ALU.add).then_inc(done, 1)
                dve.wait_ge(done, 3 * g_ + 3)

            def norm_group(i, par):
                g_ = 2 * i + par
                dve.wait_ge(x_in[par], 16 * i + 16)
                def xt(t):
                    c = g_ * GT + t
                    return x_all[:, c, :] if isinstance(c, int) else \
                        x_all[:, bass.ds(c, 1), :].rearrange("p a d -> p (a d)")
                for t in range(GT):
                    last = v.bn_stats(stats[:, par, t, :], xt(t))
                last.then_inc(s("st_ready"), 1)
                dve.wait_ge(s("st_ready"), g_ + 1)
                mean_var(par, s("mv_ready"), g_)
                free_wait(dve, s("rr_ready"), g_ - 1)
                v.tensor_scalar(varg[:, par, 0, :], mv[:, par, :, 1], LN_EPS, None, ALU.add)\
                    .then_inc(s("u_ready"), 1)
                dve.wait_ge(s("u_ready"), g_ + 1)
                v.scalar_tensor_tensor(varg[:, par, 1, :], varg[:, par, 0, :], LN_EPS, mv[:, par, :, 1],
                                       ALU.mult, ALU.add).then_inc(s("varg_ready"), 1)

            def apply_group(i, par):
                g_ = 2 * i + par
                dve.wait_ge(s("rr_ready"), g_ + 1)
                free_wait(dve, s("a_ready"), g_ - 1)
                v.scalar_tensor_tensor(nbias[:, par, :], mv[:, par, :, 0], -1.0, rr[:, par, 1, :],
                                       ALU.mult, ALU.mult).then_inc(s("nb_ready"), 1)
                dve.wait_ge(s("varg_ready"), g_ + 1)
                v.tensor_tensor(newt[:, par, :], varg[:, par, 1, :], rr[:, par, 1, :], ALU.mult)\
                    .then_inc(s("inv1"), 1)
                for t in range(GT):
                    c = g_ * GT + t
                    src = x_all[:, c, :] if isinstance(c, int) else \
                        x_all[:, bass.ds(c, 1), :].rearrange("p a d -> p (a d)")
                    dst = xn_rows[:, c, 0:D] if isinstance(c, int) else \
                        xn_rows[:, bass.ds(c, 1), 0:D].rearrange("p a d -> p (a d)")
                    v.tensor_scalar(dst, src, mv[:, par, t, 0:1], rr[:, par, 0, t:t + 1],
                                    ALU.subtract, ALU.mult).then_inc(s("xn_done"), 1)
                dve.wait_ge(s("inv1"), g_ + 1)
                dst = inv_r2[:, bass.ds(g_ * GT, GT)] if not isinstance(g_, int) else \
                    inv_r2[:, g_ * GT:(g_ + 1) * GT]
                v.tensor_tensor(dst, newt[:, par, :], rr[:, par, 0, :], ALU.mult).then_inc(s("inv_done"), 1)

            def take_gates(i, par):
                g_ = 2 * i + par
                dve.wait_ge(s("gate_done"), g_ + 1)
                dst = gates[:, bass.ds(g_ * GT, GT), :] if not isinstance(g_, int) else \
                    gates[:, g_ * GT:(g_ + 1) * GT, :]
                v.tensor_copy(dst, banks[:, 2 + par, 0:GT * NE].rearrange("p (t e) -> p t e", e=NE))\
                    .then_inc(s("gates_ready"), 1)

            dve.wait_ge(w_in, 16 * 7)
            v.tensor_scalar(wqkv_s[:, :], wqkv_raw[:, :], vec_raw[:, G1:G1 + 1], None, ALU.mult)\
                .then_inc(s("ws_ready"), 1)
            v.tensor_scalar(w1_s[:, :], w1_raw[:, :], vec_raw[:, G2:G2 + 1], None, ALU.mult)\
                .then_inc(s("ws_ready"), 1)
            dve.wait_ge(s("c_ones"), 1)
            v.tensor_scalar(be1_wide[:, :], ones_b[:, :], vec_raw[:, BE1:BE1 + 1], None, ALU.mult)\
                .then_inc(s("be_ready"), 1)
            norm_group(0, 0)
            norm_group(0, 1)
            dve.wait_ge(s("fold_done"), 1)
            v.tensor_tensor(brow_f[:, 0:2 * D], banks[:, 6, 0:2 * D], brow_f[:, 0:2 * D], ALU.add)\
                .then_inc(s("fold1"), 1)
            v.tensor_tensor(cols[:, BQ:BQ + 1], banks[:, 7, 0:1], vec_raw[:, 4:5], ALU.add).then_inc(s("fold1"), 1)
            v.tensor_tensor(cols[:, B1:B1 + NF], banks[:, 7, 1:1 + NF], vec_raw[:, 5:5 + NF], ALU.add)\
                .then_inc(s("fold1"), 1)
            dve.wait_ge(s("fold1"), 3)
            v.tensor_scalar(cols[:, BQ1:BQ1 + 1], cols[:, BQ:BQ + 1], 1.0, None, ALU.add).then_inc(s("fold2"), 1)
            v.tensor_scalar(cols[:, NBQ:NBQ + 1], cols[:, BQ:BQ + 1], -1.0, None, ALU.mult)\
                .then_inc(s("cols_ready"), 1)
            v.tensor_copy(brow_t[:, 0, :], brow_f[:, :]).then_inc(s("sp"), 1)
            dve.wait_ge(s("sp"), 1)
            v.tensor_tensor(bsp[0], brow_f[:, :], brow_t[:, 0, :], ALU.subtract).then_inc(s("sp"), 1)
            dve.wait_ge(s("sp"), 2)
            v.tensor_copy(brow_t[:, 1, :], bsp[0]).then_inc(s("sp"), 1)
            dve.wait_ge(s("sp"), 3)
            v.tensor_tensor(bsp[1], bsp[0], brow_t[:, 1, :], ALU.subtract).then_inc(s("sp"), 1)
            dve.wait_ge(s("c_row3"), 1)
            v.tensor_scalar(brow_c[0], brow_t[:, 0, :], row3[:, 0:1], None, ALU.mult).then_inc(s("sp"), 1)
            dve.wait_ge(s("sp"), 5)
            v.scalar_tensor_tensor(brow_c[1], brow_t[:, 1, :], row3[:, 1:2], brow_c[0],
                                   ALU.mult, ALU.add).then_inc(s("sp"), 1)
            dve.wait_ge(s("sp"), 6)
            v.scalar_tensor_tensor(bsp[2], bsp[1], row3[:, 2:3], brow_c[1],
                                   ALU.mult, ALU.add).then_inc(s("sp"), 1)
            dve.wait_ge(s("sp"), 7)
            for c in range(2):
                v.tensor_copy(bias_kv[:, c, :], bsp[2][:, 0:2 * D]).then_inc(s("bias_ready"), 1)
            for c in range(GT):
                v.tensor_copy(bias_o[:, c, :], bsp[2][:, 2 * D:3 * D]).then_inc(s("bias_ready"), 1)
                v.tensor_copy(bias_2[:, c, :], bsp[2][:, 3 * D:4 * D]).then_inc(s("bias_ready"), 1)

            apply_group(0, 0)
            apply_group(0, 1)
            with dve.Fori(1, NBATCH) as i:
                for par in range(2):
                    norm_group(i, par)
                for par in range(2):
                    take_gates(i - 1, par)
                for par in range(2):
                    apply_group(i, par)
            for par in range(2):
                take_gates(NBATCH - 1, par)

            rt = [0]

            def link(ins):
                rt[0] += 1
                ins.then_inc(s("route_step"), 1)
                dve.wait_ge(s("route_step"), rt[0])

            link(v.memset(small[3], 0.0))
            link(v.memset(cnt[:, 5, :], 0.0))
            dve.wait_ge(s("gates_ready"), NG)
            dve.wait_ge(s("c_j"), 2)
            V3 = [t_.rearrange("p (c e) -> p c e", e=NE) for t_ in small]
            ET = [t_.rearrange("p (e c) -> p e c", c=NT) for t_ in small]
            rev_b = rev8[:, :].rearrange("p (a e) -> p a e", a=1).broadcast_to([P, NT, NE])

            def wide(col):
                return col.rearrange("p (c a) -> p c a", a=1).broadcast_to([P, NT, NE])

            src = gates[:, :, :]
            for k in range(2):
                link(v.tensor_reduce(top[:, k, :], src, AX_X, ALU.max))
                link(v.tensor_tensor(V3[0], src, wide(top[:, k, :]), ALU.is_equal))
                link(v.tensor_tensor(V3[1], V3[0], rev_b, ALU.mult))
                link(v.tensor_reduce(top[:, 2, :], V3[1], AX_X, ALU.max))
                link(v.tensor_tensor(oneh[k][:, :, :], V3[1], wide(top[:, 2, :]), ALU.is_equal))
                v.tensor_copy(oneh_b[k][:, :, :], oneh[k][:, :, :]).then_inc(s("oneh_ready"), 1)
                if k == 0:
                    link(v.scalar_tensor_tensor(V3[2], oneh[0][:, :, :], -BIG, gates[:, :, :], ALU.mult, ALU.add))
                    src = V3[2]
            link(v.tensor_tensor(top[:, 5, :], top[:, 1, :], top[:, 0, :], ALU.subtract))
            v.tensor_tensor(top[:, 3, :], top[:, 5, :], inv_r2[:, :], ALU.mult).then_inc(s("gdiff_ready"), 1)
            for k in range(2):
                dve.wait_ge(s("rank_done"), k + 1)
                tot = banks[:, 4 + 2 * k + 1, :].rearrange("p (c e) -> p e c", e=NE)
                link(v.tensor_copy(ET[0], tot))
                link(v.tensor_tensor_scan(small[1], small[0], small[3], 0.0, ALU.add, ALU.add))
                last_c = ET[1][:, :, NT - 1]
                link(v.tensor_copy(cnt[:, 0, :], last_c))
                link(v.tensor_copy(cnt[:, 1, 0:1], cnt[:, 0, 0:1]))
                link(v.tensor_tensor(cnt[:, 1, 1:NE], cnt[:, 0, 1:NE], cnt[:, 0, 0:NE - 1], ALU.subtract))
                link(v.tensor_scalar(cnt_i[:, 0, :], cnt[:, 1, :], float(P - 1), None, ALU.add))
                link(v.tensor_scalar(cnt_i[:, 1, :], cnt_i[:, 0, :], 7, None, ALU.arith_shift_right))
                link(v.tensor_copy(cnt[:, 2, :], cnt_i[:, 1, :]))
                link(v.tensor_tensor_scan(cnt[:, 3, :], cnt[:, 2, :], cnt[:, 5, :], 0.0, ALU.add, ALU.add))
                link(v.tensor_tensor(cnt[:, 6, :], cnt[:, 3, :], cnt[:, 2, :], ALU.subtract))
                link(v.tensor_tensor(cnt[:, 7, :], cnt[:, 1, :], cnt[:, 0, :], ALU.subtract))
                link(v.scalar_tensor_tensor(cnt[:, 4, :], cnt[:, 6, :], float(P), cnt[:, 7, :],
                                            ALU.mult, ALU.add))
                link(v.tensor_tensor(ET[1], ET[1], ET[0], ALU.subtract))
                link(v.tensor_tensor(ET[1], ET[1],
                                     cnt[:, 4, :].rearrange("p (e a) -> p e a", a=1).broadcast_to([P, NE, NT]),
                                     ALU.add))
                link(v.tensor_tensor(V3[0], banks[:, 4 + 2 * k, :].rearrange("p (c e) -> p c e", e=NE),
                                     small[1].rearrange("p (e c) -> p c e", c=NT), ALU.add))
                link(v.tensor_tensor(V3[2], V3[0], oneh[k][:, :, :], ALU.mult))
                link(v.tensor_reduce(slot_f[:, :], V3[2], AX_X, ALU.add))
                v.tensor_copy(slot_u[:, k, :], slot_f[:, :]).then_inc(s("slots_ready"), 1)
                link(v.tensor_tensor(
                    tile_e[:, :, :],
                    jrow[:, :].rearrange("p (j a) -> p j a", a=1).broadcast_to([P, LP, NE]),
                    cnt[:, 3, :].rearrange("p (a e) -> p a e", a=1).broadcast_to([P, LP, NE]), ALU.is_ge))
                link(v.tensor_reduce(tile_s[:, :], tile_e[:, :, :], AX_X, ALU.add))
                v.tensor_scalar(tile_x[:, EP:].rearrange("p (j k) -> p j k", k=2)[:, :, k], tile_s[:, :],
                                float(NE - 1), None, ALU.min).then_inc(s("tile_x_ready"), 1)
            dve.wait_ge(s("gexp_ready"), 1)
            link(v.tensor_scalar(top[:, 6, :], top[:, 4, :], 1.0, None, ALU.add))
            link(v.reciprocal(wts[:, 0, :], top[:, 6, :]))
            link(v.tensor_tensor(wts[:, 1, :], wts[:, 0, :], top[:, 4, :], ALU.mult))

            def stage_batch(b):
                for k in range(2):
                    free_wait(dve, list_dma[k], 16 * (b * TPB + 1) if not isinstance(b, int) or b else 0)
                rows = xn_rows[:, bass.ds(b * TPB, TPB), :]
                v.tensor_copy(stage_rows[:, :, :], rows)
                v.tensor_copy(stage_idx[:, :, :], slot_u[:, :, bass.ds(b * TPB, TPB)])\
                    .then_inc(s("stage_ready"), 1)

            def feature(b, h):
                gi = 2 * b + h
                dve.wait_ge(s("qe_ready"), gi + 1)
                free_wait(dve, s("y_mm_done"), gi - 1)
                v.scalar_tensor_tensor(qf[:, h, :], banks[:, 4 if h == 0 else 5, :], cols[:, BQ1:BQ1 + 1],
                                       eq[:, h, :], ALU.add, ALU.max).then_inc(s("qf_ready"), 1)
                dve.wait_ge(s("ke_ready"), gi + 1)
                dve.wait_ge(s("v_ready"), gi + 1)
                free_wait(dve, s("kvacc_done"), b)
                kv = banks[:, 2 * h:2 * h + 2, :].rearrange("p a (c n) -> p (a c) n", n=2 * D)
                v.scalar_tensor_tensor(kf[:, h], kv[:, :, 0:D], 1.0, ek[:, h], ALU.add, ALU.max)\
                    .then_inc(s("kf_ready"), 1)

            def mask_kv(b):
                dve.wait_ge(s("kvacc_done"), b + 1)
                free_wait(dve, s("y_mm_done"), 2 * b)
                v.tensor_tensor(kvz[:, 0:D], banks[:, 7, 0:D], hmask[:, :], ALU.mult)
                v.tensor_scalar(kvz[:, D:D + NH], zmask[:, :], banks[:, 7, D:D + 1], None, ALU.mult)\
                    .then_inc(s("kvz_ready"), 1)

            def divide(b, h):
                gi = 2 * b + h
                dve.wait_ge(s("y_mm_done"), gi + 1)
                Y = banks[:, 2 * h:2 * h + 2, :].rearrange("p a (c n) -> p (a c) n", n=256)
                v.tensor_scalar(den[:, h], Y[:, :, D:D + NH], DEN_EPS, None, ALU.max).then_inc(s("den1"), 1)
                dve.wait_ge(s("den1"), gi + 1)
                v.reciprocal(rden[:, h], den[:, h]).then_inc(s("den2"), 1)
                dve.wait_ge(s("den2"), gi + 1)
                free_wait(dve, s("yt_done"), gi - 1)
                v.tensor_tensor(
                    ysb[:, h].rearrange("p c (m e) -> p c m e", e=HD),
                    Y[:, :, 0:D].rearrange("p c (m e) -> p c m e", e=HD),
                    rden[:, h].rearrange("p c (m a) -> p c m a", a=1).broadcast_to([P, GT, NH, HD]),
                    ALU.mult).then_inc(s("ynorm_done"), 1)

            def second_norm(b, h):
                gi = 2 * b + h
                N = 12
                dve.wait_ge(s("o_done"), gi + 1)
                v.tensor_tensor(x1[:, h], banks[:, 6, :].rearrange("p (t d) -> p t d", d=D),
                                xn_rows[:, bass.ds(gi * GT, GT), 0:D], ALU.add).then_inc(s("x1_ready"), 1)
                dve.wait_ge(s("x1_ready"), gi + 1)
                for t in range(GT):
                    last = v.bn_stats(stats[:, h, t, :], x1[:, h, t, :])
                last.then_inc(s("st2"), 1)
                dve.wait_ge(s("st2"), gi + 1)
                mean_var(h, s("mv2"), gi)
                step = s("newton")
                base = gi * N
                k = [0]

                def nl(ins):
                    k[0] += 1
                    ins.then_inc(step, 1)
                    dve.wait_ge(step, base + k[0])
                va = newt[:, 0, :]
                nl(v.tensor_scalar(va, mv[:, h, :, 1], LN_EPS, None, ALU.add))
                nl(v.tensor_scalar(newt_i[:, :], va.bitcast(I32), 1, None, ALU.arith_shift_right))
                nl(v.tensor_scalar(newt[:, 1, :].bitcast(I32), newt_i[:, :], -1.0, float(0x5F3759DF),
                                   ALU.mult, ALU.add))
                cur = 1
                for it in range(3):
                    y = newt[:, cur, :]
                    nxt = 3 - cur
                    nl(v.tensor_tensor(newt[:, 3, :], y, y, ALU.mult))
                    nl(v.scalar_tensor_tensor(newt[:, 4, :], newt[:, 3, :], -0.5, va, ALU.mult, ALU.mult))
                    nl(v.scalar_tensor_tensor(newt[:, nxt, :], newt[:, 4, :], 1.5, y, ALU.add, ALU.mult))
                    cur = nxt
                assert k[0] == N
                free_wait(dve, s("bt_done"), gi - 1)
                for t in range(GT):
                    last = v.tensor_scalar(bb[:, h, t, :], x1[:, h, t, :], mv[:, h, t, 0:1],
                                           newt[:, cur, t:t + 1], ALU.subtract, ALU.mult)
                last.then_inc(s("bb_ready"), 1)

            def residual(b, h):
                gi = 2 * b + h
                dve.wait_ge(s("w2_done"), gi + 1)
                free_wait(dve, s("res_done"), gi)
                v.tensor_tensor(tt[:, :, :], banks[:, 6, :].rearrange("p (t d) -> p t d", d=D), x1[:, h], ALU.add)\
                    .then_inc(s("rt_done"), 1)
                dve.wait_ge(s("rt_done"), gi + 1)
                xs_ = x_all[:, bass.ds(gi * GT, GT), :]
                v.tensor_tensor(xs_, xs_, tt[:, :, :], ALU.add).then_inc(s("res_done"), 1)

            def dve_batch(b, last):
                stage_batch(b)
                for h in range(2):
                    divide(b, h)
                for h in range(2):
                    second_norm(b, h)
                    if not last:
                        feature(b + 1, h)
                if not last:
                    mask_kv(b + 1)
                for h in range(2):
                    residual(b, h)

            for h in range(2):
                feature(0, h)
            dve.wait_ge(s("c_mask"), 2)
            mask_kv(0)
            dve_batch(0, False)
            with dve.Fori(1, NBATCH - 1) as b:
                dve_batch(b, False)
            dve_batch(NBATCH - 1, True)

            def add_bias(n, u, e):
                dve.wait_ge(s("d1_done"), n + 1)
                free_wait(dve, s("sg_ready"), n - 1)
                v.tensor_tensor(hb[u % 2], banks[:, 2 + u % 2, :],
                                eb1_s[:, bass.ds(e, 1), :].rearrange("p a f -> p (a f)"), ALU.add)\
                    .then_inc(s("hb_ready"), 1)
                dve.wait_ge(s("hb_ready"), n + 1)
                v.tensor_scalar(gm[u % 2], hb[u % 2][:, 0:FE], LIMIT, None, ALU.min).then_inc(s("gm_ready"), 1)
                v.tensor_scalar(vm[u % 2], hb[u % 2][:, FE:H2], LIMIT, -LIMIT, ALU.min, ALU.max)\
                    .then_inc(s("vm_ready"), 1)

            def gate_up(n, u):
                dve.wait_ge(s("sg_ready"), n + 1)
                dve.wait_ge(s("vm_ready"), n + 1)
                free_wait(dve, s("ht_done"), n - 1)
                v.scalar_tensor_tensor(hs[u % 2], vm[u % 2], 1.0, sg[u % 2], ALU.add, ALU.mult)\
                    .then_inc(s("hs_ready"), 1)

            dve.wait_ge(s("tile_x_ready"), 2)
            dve.wait_ge(wide_in, 64)

            def dve_block(i, steps):
                _, ev = nc.values_load_multi_w_load_instructions(
                    tile_x[0:1, bass.ds(i * UN, UN + EP)] if not isinstance(i, int)
                    else tile_x[0:1, i * UN:i * UN + UN + EP],
                    engines=[DVE_E], min_val=0, max_val=NE - 1,
                    skip_runtime_bounds_check_because="written as min(count, NE - 1)")
                for u in steps:
                    n = i * UN + u
                    known = isinstance(i, int)
                    if not known or n < NM:
                        add_bias(n, u % UN, ev[EP + u])
                    if not known or 1 <= n < NM + 1:
                        gate_up(n - 1, (u - 1) % UN)
                    if not known or n >= 3:
                        m, mu = n - 3, (u - 3) % UN
                        dve.wait_ge(s("d2_done"), m + 1)
                        half = (i * UN + u - 3 - (mu % 2)) // 2 if known else i * (UN // 2) + (u - 3 - (mu % 2)) // 2
                        free_wait(dve, back_dma[mu % 2], 16 * (half - 1))
                        v.tensor_tensor(yo[mu % 4], banks[:, 6 + mu % 2, 0:D],
                                        eb2_s[:, bass.ds(ev[EP + u - 3], 1), :].rearrange("p a f -> p (a f)"),
                                        ALU.add).then_inc(s("y_ready"), 1)

            dve_block(0, range(UN))
            with dve.Fori(1, NM // UN) as i:
                dve_block(i, range(UN))
            dve_block(NM // UN, range(NM % UN + 3 if NM % UN + 3 <= UN else UN))
            if NM % UN + 3 > UN:
                dve_block(NM // UN + 1, range(NM % UN + 3 - UN))

            def combine(b, p, i):
                dve.wait_ge(y_in[p], 32 * i + 32)
                for k in range(2):
                    for t in range(TPB):
                        c = b * TPB + t
                        xr = x_all[:, bass.ds(c, 1), :].rearrange("p a d -> p (a d)")
                        last = v.scalar_tensor_tensor(xr, yc[p][k][:, t, :], wts[:, k, bass.ds(c, 1)], xr,
                                                      ALU.mult, ALU.add)
                        if k == 0:
                            last.then_inc(s("comb_half"), 1)
                    if k == 0:
                        dve.wait_ge(s("comb_half"), (b + 1) * TPB)
                last.then_inc(s("comb_done"), 1)
            with dve.Fori(0, NBATCH // 2) as i:
                for p in range(2):
                    combine(2 * i + p, p, i)

        @block.tensor
        def _(pe):
            mm = nc.tensor.matmul
            tr = nc.tensor.transpose

            pe.wait_ge(w_in, 16 * 7)
            pe.wait_ge(s("be_ready"), 1)
            mm(banks[:, 6, 0:2 * D], be1_wide[:, :], wqkv_raw[:, D:3 * D], start=True, stop=True)
            mm(banks[:, 7, 0:1], wqkv_raw[:, 0:D], vec_raw[:, BE1:BE1 + 1], start=True, stop=True)
            for f in range(NF):
                last = mm(banks[:, 7, 1 + f:2 + f], w1_raw[:, f * P:(f + 1) * P], vec_raw[:, BE2:BE2 + 1],
                          start=True, stop=True)
            last.then_inc(s("fold_done"), 1)

            def trans_a(g_, par):
                pe.wait_ge(s("a_ready"), g_ + 1)
                free_wait(pe, s("aT_ready"), g_ - 1)
                for t in range(GT):
                    last = tr(banks[:, par, t * P:(t + 1) * P], a_t[:, par, t, :], ident[:, :])
                last.then_inc(s("t_done"), 1)

            def gate(g_, par):
                pe.wait_ge(s("aT_ready"), g_ + 1)
                free_wait(pe, s("gates_ready"), g_ - 1)
                for t in range(GT):
                    last = mm(banks[:, 2 + par, t * NE:(t + 1) * NE], aT_g[:, par, t * P:(t + 1) * P], wg_s[:, :],
                              start=True, stop=True)
                last.then_inc(s("gate_done"), 1)
            pe.wait_ge(s("c_ident"), 1)
            for par in range(2):
                trans_a(par, par)
                gate(par, par)
            with pe.Fori(1, NG // 2) as i:
                for par in range(2):
                    trans_a(2 * i + par, par)
                    gate(2 * i + par, par)

            pe.wait_ge(s("c_upper"), 1)
            pe.wait_ge(s("cols_ready"), 1)
            for k in range(2):
                pe.wait_ge(s("oneh_ready"), k + 1)
                oh = oneh_b[k][:, :, :].rearrange("p c e -> p (c e)")
                mm(banks[:, 4 + 2 * k, :], upper_b[:, :], oh, start=True, stop=True)
                mm(banks[:, 5 + 2 * k, :], ones_b[:, :], oh, start=True, stop=True).then_inc(s("rank_done"), 1)

            def project(b, h):
                gi = 2 * b + h
                pe.wait_ge(aT_in[h], 16 * b + 16)
                if h == 0:
                    free_wait(pe, s("gelu_done"), 2 * (b - 1) * NF)
                else:
                    free_wait(pe, s("tev"), 4 * (b - 1) + 2)
                mm(banks[:, 4 if h == 0 else 5, :], wqkv_s[:, 0:D], aT_g[:, h, :], start=True, stop=True)\
                    .then_inc(s("q_done"), 1)
                free_wait(pe, s("ynorm_done"), gi - 1)
                for a_ in range(2):
                    bank = 2 * h + a_
                    mm(banks[:, bank, :], ones_b[:, :], bias_kv[:, :, :].rearrange("p c n -> p (c n)"),
                       start=True, stop=False)
                    for c in range(2):
                        t = 2 * a_ + c
                        last = mm(banks[:, bank, c * 2 * D:(c + 1) * 2 * D], aT_g[:, h, t * P:(t + 1) * P],
                                  wqkv_s[:, D:3 * D], start=False, stop=(c == 1))
                last.then_inc(s("kv_done"), 1)

            def kv_acc(b):
                pe.wait_ge(s("kf_ready"), 2 * b + 2)
                pe.wait_ge(s("v_ready"), 2 * b + 2)
                free_wait(pe, s("kvz_ready"), b)
                for h in range(2):
                    for t in range(GT):
                        last = mm(banks[:, 7, 0:D + 1], kf[:, h, t, :], vv[:, h, t, :],
                                  start=(h == 0 and t == 0), stop=(h == 1 and t == GT - 1))
                last.then_inc(s("kvacc_done"), 1)

            def attend(b, h):
                gi = 2 * b + h
                pe.wait_ge(s("kvz_ready"), b + 1)
                pe.wait_ge(s("qf_ready"), gi + 1)
                free_wait(pe, s("gelu_done"), 2 * b * NF)
                if h == 0:
                    free_wait(pe, s("tev"), 4 * b)
                for t in range(GT):
                    last = mm(banks[:, 2 * h + t // 2, (t % 2) * 256:(t % 2) * 256 + D + NH],
                              qf[:, h, t * P:(t + 1) * P], kvz[:, :], start=True, stop=True)
                last.then_inc(s("y_mm_done"), 1)

            def trans_y(b, h):
                pe.wait_ge(s("ynorm_done"), 2 * b + h + 1)
                free_wait(pe, s("tev"), 4 * b + h)
                for t in range(GT):
                    last = tr(banks[:, 5, t * P:(t + 1) * P], ysb[:, h, t, :], ident[:, :])
                last.then_inc(s("yt_done"), 1)

            def out_proj(b, h):
                gi = 2 * b + h
                pe.wait_ge(s("tev"), 4 * b + h + 1)
                if h == 0:
                    free_wait(pe, s("rt_done"), 2 * b)
                else:
                    pe.wait_ge(s("x1_ready"), gi)
                mm(banks[:, 6, :], ones_b[:, :], bias_o[:, :, :].rearrange("p c n -> p (c n)"),
                   start=True, stop=False)
                for t in range(GT):
                    last = mm(banks[:, 6, t * D:(t + 1) * D], yTs[:, h, t * P:(t + 1) * P], wo_s[:, :],
                              start=False, stop=(t == GT - 1))
                last.then_inc(s("o_done"), 1)

            def trans_b(b, h, last_batch):
                gi = 2 * b + h
                pe.wait_ge(s("bb_ready"), gi + 1)
                if not last_batch:
                    if h == 0:
                        pe.wait_ge(s("kf_ready"), 2 * b + 3)
                    else:
                        pe.wait_ge(s("qf_ready"), 2 * b + 4)
                bank = 1 if h == 0 else 5
                for t in range(GT):
                    last = tr(banks[:, bank, t * P:(t + 1) * P], bb[:, h, t, :], ident[:, :])
                last.then_inc(s("bt_done"), 1)

            def ff_up(b, h, last_batch):
                gi = 2 * b + h
                pe.wait_ge(s("tev"), 4 * b + h + 3)
                if not last_batch and h == 0:
                    pe.wait_ge(s("qf_ready"), 2 * b + 3)
                    pe.wait_ge(s("kf_ready"), 2 * b + 3)
                for f in range(NF):
                    free_wait(pe, s("gelu_done"), gi * NF + f - 1)
                    mm(banks[:, 4 if f % 2 == 0 else 0, :], w1_s[:, f * P:(f + 1) * P], bTs[:, h, :],
                       start=True, stop=True).then_inc(s("w1_done"), 1)

            def ff_down(b, h):
                gi = 2 * b + h
                if h == 0:
                    pe.wait_ge(s("x1_ready"), 2 * b + 2)
                else:
                    pe.wait_ge(s("rt_done"), gi)
                mm(banks[:, 6, :], ones_b[:, :], bias_2[:, :, :].rearrange("p c n -> p (c n)"),
                   start=True, stop=False)
                for f in range(NF):
                    pe.wait_ge(s("gelu_done"), gi * NF + f + 1)
                    for t in range(GT):
                        last = mm(banks[:, 6, t * D:(t + 1) * D], hh[:, f, t * P:(t + 1) * P], w2_s[:, f, :],
                                  start=False, stop=(f == NF - 1 and t == GT - 1))
                last.then_inc(s("w2_done"), 1)

            def pe_batch(b, last):
                for h in range(2):
                    attend(b, h)
                for h in range(2):
                    trans_y(b, h)
                for h in range(2):
                    out_proj(b, h)
                if not last:
                    for h in range(2):
                        project(b + 1, h)
                trans_b(b, 0, last)
                ff_up(b, 0, last)
                trans_b(b, 1, last)
                if not last:
                    kv_acc(b + 1)
                ff_down(b, 0)
                ff_up(b, 1, last)
                ff_down(b, 1)

            pe.wait_ge(s("ws_ready"), 2)
            pe.wait_ge(s("bias_ready"), 10)
            pe.wait_ge(s("gates_ready"), NG)
            pe.wait_ge(s("slots_ready"), 2)
            pe.wait_ge(s("c_vv"), 1)
            for h in range(2):
                project(0, h)
            kv_acc(0)
            pe_batch(0, False)
            with pe.Fori(1, NBATCH - 1) as b:
                pe_batch(b, False)
            pe_batch(NBATCH - 1, True)

            pe.wait_ge(s("res_done"), NG)
            pe.wait_ge(s("tile_x_ready"), 2)
            pe.wait_ge(wide_in, 64)

            def pe_block(i, steps):
                known = isinstance(i, int)
                _, ev = nc.values_load_multi_w_load_instructions(
                    tile_x[0:1, i * UN:i * UN + UN + EP] if known else tile_x[0:1, bass.ds(i * UN, UN + EP)],
                    engines=[PE_E], min_val=0, max_val=NE - 1,
                    skip_runtime_bounds_check_because="written as min(count, NE - 1)")
                for u in steps:
                    n = i * UN + u
                    if not known or n + 1 < NM:
                        m, mu = n + 1, (u + 1) % UN
                        pe.wait_ge(rows_in[mu], 16 * (i + (u + 1) // UN + 1))
                        free_wait(pe, s("xT_ready"), m - 1)
                        tr(banks[:, mu % 2, 0:P], xg[mu][:, 0:D], ident[:, :]).then_inc(s("xt_done"), 1)
                    if not known or n >= 2:
                        m, mu = n - 2, (u - 2) % UN
                        pe.wait_ge(s("hs_ready"), m + 1)
                        free_wait(pe, s("hT_ready"), m - 1)
                        for c in range(2):
                            last = tr(banks[:, 4 + mu % 2, c * P:(c + 1) * P], hs[mu % 2][:, c * P:(c + 1) * P],
                                      ident[:, :])
                        last.then_inc(s("ht_done"), 1)
                    if not known or n < NM:
                        pe.wait_ge(s("xT_ready"), n + 1)
                        free_wait(pe, s("hb_ready"), n - 1)
                        mm(banks[:, 2 + u % 2, :], xTs[u % 2],
                           ew1_s[:, bass.ds(ev[EP + u], 1), :].rearrange("p a f -> p (a f)"),
                           start=True, stop=True).then_inc(s("d1_done"), 1)
                    if not known or n >= 2:
                        m, mu = n - 2, (u - 2) % UN
                        pe.wait_ge(s("hT_ready"), m + 1)
                        free_wait(pe, s("y_ready"), m - 1)
                        for c in range(2):
                            last = mm(banks[:, 6 + mu % 2, 0:D], hTs[mu % 2][:, c * P:(c + 1) * P],
                                      ew2_s[:, bass.ds(ev[EP + u - 2], 1), c, :].rearrange("p a d -> p (a d)"),
                                      start=(c == 0), stop=(c == 1))
                        last.then_inc(s("d2_done"), 1)

            pe.wait_ge(rows_in[0], 16)
            tr(banks[:, 0, 0:P], xg[0][:, 0:D], ident[:, :]).then_inc(s("xt_done"), 1)
            pe_block(0, range(UN))
            with pe.Fori(1, NM // UN) as i:
                pe_block(i, range(UN))
            pe_block(NM // UN, range(NM % UN + 2))


_OUT = ((8, 1024, 128), "float32")


def kernel(**inputs):
    import numpy as np
    import concourse.bacc as bacc
    from concourse.bass_utils import run_bass_kernel_spmd

    t = {k: np.asarray(v) for k, v in inputs.items()}
    E, H2, D = t["L0_ffn_dense_1_w"].shape
    F = H2 // 2
    ew1 = t["L0_ffn_dense_1_w"].reshape(E, F, 2, D).transpose(3, 0, 2, 1)
    eb1 = t["L0_ffn_dense_1_b"].reshape(E, F, 2).transpose(0, 2, 1)
    ew2 = t["L0_ffn_dense_2_w"].reshape(E, D, 2, F // 2).transpose(3, 0, 2, 1).reshape(F // 2, E, 2 * D)
    a = {k[len("L0_attn_"):]: v for k, v in t.items() if k.startswith("L0_attn_")}
    vecs = np.stack([a["g1"], a["be1"], a["g2"], a["be2"], a["qkv_b"][:D], *a["b1"].reshape(-1, D)], axis=1)
    brow = np.concatenate([a["qkv_b"][D:], a["out_b"], a["b2"]])
    arrays = {"src": a["src"], "qkv_w": a["qkv_w"], "out_w": a["out_w"], "w1": a["w1"], "w2": a["w2"],
              "gate_w": t["L0_ffn_gate_w"], "vecs": vecs, "brow": brow,
              "ew1": ew1, "eb1": eb1, "ew2": ew2, "eb2": t["L0_ffn_dense_2_b"]}
    nc = bacc.Bacc("TRN2", target_bir_lowering=False, num_devices=1)
    args, feed = [], {}
    for n, v in arrays.items():
        v = np.ascontiguousarray(v)
        feed["in_" + n] = v
        args.append(nc.dram_tensor("in_" + n, v.shape, mybir.dt.from_np(v.dtype), kind="ExternalInput").ap())
    args.append(nc.dram_tensor("out_0", _OUT[0], F32, kind="ExternalOutput").ap())
    layer_kernel(nc, *args)
    r = run_bass_kernel_spmd(nc, [feed], core_ids=[0])
    return r.results[0]["out_0"]
```

```python
from contextlib import ExitStack

import concourse.bass as bass
from concourse import mybir

P = 128
F32 = mybir.dt.float32
BF16 = mybir.dt.bfloat16
U32 = mybir.dt.uint32
I32 = mybir.dt.int32
ALU = mybir.AluOpType
ACT = mybir.ActivationFunctionType
AX_X = mybir.AxisListType.X
PE_E = mybir.EngineType.PE
DVE_E = mybir.EngineType.DVE

LN_EPS = 1e-5
DEN_EPS = 1e-6
LIMIT = 9.0
BIG = 3.0e38


def free_wait(eng, sem, value):
    if isinstance(value, int) and value <= 0:
        return
    eng.wait_ge(sem, value)


def layer_kernel(nc, x, wqkv, wo, w1, w2, wgate, vecs, brow, ew1, eb1, ew2, eb2, out):
    NBATCH, SEQ, D = x.shape
    NE = wgate.shape[1]
    H2 = eb1.shape[1] * eb1.shape[2]
    FE = H2 // 2
    FF = w1.shape[1]
    NF = FF // P
    HD = 8
    NH = D // HD
    TPB = SEQ // P
    NT = NBATCH * TPB
    TOKENS = NBATCH * SEQ
    GT = 4
    NG = NT // GT
    GB = TPB // GT
    NXD = 5
    W = D + 4
    LT = TOKENS // P + NE - 1
    NM = 2 * LT
    UN = 14
    LP = (2 * LT // UN + 1) * UN // 2
    EP = 4
    assert D == P and GB == 2 and NG == 16 and NE == 8

    xs = [nc.dram_tensor(f"expert_rows_{k}", (LT * P, W), F32).ap() for k in range(2)]
    ye = [nc.dram_tensor(f"expert_out_{k}", (TOKENS, D), F32).ap() for k in range(2)]
    x_v = x.rearrange("b (p t) d -> p b t d", t=TPB)
    out_v = out.rearrange("b (p t) d -> p b t d", t=TPB)
    ye_v = [y.rearrange("(b p t) d -> p b t d", b=NBATCH, t=TPB) for y in ye]
    xs_v = [s.rearrange("(j p) w -> p j w", p=P) for s in xs]

    with ExitStack() as ctx:
        def sb(name, shape, dt=F32):
            return ctx.enter_context(nc.sbuf_tensor(name, shape, dt))

        def sem(name):
            return ctx.enter_context(nc.semaphore(name))

        x_all = sb("x_all", [P, NT, D])
        xn_rows = sb("xn_rows", [P, NT, W])
        aT_all = sb("aT_all", [P, NT * P])
        wqkv_raw = sb("wqkv_raw", [P, 3 * D])
        wqkv_s = sb("wqkv_s", [P, 3 * D])
        wo_s = sb("wo_s", [P, D])
        w1_raw = sb("w1_raw", [P, FF])
        w1_s = sb("w1_s", [P, FF])
        w2_s = sb("w2_s", [P, NF, D])
        wg_s = sb("wg_s", [P, NE])
        ew2_s = sb("ew2_s", [P, NE, 2, D])
        eb2_s = sb("eb2_s", [P, NE, D])
        cols = sb("cols", [P, 8])
        G1, BE1, G2, BE2 = range(4)
        BQ, NBQ, BQ1, B1 = 0, 1, 2, 4
        vec_raw = sb("vec_raw", [P, 5 + NF])
        be1_wide = sb("be1_wide", [P, P])
        brow_f = sb("brow_f", [P, 4 * D])
        brow_t = sb("brow_t", [P, 3, 4 * D], BF16)
        bias_kv = sb("bias_kv", [P, 2, 2 * D], BF16)
        bias_o = sb("bias_o", [P, GT, D], BF16)
        bias_2 = sb("bias_2", [P, GT, D], BF16)
        row3 = sb("row3", [P, 3])
        ones_b = sb("ones_b", [P, P], BF16)
        upper_b = sb("upper_b", [P, P], BF16)
        ident = sb("ident", [P, P])
        hmask = sb("hmask", [P, D])
        zmask = sb("zmask", [P, NH])
        pad_row = sb("pad_row", [P, W])
        halfm = sb("halfm", [P, 2 * TPB])
        stats = sb("stats", [P, 2, TPB, 6])
        mv = sb("mv", [P, 2, TPB, 2])
        part = sb("part", [P, 4, TPB])
        varg = sb("varg", [P, 2, 2, TPB])
        rr = sb("rr", [P, 2, 2, TPB])
        nbias = sb("nbias", [P, 2, 2, TPB])
        inv_r2 = sb("inv_r2", [P, NT])
        aT_g = sb("aT_g", [P, 2, GT * P])
        rev8 = sb("rev8", [P, NE])
        top = sb("top", [P, 8, NT])
        wts = sb("wts", [P, 2, NT])
        slot_f = sb("slot_f", [P, NT])
        slot_u = sb("slot_u", [P, 2, NT], U32)
        cnt = sb("cnt", [P, 12, NE])
        cnt_i = sb("cnt_i", [P, 2, NE], I32)
        jrow = sb("jrow", [P, LP])
        tile_e = sb("tile_e", [P, LP, NE])
        tile_s = sb("tile_s", [P, LP])
        tile_x = sb("tile_x", [P, EP + 2 * LP], U32)
        stage_rows = sb("stage_rows", [P, TPB, W])
        stage_idx = sb("stage_idx", [P, 2, TPB], U32)

        eq = sb("eq", [P, 2, 512])
        ek = sb("ek", [P, 2, GT, D])
        qf = sb("qf", [P, 2, GT * P])
        kf = sb("kf", [P, 2, GT, D])
        vv = sb("vv", [P, 2, GT, D + 1])
        kvz = sb("kvz", [P, D + NH])
        den = sb("den", [P, 2, GT, NH])
        rden = sb("rden", [P, 2, GT, NH])
        ysb = sb("ysb", [P, 2, GT, D])
        yTs = sb("yTs", [P, 2, GT * P])
        x1 = sb("x1", [P, 2, GT, D])
        newt = sb("newt", [P, 5, TPB])
        newt_i = sb("newt_i", [P, TPB], I32)
        bb = sb("bb", [P, 2, GT, D])
        bTs = sb("bTs", [P, 2, GT * P])
        hh = sb("hh", [P, NF, GT * P])

        ctx_ps = ctx.enter_context(nc.psum_tensor("banks", [P, 8, 512], F32))
        banks = ctx_ps

        S = {}

        def s(name):
            if name not in S:
                S[name] = sem(name)
            return S[name]

        w_in = s("w_in")
        wide_in = s("wide_in")
        x_in = [s(f"x_in_{p}") for p in range(2)]
        aT_saved = [s(f"aT_saved_{p}") for p in range(2)]
        aT_in = [s(f"aT_in_{p}") for p in range(2)]
        rows_in = [s(f"rows_in_{u}") for u in range(UN)]
        list_dma = [s(f"list_dma_{k}") for k in range(2)]
        back_dma = [s(f"back_dma_{k}") for k in range(2)]
        y_in = [s(f"y_in_{b}") for b in range(NBATCH)]

        a_t = bb
        small = [hh[:, i, :] for i in range(4)]
        oneh = [kf[:, k].rearrange("p t d -> p (t d)").rearrange("p (c e) -> p c e", e=NE) for k in range(2)]
        oneh_b = [qf[:, k, 0:NT * NE // 2].bitcast(BF16).rearrange("p (c e) -> p c e", e=NE) for k in range(2)]
        gates = ysb[:, 0].rearrange("p t d -> p (t d)").rearrange("p (c e) -> p c e", e=NE)
        bsp = [bTs[:, 0, :], bTs[:, 1, :], yTs[:, 0, :]]
        brow_c = [x1[:, k].rearrange("p t d -> p (t d)") for k in range(2)]
        ew1_s = aT_all[:, 0:NE * H2].rearrange("p (e f) -> p e f", e=NE)
        eb1_s = aT_all[:, NE * H2:2 * NE * H2].rearrange("p (e f) -> p e f", e=NE)
        xg = [xn_rows[:, u, :] for u in range(UN)]
        xTs = [bTs[:, u, 0:P] for u in range(2)]
        hb = [ek[:, u].rearrange("p t d -> p (t d)") for u in range(2)]
        gm = [qf[:, u, 0:FE] for u in range(2)]
        vm = [kf[:, u].rearrange("p t d -> p (t d)")[:, 0:FE] for u in range(2)]
        sg = [eq[:, u, 0:FE] for u in range(2)]
        hs = [ysb[:, u].rearrange("p t d -> p (t d)")[:, 0:FE] for u in range(2)]
        hTs = [yTs[:, u, 0:FE] for u in range(2)]
        yo = [(bb if u < 2 * GT else x1)[:, u // GT % 2, u % GT, :] for u in range(UN)]
        yc = [t_.rearrange("p (c d) -> p c d", d=D)
              for t_ in (aT_all[:, :], xn_rows[:, :, :].rearrange("p c w -> p (c w)")[:, 0:NT * D])]

        block = ctx.enter_context(nc.Block())

        @block.sync
        def _(sp):
            def load_x(b, par):
                src = x_v[:, b] if isinstance(b, int) else \
                    x_v[:, bass.ds(b, 1)].rearrange("p b t d -> p (b t) d")
                dst = x_all[:, b * TPB:(b + 1) * TPB, :] if isinstance(b, int) else \
                    x_all[:, bass.ds(b * TPB, TPB), :]
                sp.dma_start(dst, src).then_inc(x_in[par], 16)

            for par in range(2):
                load_x(par, par)
            loads = [(wqkv_raw[:, :], wqkv), (wo_s[:, :], wo), (w1_raw[:, :], w1),
                     (w2_s[:, :, :], w2.rearrange("(f p) d -> p f d", p=P)), (wg_s[:, :], wgate),
                     (vec_raw[:, :], vecs), (brow_f[:, :], brow.partition_broadcast(P))]
            for dst, src in loads:
                sp.dma_start(dst, src).then_inc(w_in, 16)
            with sp.Fori(1, NBATCH // 2) as i:
                for par in range(2):
                    sp.wait_ge(x_in[par], i * 16)
                    load_x(2 * i + par, par)
            for par in range(2):
                sp.wait_ge(aT_saved[par], 16 * NBATCH)
            sp.wait_ge(s("gate_done"), NG)

            def attn_in(b, h):
                free_wait(sp, s("kv_done"), 2 * b + h - 1)
                sp.dma_start(aT_g[:, h, :], aT_all[:, bass.ds(b * (TPB * P) + h * GT * P, GT * P)])\
                    .then_inc(aT_in[h], 16)
            for h in range(2):
                attn_in(0, h)
            with sp.Fori(1, NBATCH) as b:
                for h in range(2):
                    attn_in(b, h)

            for h in range(2):
                sp.wait_ge(aT_in[h], 16 * NBATCH)
            sp.dma_start(ew1_s[:, :, :], ew1.rearrange("p e a f -> p e (a f)")).then_inc(wide_in, 16)
            sp.dma_start(ew2_s[:, :, :, :], ew2.rearrange("p e (c d) -> p e c d", c=2)).then_inc(wide_in, 16)
            sp.dma_start(eb1_s[:, :, :].rearrange("p e f -> p (e f)"),
                         eb1.rearrange("e a f -> (e a f)").partition_broadcast(P)).then_inc(wide_in, 16)
            sp.dma_start(eb2_s[:, :, :].rearrange("p e f -> p (e f)"),
                         eb2.rearrange("e d -> (e d)").partition_broadcast(P)).then_inc(wide_in, 16)

            for k in range(2):
                sp.wait_ge(list_dma[k], 16 * (NT + 1))
            sp.wait_ge(s("res_done"), NG)

            def load_rows(i, u):
                free_wait(sp, back_dma[u % 2], 16 * (i * (UN // 2) + u // 2 - UN // 2 + 1))
                j = i * (UN // 2) + u // 2
                src = xs_v[u % 2][:, j, :] if isinstance(i, int) else \
                    xs_v[u % 2][:, bass.ds(j, 1), :].rearrange("p a w -> p (a w)")
                sp.dma_start(xg[u], src).then_inc(rows_in[u], 16)

            for u in range(UN):
                load_rows(0, u)
            with sp.Fori(1, NM // UN) as i:
                for u in range(UN):
                    load_rows(i, u)
            for u in range(NM % UN):
                load_rows(NM // UN, u)

            for k in range(2):
                sp.wait_ge(back_dma[k], 16 * LT)
            sp.wait_ge(s("d1_done"), NM)

            for b in range(NBATCH):
                for k in range(2):
                    sp.dma_start(yc[k][:, b * TPB:(b + 1) * TPB, :], ye_v[k][:, b]).then_inc(y_in[b], 16)
            for b in range(NBATCH):
                sp.wait_ge(s("comb_done"), b + 1)
                sp.dma_start(out_v[:, b], x_all[:, b * TPB:(b + 1) * TPB, :]).then_inc(s("out_dma"), 16)
            sp.wait_ge(s("out_dma"), 16 * NBATCH)

        @block.gpsimd
        def _(pool):
            g = nc.gpsimd
            g.memset(ones_b[:, :], 1.0).then_inc(s("c_ones"), 1)
            g.memset(upper_b[:, :], 1.0).then_inc(s("c_set"), 1)
            g.memset(ident[:, :], 0.0).then_inc(s("c_set"), 1)
            g.memset(hmask[:, :], 1.0).then_inc(s("c_set"), 1)
            g.memset(zmask[:, :], 1.0).then_inc(s("c_set"), 1)
            g.memset(row3[:, :], 1.0).then_inc(s("c_set"), 1)
            g.memset(halfm[:, :], -0.5).then_inc(s("c_set"), 1)
            g.memset(pad_row[:, :], 0.0).then_inc(s("c_set"), 1)
            g.memset(xn_rows[:, :, D:W], 0.0).then_inc(s("c_set"), 1)
            g.memset(vv[:, :, :, D:D + 1], 1.0).then_inc(s("c_vv"), 1)
            g.memset(tile_x[:, 0:EP], 0).then_inc(s("c_set"), 1)
            pool.wait_ge(s("c_set"), 9)
            g.affine_select(out=ident[:, :], in_=ident[:, :], compare_op=ALU.not_equal, fill=1.0, base=0,
                            pattern=[[-1, P]], channel_multiplier=1).then_inc(s("c_ident"), 1)
            g.iota(pad_row[:, D:D + 1].bitcast(I32), pattern=[[0, 1]], base=2 * TOKENS, channel_multiplier=0)\
                .then_inc(s("c_pad"), 1)
            pool.wait_ge(s("c_pad"), 1)
            for k in range(2):
                pool.dma_start(xs_v[k], pad_row[:, :].rearrange("p (a w) -> p a w", a=1).broadcast_to([P, LT, W]))\
                    .then_inc(list_dma[k], 16)
            g.iota(xn_rows[:, :, D:D + 1].bitcast(I32).rearrange("p (b t) a -> p b (t a)", t=TPB),
                   pattern=[[SEQ, NBATCH], [1, TPB]], base=0, channel_multiplier=TPB).then_inc(s("c_ids"), 1)
            g.affine_select(out=upper_b[:, :], in_=upper_b[:, :], compare_op=ALU.is_gt, fill=0.0, base=0,
                            pattern=[[1, P]], channel_multiplier=-1).then_inc(s("c_upper"), 1)
            hm = hmask[:, :].rearrange("p (h e) -> p h e", e=HD)
            g.affine_select(out=hm, in_=hm, compare_op=ALU.is_ge, fill=0.0, base=0,
                            pattern=[[-HD, NH], [0, HD]], channel_multiplier=1).then_inc(s("c_m1"), 1)
            g.affine_select(out=zmask[:, :], in_=zmask[:, :], compare_op=ALU.is_ge, fill=0.0, base=0,
                            pattern=[[-HD, NH]], channel_multiplier=1).then_inc(s("c_m1"), 1)
            g.affine_select(out=row3[:, :], in_=row3[:, :], compare_op=ALU.is_equal, fill=0.0, base=0,
                            pattern=[[-1, 3]], channel_multiplier=1).then_inc(s("c_row3"), 1)
            pool.wait_ge(s("c_m1"), 2)
            g.affine_select(out=hm, in_=hm, compare_op=ALU.is_ge, fill=0.0, base=HD - 1,
                            pattern=[[HD, NH], [0, HD]], channel_multiplier=-1).then_inc(s("c_mask"), 1)
            g.affine_select(out=zmask[:, :], in_=zmask[:, :], compare_op=ALU.is_ge, fill=0.0, base=HD - 1,
                            pattern=[[HD, NH]], channel_multiplier=-1).then_inc(s("c_mask"), 1)
            g.iota(jrow[:, :], pattern=[[1, LP]], base=0, channel_multiplier=0,
                   allow_small_or_imprecise_dtypes=True).then_inc(s("c_j"), 1)
            g.iota(rev8[:, :], pattern=[[-1, NE]], base=NE, channel_multiplier=0,
                   allow_small_or_imprecise_dtypes=True).then_inc(s("c_j"), 1)

            def roots(b, par):
                pool.wait_ge(s("varg_ready"), b + 1)
                free_wait(pool, s("xn_act"), b - 1)
                free_wait(pool, s("inv_done"), b - 1)
                g.tensor_tensor(rr[:, par].rearrange("p a t -> p (a t)"),
                                varg[:, par].rearrange("p a t -> p (a t)"), halfm[:, :], ALU.pow)\
                    .then_inc(s("rr_ready"), 1)
            for par in range(2):
                roots(par, par)
            with pool.Fori(1, NBATCH // 2) as i:
                for par in range(2):
                    roots(2 * i + par, par)

            def scatter_batch(b):
                pool.wait_ge(s("stage_ready"), b + 1)
                for t in range(TPB):
                    for k in range(2):
                        pool.wait_ge(list_dma[k], 16 * (b * TPB + t + 1))
                        g.indirect_dma_start(
                            xs[k], bass.IndirectOffsetOnAxis(ap=stage_idx[:, k, t:t + 1], axis=0),
                            stage_rows[:, t, :], None)\
                            .then_inc(list_dma[k], 16)
            for b in range(NBATCH):
                scatter_batch(b)

            def scatter_back(i, u):
                n = i * UN + u
                pool.wait_ge(s("y_ready"), n + 1)
                free_wait(pool, back_dma[u % 2], 16 * (i * (UN // 2) + u // 2))
                g.indirect_dma_start(
                    ye[u % 2], bass.IndirectOffsetOnAxis(ap=xg[u][:, D:D + 1].bitcast(U32), axis=0),
                    yo[u], None, bounds_check=TOKENS - 1, oob_is_err=False).then_inc(back_dma[u % 2], 16)
            for n in range(NM):
                scatter_back(n // UN, n % UN)

        @block.scalar
        def _(act):
            a = nc.scalar
            def norm_a(b, h, par):
                act.wait_ge(s("nb_ready"), b + 1)
                free_wait(act, s("t_done"), 2 * b + h - 1)
                for t in range(GT):
                    c = b * TPB + h * GT + t
                    src = x_all[:, c, :] if isinstance(c, int) else \
                        x_all[:, bass.ds(c, 1), :].rearrange("p a d -> p (a d)")
                    i = h * GT + t
                    last = a.activation(a_t[:, h, t, :], src, ACT.Identity,
                                        bias=nbias[:, par, 1, i:i + 1], scale=rr[:, par, 1, i:i + 1])
                last.then_inc(s("a_ready"), 1)

            def evac_a(b, h):
                g_ = 2 * b + h
                act.wait_ge(s("t_done"), g_ + 1)
                free_wait(act, s("gate_done"), g_ - 1)
                free_wait(act, aT_saved[h], 16 * b)
                a.activation(aT_g[:, h, :], banks[:, h, :], ACT.Copy).then_inc(s("aT_ready"), 1)
                act.wait_ge(s("aT_ready"), g_ + 1)
                act.dma_start(aT_all[:, bass.ds(g_ * (GT * P), GT * P)], aT_g[:, h, :])\
                    .then_inc(aT_saved[h], 16)

            def act_norm(b, par):
                norm_a(b, 0, par)
                norm_a(b, 1, par)
                evac_a(b, 0)
                for i in range(NXD, TPB):
                    c = b * TPB + i
                    src = x_all[:, c, :] if isinstance(c, int) else \
                        x_all[:, bass.ds(c, 1), :].rearrange("p a d -> p (a d)")
                    dst = xn_rows[:, c, 0:D] if isinstance(c, int) else \
                        xn_rows[:, bass.ds(c, 1), 0:D].rearrange("p a d -> p (a d)")
                    last = a.activation(dst, src, ACT.Identity,
                                        bias=nbias[:, par, 0, i:i + 1], scale=rr[:, par, 0, i:i + 1])
                last.then_inc(s("xn_act"), 1)
                evac_a(b, 1)

            for par in range(2):
                act_norm(par, par)
            with act.Fori(1, NBATCH // 2) as i:
                for par in range(2):
                    act_norm(2 * i + par, par)

            act.wait_ge(s("gdiff_ready"), 1)
            a.activation(top[:, 4, :], top[:, 3, :], ACT.Exp).then_inc(s("gexp_ready"), 1)

            def elu_q(b, h):
                gi = 2 * b + h
                act.wait_ge(s("q_done"), gi + 1)
                free_wait(act, s("qf_ready"), gi - 1)
                a.activation(eq[:, h, :], banks[:, 4 + h, :], ACT.Relu, bias=cols[:, NBQ:NBQ + 1], scale=-1.0)\
                    .then_inc(s("qe1"), 1)
                act.wait_ge(s("qe1"), gi + 1)
                a.activation(eq[:, h, :], eq[:, h, :], ACT.Exp, scale=-1.0).then_inc(s("qe_ready"), 1)

            def elu_k(b, h):
                gi = 2 * b + h
                act.wait_ge(s("kv_done"), gi + 1)
                free_wait(act, s("kf_ready"), gi - 1)
                kv = banks[:, 2 * h:2 * h + 2, :].rearrange("p a (c n) -> p (a c) n", n=2 * D)
                a.activation(ek[:, h], kv[:, :, 0:D], ACT.Relu, scale=-1.0).then_inc(s("ke1"), 1)
                free_wait(act, s("kvacc_done"), b)
                a.activation(vv[:, h, :, 0:D], kv[:, :, D:2 * D], ACT.Copy).then_inc(s("v_ready"), 1)
                act.wait_ge(s("ke1"), gi + 1)
                a.activation(ek[:, h], ek[:, h], ACT.Exp, scale=-1.0).then_inc(s("ke_ready"), 1)

            def evac_y(b, h):
                act.wait_ge(s("yt_done"), 2 * b + h + 1)
                free_wait(act, s("o_done"), 2 * b + h - 1)
                a.activation(yTs[:, h, :], banks[:, 2 * h, :], ACT.Copy).then_inc(s("yT_ready"), 1)

            def evac_b(b, h):
                act.wait_ge(s("bt_done"), 2 * b + h + 1)
                free_wait(act, s("w1_done"), (2 * b + h - 1) * NF)
                a.activation(bTs[:, h, :], banks[:, 7 - h, :], ACT.Copy).then_inc(s("bT_ready"), 1)

            def gelus(b, h):
                gi = 2 * b + h
                free_wait(act, s("w2_done"), gi)
                for f in range(NF):
                    act.wait_ge(s("w1_done"), gi * NF + f + 1)
                    a.activation(hh[:, f, :], banks[:, 7 - f % 2, :], ACT.Gelu,
                                 bias=cols[:, B1 + f:B1 + f + 1]).then_inc(s("gelu_done"), 1)

            def act_step3(b, ff, att, proj):
                if ff:
                    for h in range(2):
                        gelus(b, h)
                if att:
                    for h in range(2):
                        evac_y(b + 1, h)
                if proj:
                    elu_q(b + 2, 0)
                    elu_k(b + 2, 0)
                    elu_q(b + 2, 1)
                if att:
                    for h in range(2):
                        evac_b(b + 1, h)
                if proj:
                    elu_k(b + 2, 1)

            act.wait_ge(s("cols_ready"), 1)
            for h in range(2):
                elu_q(0, h)
                elu_k(0, h)
            act_step3(-1, False, True, True)
            act_step3(0, True, True, True)
            with act.Fori(1, NBATCH - 2) as b:
                act_step3(b, True, True, True)
            act_step3(NBATCH - 2, True, True, False)
            act_step3(NBATCH - 1, True, False, False)

            def evac_x(n, u):
                act.wait_ge(s("xt_done"), n + 1)
                free_wait(act, s("d1_done"), n - 1)
                a.activation(xTs[u % 2], banks[:, u % 2, 0:P], ACT.Copy).then_inc(s("xT_ready"), 1)

            def evac_h(n, u):
                act.wait_ge(s("ht_done"), n + 1)
                free_wait(act, s("d2_done"), n - 1)
                a.activation(hTs[u % 2], banks[:, 4 + u % 2, 0:FE], ACT.Copy).then_inc(s("hT_ready"), 1)

            def swish(n, u):
                act.wait_ge(s("gm_ready"), n + 1)
                free_wait(act, s("hs_ready"), n - 1)
                a.activation(sg[u % 2], gm[u % 2], ACT.Gelu_apprx_sigmoid).then_inc(s("sg_ready"), 1)

            def act_step(n, u):
                known = isinstance(n, int)
                if not known or n >= 3:
                    evac_h(n - 3, u - 3)
                if not known or n + 1 < NM:
                    evac_x(n + 1, u + 1)
                if not known or 1 <= n <= NM:
                    swish(n - 1, u - 1)
            act_step(-1, -1)
            for u in range(UN):
                act_step(u, u)
            with act.Fori(1, NM // UN) as i:
                for u in range(UN):
                    act_step(UN * i + u, u)
            for n in range(NM // UN * UN, NM + 3):
                act_step(n, n % UN)

        @block.vector
        def _(dve):
            v = nc.vector

            def mean_var(par, done, i):
                st = [stats[:, par, :, q] for q in range(6)]
                v.tensor_tensor(part[:, 0, :], st[1], st[4], ALU.subtract)
                v.tensor_tensor(part[:, 1, :], st[2], st[5], ALU.add)
                v.tensor_tensor(part[:, 2, :], st[1], st[4], ALU.add).then_inc(done, 1)
                dve.wait_ge(done, 3 * i + 1)
                v.scalar_tensor_tensor(part[:, 3, :], part[:, 0, :], 0.25, part[:, 0, :], ALU.mult, ALU.mult)
                v.tensor_scalar(mv[:, par, :, 0], part[:, 2, :], 0.5, None, ALU.mult).then_inc(done, 1)
                dve.wait_ge(done, 3 * i + 2)
                v.scalar_tensor_tensor(mv[:, par, :, 1], part[:, 1, :], 1.0 / D, part[:, 3, :],
                                       ALU.mult, ALU.add).then_inc(done, 1)
                dve.wait_ge(done, 3 * i + 3)

            def norm_batch(b, i, par):
                dve.wait_ge(x_in[par], 16 * i + 16)
                for t in range(TPB):
                    c = b * TPB + t
                    src = x_all[:, c, :] if isinstance(c, int) else \
                        x_all[:, bass.ds(c, 1), :].rearrange("p a d -> p (a d)")
                    last = v.bn_stats(stats[:, par, t, :], src)
                last.then_inc(s("st_ready"), 1)
                dve.wait_ge(s("st_ready"), b + 1)
                mean_var(par, s("mv_ready"), b)
                free_wait(dve, s("rr_ready"), b - 1)
                v.tensor_scalar(varg[:, par, 0, :], mv[:, par, :, 1], LN_EPS, None, ALU.add)\
                    .then_inc(s("u_ready"), 1)
                dve.wait_ge(s("u_ready"), b + 1)
                v.scalar_tensor_tensor(varg[:, par, 1, :], varg[:, par, 0, :], LN_EPS, mv[:, par, :, 1],
                                       ALU.mult, ALU.add).then_inc(s("varg_ready"), 1)

            def apply_batch(b, par):
                dve.wait_ge(s("rr_ready"), b + 1)
                free_wait(dve, s("xn_act"), b - 1)
                v.scalar_tensor_tensor(nbias[:, par], mv[:, par, :, 0].rearrange("p (a t) -> p a t", a=1)
                                       .broadcast_to([P, 2, TPB]), -1.0, rr[:, par],
                                       ALU.mult, ALU.mult).then_inc(s("nb_ready"), 1)
                v.tensor_tensor(newt[:, par, :], varg[:, par, 1, :], rr[:, par, 1, :], ALU.mult)\
                    .then_inc(s("inv1"), 1)
                for t in range(NXD):
                    c = b * TPB + t
                    src = x_all[:, c, :] if isinstance(c, int) else \
                        x_all[:, bass.ds(c, 1), :].rearrange("p a d -> p (a d)")
                    dst = xn_rows[:, c, 0:D] if isinstance(c, int) else \
                        xn_rows[:, bass.ds(c, 1), 0:D].rearrange("p a d -> p (a d)")
                    v.tensor_scalar(dst, src, mv[:, par, t, 0:1], rr[:, par, 0, t:t + 1],
                                    ALU.subtract, ALU.mult)
                dve.wait_ge(s("inv1"), b + 1)
                v.tensor_tensor(inv_r2[:, bass.ds(b * TPB, TPB)], newt[:, par, :], rr[:, par, 0, :], ALU.mult)\
                    .then_inc(s("inv_done"), 1)

            def take_gates(b):
                dve.wait_ge(s("gate_done"), 2 * b + 2)
                v.tensor_copy(gates[:, bass.ds(b * TPB, TPB), :].rearrange("p (a t) e -> p a t e", a=2),
                              banks[:, 2:4, 0:GT * NE].rearrange("p a (t e) -> p a t e", e=NE))\
                    .then_inc(s("gates_ready"), 1)

            norm_batch(0, 0, 0)
            norm_batch(1, 0, 1)
            dve.wait_ge(w_in, 16 * 7)
            v.tensor_scalar(wqkv_s[:, :], wqkv_raw[:, :], vec_raw[:, G1:G1 + 1], None, ALU.mult)\
                .then_inc(s("ws_ready"), 1)
            v.tensor_scalar(w1_s[:, :], w1_raw[:, :], vec_raw[:, G2:G2 + 1], None, ALU.mult)\
                .then_inc(s("ws_ready"), 1)
            dve.wait_ge(s("c_ones"), 1)
            v.tensor_scalar(be1_wide[:, :], ones_b[:, :], vec_raw[:, BE1:BE1 + 1], None, ALU.mult)\
                .then_inc(s("be_ready"), 1)
            dve.wait_ge(s("fold_done"), 1)
            v.tensor_tensor(brow_f[:, 0:2 * D], banks[:, 6, 0:2 * D], brow_f[:, 0:2 * D], ALU.add)\
                .then_inc(s("fold1"), 1)
            v.tensor_tensor(cols[:, BQ:BQ + 1], banks[:, 7, 0:1], vec_raw[:, 4:5], ALU.add).then_inc(s("fold1"), 1)
            v.tensor_tensor(cols[:, B1:B1 + NF], banks[:, 7, 1:1 + NF], vec_raw[:, 5:5 + NF], ALU.add)\
                .then_inc(s("fold1"), 1)
            dve.wait_ge(s("fold1"), 3)
            v.tensor_scalar(cols[:, BQ1:BQ1 + 1], cols[:, BQ:BQ + 1], 1.0, None, ALU.add).then_inc(s("fold2"), 1)
            v.tensor_scalar(cols[:, NBQ:NBQ + 1], cols[:, BQ:BQ + 1], -1.0, None, ALU.mult)\
                .then_inc(s("cols_ready"), 1)
            v.tensor_copy(brow_t[:, 0, :], brow_f[:, :]).then_inc(s("sp"), 1)
            dve.wait_ge(s("sp"), 1)
            v.tensor_tensor(bsp[0], brow_f[:, :], brow_t[:, 0, :], ALU.subtract).then_inc(s("sp"), 1)
            dve.wait_ge(s("sp"), 2)
            v.tensor_copy(brow_t[:, 1, :], bsp[0]).then_inc(s("sp"), 1)
            dve.wait_ge(s("sp"), 3)
            v.tensor_tensor(bsp[1], bsp[0], brow_t[:, 1, :], ALU.subtract).then_inc(s("sp"), 1)
            dve.wait_ge(s("c_row3"), 1)
            v.tensor_scalar(brow_c[0], brow_t[:, 0, :], row3[:, 0:1], None, ALU.mult).then_inc(s("sp"), 1)
            dve.wait_ge(s("sp"), 5)
            v.scalar_tensor_tensor(brow_c[1], brow_t[:, 1, :], row3[:, 1:2], brow_c[0],
                                   ALU.mult, ALU.add).then_inc(s("sp"), 1)
            dve.wait_ge(s("sp"), 6)
            v.scalar_tensor_tensor(bsp[2], bsp[1], row3[:, 2:3], brow_c[1],
                                   ALU.mult, ALU.add).then_inc(s("sp"), 1)
            dve.wait_ge(s("sp"), 7)
            for c in range(2):
                v.tensor_copy(bias_kv[:, c, :], bsp[2][:, 0:2 * D]).then_inc(s("bias_ready"), 1)
            for c in range(GT):
                v.tensor_copy(bias_o[:, c, :], bsp[2][:, 2 * D:3 * D]).then_inc(s("bias_ready"), 1)
                v.tensor_copy(bias_2[:, c, :], bsp[2][:, 3 * D:4 * D]).then_inc(s("bias_ready"), 1)

            apply_batch(0, 0)
            norm_batch(2, 1, 0)
            apply_batch(1, 1)
            take_gates(0)
            with dve.Fori(1, NBATCH // 2 - 1) as i:
                for par in range(2):
                    norm_batch(2 * i + par + 1, i + par, 1 - par)
                    apply_batch(2 * i + par, par)
                    take_gates(2 * i + par - 1)
            norm_batch(NBATCH - 1, NBATCH // 2 - 1, 1)
            apply_batch(NBATCH - 2, 0)
            take_gates(NBATCH - 3)
            apply_batch(NBATCH - 1, 1)
            take_gates(NBATCH - 2)
            take_gates(NBATCH - 1)
            dve.wait_ge(s("xn_act"), NBATCH)

            rt = [0]

            def link(ins):
                rt[0] += 1
                ins.then_inc(s("route_step"), 1)
                dve.wait_ge(s("route_step"), rt[0])

            link(v.memset(small[3], 0.0))
            link(v.memset(cnt[:, 5, :], 0.0))
            dve.wait_ge(s("gates_ready"), NBATCH)
            dve.wait_ge(s("c_j"), 2)
            V3 = [t_.rearrange("p (c e) -> p c e", e=NE) for t_ in small]
            ET = [t_.rearrange("p (e c) -> p e c", c=NT) for t_ in small]
            rev_b = rev8[:, :].rearrange("p (a e) -> p a e", a=1).broadcast_to([P, NT, NE])

            def wide(col):
                return col.rearrange("p (c a) -> p c a", a=1).broadcast_to([P, NT, NE])

            src = gates[:, :, :]
            for k in range(2):
                link(v.tensor_reduce(top[:, k, :], src, AX_X, ALU.max))
                link(v.tensor_tensor(V3[0], src, wide(top[:, k, :]), ALU.is_equal))
                link(v.tensor_tensor(V3[1], V3[0], rev_b, ALU.mult))
                link(v.tensor_reduce(top[:, 2, :], V3[1], AX_X, ALU.max))
                link(v.tensor_tensor(oneh[k][:, :, :], V3[1], wide(top[:, 2, :]), ALU.is_equal))
                v.tensor_copy(oneh_b[k][:, :, :], oneh[k][:, :, :]).then_inc(s("oneh_ready"), 1)
                if k == 0:
                    link(v.scalar_tensor_tensor(V3[2], oneh[0][:, :, :], -BIG, gates[:, :, :], ALU.mult, ALU.add))
                    src = V3[2]
            link(v.tensor_tensor(top[:, 5, :], top[:, 1, :], top[:, 0, :], ALU.subtract))
            v.tensor_tensor(top[:, 3, :], top[:, 5, :], inv_r2[:, :], ALU.mult).then_inc(s("gdiff_ready"), 1)
            for k in range(2):
                dve.wait_ge(s("rank_done"), k + 1)
                tot = banks[:, 4 + 2 * k + 1, :].rearrange("p (c e) -> p e c", e=NE)
                link(v.tensor_copy(ET[0], tot))
                link(v.tensor_tensor_scan(small[1], small[0], small[3], 0.0, ALU.add, ALU.add))
                last_c = ET[1][:, :, NT - 1]
                link(v.tensor_copy(cnt[:, 0, :], last_c))
                link(v.tensor_copy(cnt[:, 1, 0:1], cnt[:, 0, 0:1]))
                link(v.tensor_tensor(cnt[:, 1, 1:NE], cnt[:, 0, 1:NE], cnt[:, 0, 0:NE - 1], ALU.subtract))
                link(v.tensor_scalar(cnt_i[:, 0, :], cnt[:, 1, :], float(P - 1), None, ALU.add))
                link(v.tensor_scalar(cnt_i[:, 1, :], cnt_i[:, 0, :], 7, None, ALU.arith_shift_right))
                link(v.tensor_copy(cnt[:, 2, :], cnt_i[:, 1, :]))
                link(v.tensor_tensor_scan(cnt[:, 3, :], cnt[:, 2, :], cnt[:, 5, :], 0.0, ALU.add, ALU.add))
                link(v.tensor_tensor(cnt[:, 6, :], cnt[:, 3, :], cnt[:, 2, :], ALU.subtract))
                link(v.tensor_tensor(cnt[:, 7, :], cnt[:, 1, :], cnt[:, 0, :], ALU.subtract))
                link(v.scalar_tensor_tensor(cnt[:, 4, :], cnt[:, 6, :], float(P), cnt[:, 7, :],
                                            ALU.mult, ALU.add))
                link(v.tensor_tensor(ET[1], ET[1], ET[0], ALU.subtract))
                link(v.tensor_tensor(ET[1], ET[1],
                                     cnt[:, 4, :].rearrange("p (e a) -> p e a", a=1).broadcast_to([P, NE, NT]),
                                     ALU.add))
                link(v.tensor_tensor(V3[0], banks[:, 4 + 2 * k, :].rearrange("p (c e) -> p c e", e=NE),
                                     small[1].rearrange("p (e c) -> p c e", c=NT), ALU.add))
                link(v.tensor_tensor(V3[2], V3[0], oneh[k][:, :, :], ALU.mult))
                link(v.tensor_reduce(slot_f[:, :], V3[2], AX_X, ALU.add))
                v.tensor_copy(slot_u[:, k, :], slot_f[:, :]).then_inc(s("slots_ready"), 1)
                link(v.tensor_tensor(
                    tile_e[:, :, :],
                    jrow[:, :].rearrange("p (j a) -> p j a", a=1).broadcast_to([P, LP, NE]),
                    cnt[:, 3, :].rearrange("p (a e) -> p a e", a=1).broadcast_to([P, LP, NE]), ALU.is_ge))
                link(v.tensor_reduce(tile_s[:, :], tile_e[:, :, :], AX_X, ALU.add))
                v.tensor_scalar(tile_x[:, EP:].rearrange("p (j k) -> p j k", k=2)[:, :, k], tile_s[:, :],
                                float(NE - 1), None, ALU.min).then_inc(s("tile_x_ready"), 1)
            dve.wait_ge(s("gexp_ready"), 1)
            link(v.tensor_scalar(top[:, 6, :], top[:, 4, :], 1.0, None, ALU.add))
            link(v.reciprocal(wts[:, 0, :], top[:, 6, :]))
            link(v.tensor_tensor(wts[:, 1, :], wts[:, 0, :], top[:, 4, :], ALU.mult))

            def stage_batch(b):
                for k in range(2):
                    free_wait(dve, list_dma[k], 16 * (b * TPB + 1) if not isinstance(b, int) or b else 0)
                rows = xn_rows[:, bass.ds(b * TPB, TPB), :]
                v.tensor_copy(stage_rows[:, :, :], rows)
                v.tensor_copy(stage_idx[:, :, :], slot_u[:, :, bass.ds(b * TPB, TPB)])\
                    .then_inc(s("stage_ready"), 1)

            def feature(b, h):
                gi = 2 * b + h
                dve.wait_ge(s("qe_ready"), gi + 1)
                free_wait(dve, s("y_mm_done"), gi - 1)
                v.scalar_tensor_tensor(qf[:, h, :], banks[:, 4 + h, :], cols[:, BQ1:BQ1 + 1],
                                       eq[:, h, :], ALU.add, ALU.max).then_inc(s("qf_ready"), 1)
                dve.wait_ge(s("ke_ready"), gi + 1)
                dve.wait_ge(s("v_ready"), gi + 1)
                free_wait(dve, s("kvacc_done"), b)
                kv = banks[:, 2 * h:2 * h + 2, :].rearrange("p a (c n) -> p (a c) n", n=2 * D)
                v.scalar_tensor_tensor(kf[:, h], kv[:, :, 0:D], 1.0, ek[:, h], ALU.add, ALU.max)\
                    .then_inc(s("kf_ready"), 1)

            def mask_kv(b):
                dve.wait_ge(s("kvacc_done"), b + 1)
                free_wait(dve, s("y_mm_done"), 2 * b)
                v.tensor_tensor(kvz[:, 0:D], banks[:, 4, 0:D], hmask[:, :], ALU.mult)
                v.tensor_scalar(kvz[:, D:D + NH], zmask[:, :], banks[:, 4, D:D + 1], None, ALU.mult)\
                    .then_inc(s("kvz_ready"), 1)

            def divide(b, h):
                gi = 2 * b + h
                dve.wait_ge(s("y_mm_done"), gi + 1)
                Y = banks[:, 2 * h:2 * h + 2, :].rearrange("p a (c n) -> p (a c) n", n=256)
                v.tensor_scalar(den[:, h], Y[:, :, D:D + NH], DEN_EPS, None, ALU.max).then_inc(s("den1"), 1)
                dve.wait_ge(s("den1"), gi + 1)
                v.reciprocal(rden[:, h], den[:, h]).then_inc(s("den2"), 1)
                dve.wait_ge(s("den2"), gi + 1)
                free_wait(dve, s("yt_done"), gi - 1)
                v.tensor_tensor(
                    ysb[:, h].rearrange("p c (m e) -> p c m e", e=HD),
                    Y[:, :, 0:D].rearrange("p c (m e) -> p c m e", e=HD),
                    rden[:, h].rearrange("p c (m a) -> p c m a", a=1).broadcast_to([P, GT, NH, HD]),
                    ALU.mult).then_inc(s("ynorm_done"), 1)

            def after_attention(b):
                for h in range(2):
                    dve.wait_ge(s("o_done"), 2 * b + h + 1)
                    v.tensor_tensor(x1[:, h], banks[:, 2 * h + 1, :].rearrange("p (t d) -> p t d", d=D),
                                    xn_rows[:, bass.ds((2 * b + h) * GT, GT), 0:D], ALU.add)\
                        .then_inc(s("x1_ready"), 1)
                for h in range(2):
                    dve.wait_ge(s("x1_ready"), 2 * b + h + 1)
                    for t in range(GT):
                        last = v.bn_stats(stats[:, 0, h * GT + t, :], x1[:, h, t, :])
                last.then_inc(s("st2"), 1)

            def second_norm(b):
                N = 12
                dve.wait_ge(s("st2"), b + 1)
                mean_var(0, s("mv2"), b)
                step = s("newton")
                k = [0]

                def nl(ins):
                    k[0] += 1
                    ins.then_inc(step, 1)
                    dve.wait_ge(step, b * N + k[0])
                va = newt[:, 0, :]
                nl(v.tensor_scalar(va, mv[:, 0, :, 1], LN_EPS, None, ALU.add))
                nl(v.tensor_scalar(newt_i[:, :], va.bitcast(I32), 1, None, ALU.arith_shift_right))
                nl(v.tensor_scalar(newt[:, 1, :].bitcast(I32), newt_i[:, :], -1.0, float(0x5F3759DF),
                                   ALU.mult, ALU.add))
                cur = 1
                for it in range(3):
                    y = newt[:, cur, :]
                    nxt = 3 - cur
                    nl(v.tensor_tensor(newt[:, 3, :], y, y, ALU.mult))
                    nl(v.scalar_tensor_tensor(newt[:, 4, :], newt[:, 3, :], -0.5, va, ALU.mult, ALU.mult))
                    nl(v.scalar_tensor_tensor(newt[:, nxt, :], newt[:, 4, :], 1.5, y, ALU.add, ALU.mult))
                    cur = nxt
                assert k[0] == N
                for h in range(2):
                    free_wait(dve, s("bt_done"), 2 * b + h - 1)
                    for t in range(GT):
                        i = h * GT + t
                        last = v.tensor_scalar(bb[:, h, t, :], x1[:, h, t, :], mv[:, 0, i, 0:1],
                                               newt[:, cur, i:i + 1], ALU.subtract, ALU.mult)
                    last.then_inc(s("bb_ready"), 1)

            def add_x1(b):
                xs_ = x_all[:, bass.ds(b * TPB, TPB), :].rearrange("p t d -> p (t d)")
                v.tensor_tensor(xs_, xs_, x1[:, :, :, :].rearrange("p h t d -> p (h t d)"), ALU.add)\
                    .then_inc(s("x1_added"), 1)

            def add_ff(b, h):
                gi = 2 * b + h
                dve.wait_ge(s("w2_done"), gi + 1)
                dve.wait_ge(s("x1_added"), b + 1)
                xs_ = x_all[:, bass.ds(gi * GT, GT), :].rearrange("p t d -> p (t d)")
                v.tensor_tensor(xs_, xs_, banks[:, 5, :], ALU.add).then_inc(s("res_done"), 1)

            def dve_step3(b, ff, att, proj):
                if att:
                    mask_kv(b + 1)
                if ff:
                    add_ff(b, 0)
                if att:
                    for h in range(2):
                        divide(b + 1, h)
                    stage_batch(b + 1)
                    after_attention(b + 1)
                if ff:
                    add_ff(b, 1)
                if att:
                    second_norm(b + 1)
                if proj:
                    for h in range(2):
                        feature(b + 2, h)
                if att:
                    add_x1(b + 1)

            for h in range(2):
                feature(0, h)
            dve.wait_ge(s("c_mask"), 2)
            dve_step3(-1, False, True, True)
            dve_step3(0, True, True, True)
            with dve.Fori(1, NBATCH - 2) as b:
                dve_step3(b, True, True, True)
            dve_step3(NBATCH - 2, True, True, False)
            dve_step3(NBATCH - 1, True, False, False)

            def add_bias(n, u, e):
                dve.wait_ge(s("d1_done"), n + 1)
                free_wait(dve, s("sg_ready"), n - 1)
                v.tensor_tensor(hb[u % 2], banks[:, 2 + u % 2, :],
                                eb1_s[:, bass.ds(e, 1), :].rearrange("p a f -> p (a f)"), ALU.add)\
                    .then_inc(s("hb_ready"), 1)
                dve.wait_ge(s("hb_ready"), n + 1)
                v.tensor_scalar(gm[u % 2], hb[u % 2][:, 0:FE], LIMIT, None, ALU.min).then_inc(s("gm_ready"), 1)
                v.tensor_scalar(vm[u % 2], hb[u % 2][:, FE:H2], LIMIT, -LIMIT, ALU.min, ALU.max)\
                    .then_inc(s("vm_ready"), 1)

            def gate_up(n, u):
                dve.wait_ge(s("sg_ready"), n + 1)
                dve.wait_ge(s("vm_ready"), n + 1)
                free_wait(dve, s("ht_done"), n - 1)
                v.scalar_tensor_tensor(hs[u % 2], vm[u % 2], 1.0, sg[u % 2], ALU.add, ALU.mult)\
                    .then_inc(s("hs_ready"), 1)

            dve.wait_ge(s("tile_x_ready"), 2)
            dve.wait_ge(wide_in, 64)

            def dve_block(i, steps):
                _, ev = nc.values_load_multi_w_load_instructions(
                    tile_x[0:1, bass.ds(i * UN, UN + EP)] if not isinstance(i, int)
                    else tile_x[0:1, i * UN:i * UN + UN + EP],
                    engines=[DVE_E], min_val=0, max_val=NE - 1,
                    skip_runtime_bounds_check_because="written as min(count, NE - 1)")
                for u in steps:
                    n = i * UN + u
                    known = isinstance(i, int)
                    if not known or n < NM:
                        add_bias(n, u % UN, ev[EP + u])
                    if not known or 1 <= n < NM + 1:
                        gate_up(n - 1, (u - 1) % UN)
                    if not known or n >= 3:
                        m, mu = n - 3, (u - 3) % UN
                        dve.wait_ge(s("d2_done"), m + 1)
                        half = (i * UN + u - 3 - (mu % 2)) // 2 if known else i * (UN // 2) + (u - 3 - (mu % 2)) // 2
                        free_wait(dve, back_dma[mu % 2], 16 * (half - 3))
                        v.tensor_tensor(yo[mu], banks[:, 6 + mu % 2, 0:D],
                                        eb2_s[:, bass.ds(ev[EP + u - 3], 1), :].rearrange("p a f -> p (a f)"),
                                        ALU.add).then_inc(s("y_ready"), 1)

            dve_block(0, range(UN))
            with dve.Fori(1, NM // UN) as i:
                dve_block(i, range(UN))
            dve_block(NM // UN, range(NM % UN + 3 if NM % UN + 3 <= UN else UN))
            if NM % UN + 3 > UN:
                dve_block(NM // UN + 1, range(NM % UN + 3 - UN))

            def combine(b):
                dve.wait_ge(y_in[b], 32)
                for k in range(2):
                    for c in range(b * TPB, (b + 1) * TPB):
                        last = v.scalar_tensor_tensor(x_all[:, c, :], yc[k][:, c, :], wts[:, k, c:c + 1],
                                                      x_all[:, c, :], ALU.mult, ALU.add)
                        if k == 0:
                            last.then_inc(s("comb_half"), 1)
                    if k == 0:
                        dve.wait_ge(s("comb_half"), (b + 1) * TPB)
                last.then_inc(s("comb_done"), 1)
            for b in range(NBATCH):
                combine(b)

        @block.tensor
        def _(pe):
            mm = nc.tensor.matmul
            tr = nc.tensor.transpose

            pe.wait_ge(w_in, 16 * 7)
            pe.wait_ge(s("be_ready"), 1)
            mm(banks[:, 6, 0:2 * D], be1_wide[:, :], wqkv_raw[:, D:3 * D], start=True, stop=True)
            mm(banks[:, 7, 0:1], wqkv_raw[:, 0:D], vec_raw[:, BE1:BE1 + 1], start=True, stop=True)
            for f in range(NF):
                last = mm(banks[:, 7, 1 + f:2 + f], w1_raw[:, f * P:(f + 1) * P], vec_raw[:, BE2:BE2 + 1],
                          start=True, stop=True)
            last.then_inc(s("fold_done"), 1)

            def trans_a(b, h):
                pe.wait_ge(s("a_ready"), 2 * b + h + 1)
                free_wait(pe, s("aT_ready"), 2 * b + h - 1)
                for t in range(GT):
                    last = tr(banks[:, h, t * P:(t + 1) * P], a_t[:, h, t, :], ident[:, :])
                last.then_inc(s("t_done"), 1)

            def gate(b, h):
                pe.wait_ge(s("aT_ready"), 2 * b + h + 1)
                free_wait(pe, s("gates_ready"), b)
                for t in range(GT):
                    last = mm(banks[:, 2 + h, t * NE:(t + 1) * NE], aT_g[:, h, t * P:(t + 1) * P], wg_s[:, :],
                              start=True, stop=True)
                last.then_inc(s("gate_done"), 1)

            def pe_norm(b):
                for h in range(2):
                    trans_a(b, h)
                for h in range(2):
                    gate(b, h)
            pe.wait_ge(s("c_ident"), 1)
            pe_norm(0)
            with pe.Fori(1, NBATCH) as b:
                pe_norm(b)

            pe.wait_ge(s("c_upper"), 1)
            pe.wait_ge(s("cols_ready"), 1)
            for k in range(2):
                pe.wait_ge(s("oneh_ready"), k + 1)
                oh = oneh_b[k][:, :, :].rearrange("p c e -> p (c e)")
                mm(banks[:, 4 + 2 * k, :], upper_b[:, :], oh, start=True, stop=True)
                mm(banks[:, 5 + 2 * k, :], ones_b[:, :], oh, start=True, stop=True).then_inc(s("rank_done"), 1)

            def project(b, h):
                gi = 2 * b + h
                pe.wait_ge(aT_in[h], 16 * b + 16)
                if h == 0:
                    free_wait(pe, s("kvz_ready"), b)
                else:
                    free_wait(pe, s("res_done"), 2 * (b - 1))
                mm(banks[:, 4 + h, :], wqkv_s[:, 0:D], aT_g[:, h, :], start=True, stop=True)\
                    .then_inc(s("q_done"), 1)
                free_wait(pe, s("x1_ready"), gi - 1)
                for a_ in range(2):
                    bank = 2 * h + a_
                    mm(banks[:, bank, :], ones_b[:, :], bias_kv[:, :, :].rearrange("p c n -> p (c n)"),
                       start=True, stop=False)
                    for c in range(2):
                        t = 2 * a_ + c
                        last = mm(banks[:, bank, c * 2 * D:(c + 1) * 2 * D], aT_g[:, h, t * P:(t + 1) * P],
                                  wqkv_s[:, D:3 * D], start=False, stop=(c == 1))
                last.then_inc(s("kv_done"), 1)

            def kv_acc(b):
                pe.wait_ge(s("kf_ready"), 2 * b + 2)
                pe.wait_ge(s("v_ready"), 2 * b + 2)
                for h in range(2):
                    for t in range(GT):
                        last = mm(banks[:, 4, 0:D + 1], kf[:, h, t, :], vv[:, h, t, :],
                                  start=(h == 0 and t == 0), stop=(h == 1 and t == GT - 1))
                last.then_inc(s("kvacc_done"), 1)

            def attend(b, h):
                gi = 2 * b + h
                pe.wait_ge(s("kvz_ready"), b + 1)
                pe.wait_ge(s("qf_ready"), gi + 1)
                for t in range(GT):
                    last = mm(banks[:, 2 * h + t // 2, (t % 2) * 256:(t % 2) * 256 + D + NH],
                              qf[:, h, t * P:(t + 1) * P], kvz[:, :], start=True, stop=True)
                last.then_inc(s("y_mm_done"), 1)

            def trans_y(b, h):
                pe.wait_ge(s("ynorm_done"), 2 * b + h + 1)
                for t in range(GT):
                    last = tr(banks[:, 2 * h, t * P:(t + 1) * P], ysb[:, h, t, :], ident[:, :])
                last.then_inc(s("yt_done"), 1)

            def out_proj(b, h):
                pe.wait_ge(s("yT_ready"), 2 * b + h + 1)
                mm(banks[:, 2 * h + 1, :], ones_b[:, :], bias_o[:, :, :].rearrange("p c n -> p (c n)"),
                   start=True, stop=False)
                for t in range(GT):
                    last = mm(banks[:, 2 * h + 1, t * D:(t + 1) * D], yTs[:, h, t * P:(t + 1) * P], wo_s[:, :],
                              start=False, stop=(t == GT - 1))
                last.then_inc(s("o_done"), 1)

            def trans_b(b, h):
                pe.wait_ge(s("bb_ready"), 2 * b + h + 1)
                free_wait(pe, s("gelu_done"), 2 * b * NF)
                for t in range(GT):
                    last = tr(banks[:, 7 - h, t * P:(t + 1) * P], bb[:, h, t, :], ident[:, :])
                last.then_inc(s("bt_done"), 1)

            def ff_up(b, h, fs):
                gi = 2 * b + h
                for f in fs:
                    if f < 2:
                        pe.wait_ge(s("bT_ready"), 2 * b + max(f, h) + 1)
                    free_wait(pe, s("gelu_done"), gi * NF + f - 1)
                    mm(banks[:, 7 - f % 2, :], w1_s[:, f * P:(f + 1) * P], bTs[:, h, :],
                       start=True, stop=True).then_inc(s("w1_done"), 1)

            def ff_down(b, h, fs, after_att):
                gi = 2 * b + h
                if 0 in fs:
                    if h == 0 and after_att:
                        pe.wait_ge(s("qf_ready"), 2 * b + 4)
                    else:
                        pe.wait_ge(s("res_done"), gi)
                    mm(banks[:, 5, :], ones_b[:, :], bias_2[:, :, :].rearrange("p c n -> p (c n)"),
                       start=True, stop=False)
                for f in fs:
                    pe.wait_ge(s("gelu_done"), gi * NF + f + 1)
                    for t in range(GT):
                        last = mm(banks[:, 5, t * D:(t + 1) * D], hh[:, f, t * P:(t + 1) * P], w2_s[:, f, :],
                                  start=False, stop=(f == NF - 1 and t == GT - 1))
                if NF - 1 in fs:
                    last.then_inc(s("w2_done"), 1)

            def pe_step3(b, ff, att, proj):
                first, rest, full = range(NF // 2), range(NF // 2, NF), range(NF)
                if ff:
                    ff_up(b, 0, first)
                if att:
                    kv_acc(b + 1)
                if ff:
                    ff_up(b, 0, rest)
                    ff_down(b, 0, full, att)
                if att:
                    for h in range(2):
                        attend(b + 1, h)
                if ff:
                    ff_up(b, 1, full)
                if att:
                    for h in range(2):
                        trans_y(b + 1, h)
                if ff:
                    ff_down(b, 1, first, att)
                if att:
                    for h in range(2):
                        out_proj(b + 1, h)
                if ff:
                    ff_down(b, 1, rest, att)
                if proj:
                    for h in range(2):
                        project(b + 2, h)
                if att:
                    for h in range(2):
                        trans_b(b + 1, h)

            pe.wait_ge(s("ws_ready"), 2)
            pe.wait_ge(s("bias_ready"), 10)
            pe.wait_ge(s("gates_ready"), NBATCH)
            pe.wait_ge(s("slots_ready"), 2)
            pe.wait_ge(s("c_vv"), 1)
            for h in range(2):
                project(0, h)
            pe_step3(-1, False, True, True)
            pe_step3(0, True, True, True)
            with pe.Fori(1, NBATCH - 2) as b:
                pe_step3(b, True, True, True)
            pe_step3(NBATCH - 2, True, True, False)
            pe_step3(NBATCH - 1, True, False, False)

            pe.wait_ge(s("res_done"), NG)
            pe.wait_ge(s("tile_x_ready"), 2)
            pe.wait_ge(wide_in, 64)

            def pe_block(i, steps):
                known = isinstance(i, int)
                _, ev = nc.values_load_multi_w_load_instructions(
                    tile_x[0:1, i * UN:i * UN + UN + EP] if known else tile_x[0:1, bass.ds(i * UN, UN + EP)],
                    engines=[PE_E], min_val=0, max_val=NE - 1,
                    skip_runtime_bounds_check_because="written as min(count, NE - 1)")
                for u in steps:
                    n = i * UN + u
                    m, mu = n - 3, (u - 3) % UN
                    if not known or n >= 3:
                        pe.wait_ge(s("hs_ready"), m + 1)
                        free_wait(pe, s("hT_ready"), m - 1)
                        for c in range(2):
                            last = tr(banks[:, 4 + mu % 2, c * P:(c + 1) * P], hs[mu % 2][:, c * P:(c + 1) * P],
                                      ident[:, :])
                        last.then_inc(s("ht_done"), 1)
                    if not known or n + 1 < NM:
                        xu = (u + 1) % UN
                        pe.wait_ge(rows_in[xu], 16 * (i + (u + 1) // UN + 1))
                        free_wait(pe, s("xT_ready"), n)
                        tr(banks[:, xu % 2, 0:P], xg[xu][:, 0:D], ident[:, :]).then_inc(s("xt_done"), 1)
                    if not known or n < NM:
                        pe.wait_ge(s("xT_ready"), n + 1)
                        free_wait(pe, s("hb_ready"), n - 1)
                        mm(banks[:, 2 + u % 2, :], xTs[u % 2],
                           ew1_s[:, bass.ds(ev[EP + u], 1), :].rearrange("p a f -> p (a f)"),
                           start=True, stop=True).then_inc(s("d1_done"), 1)
                    if not known or n >= 3:
                        pe.wait_ge(s("hT_ready"), m + 1)
                        free_wait(pe, s("y_ready"), m - 1)
                        for c in range(2):
                            last = mm(banks[:, 6 + mu % 2, 0:D], hTs[mu % 2][:, c * P:(c + 1) * P],
                                      ew2_s[:, bass.ds(ev[EP + u - 3], 1), c, :].rearrange("p a d -> p (a d)"),
                                      start=(c == 0), stop=(c == 1))
                        last.then_inc(s("d2_done"), 1)

            pe.wait_ge(rows_in[0], 16)
            tr(banks[:, 0, 0:P], xg[0][:, 0:D], ident[:, :]).then_inc(s("xt_done"), 1)
            pe_block(0, range(UN))
            with pe.Fori(1, NM // UN) as i:
                pe_block(i, range(UN))
            pe_block(NM // UN, range(NM % UN + 3))


_OUT = ((8, 1024, 128), "float32")


def kernel(**inputs):
    import numpy as np
    import concourse.bacc as bacc
    from concourse.bass_utils import run_bass_kernel_spmd

    t = {k: np.asarray(v) for k, v in inputs.items()}
    E, H2, D = t["L0_ffn_dense_1_w"].shape
    F = H2 // 2
    ew1 = t["L0_ffn_dense_1_w"].reshape(E, F, 2, D).transpose(3, 0, 2, 1)
    eb1 = t["L0_ffn_dense_1_b"].reshape(E, F, 2).transpose(0, 2, 1)
    ew2 = t["L0_ffn_dense_2_w"].reshape(E, D, 2, F // 2).transpose(3, 0, 2, 1).reshape(F // 2, E, 2 * D)
    a = {k[len("L0_attn_"):]: v for k, v in t.items() if k.startswith("L0_attn_")}
    vecs = np.stack([a["g1"], a["be1"], a["g2"], a["be2"], a["qkv_b"][:D], *a["b1"].reshape(-1, D)], axis=1)
    brow = np.concatenate([a["qkv_b"][D:], a["out_b"], a["b2"]])
    arrays = {"src": a["src"], "qkv_w": a["qkv_w"], "out_w": a["out_w"], "w1": a["w1"], "w2": a["w2"],
              "gate_w": t["L0_ffn_gate_w"], "vecs": vecs, "brow": brow,
              "ew1": ew1, "eb1": eb1, "ew2": ew2, "eb2": t["L0_ffn_dense_2_b"]}
    nc = bacc.Bacc("TRN2", target_bir_lowering=False, num_devices=1)
    args, feed = [], {}
    for n, v in arrays.items():
        v = np.ascontiguousarray(v)
        feed["in_" + n] = v
        args.append(nc.dram_tensor("in_" + n, v.shape, mybir.dt.from_np(v.dtype), kind="ExternalInput").ap())
    args.append(nc.dram_tensor("out_0", _OUT[0], F32, kind="ExternalOutput").ap())
    layer_kernel(nc, *args)
    r = run_bass_kernel_spmd(nc, [feed], core_ids=[0])
    return r.results[0]["out_0"]
```

```python
import math
from contextlib import ExitStack

import concourse.bass as bass
from concourse import mybir

P = 128
F32 = mybir.dt.float32
BF16 = mybir.dt.bfloat16
F32R = mybir.dt.float32r
U32 = mybir.dt.uint32
I32 = mybir.dt.int32
ALU = mybir.AluOpType
ACT = mybir.ActivationFunctionType
AX_X = mybir.AxisListType.X
PE_E = mybir.EngineType.PE
DVE_E = mybir.EngineType.DVE

LN_EPS = 1e-5
DEN_EPS = 1e-6
LIMIT = 9.0
ALPHA = 1.702
GATED_LIMIT = LIMIT / (1.0 + math.exp(-ALPHA * LIMIT))
BIG = 3.0e38


def free_wait(eng, sem, value):
    if isinstance(value, int) and value <= 0:
        return
    eng.wait_ge(sem, value)


def layer_kernel(nc, x, wqkv, wo, w1, w2, wgate, vecs, ew1, eb1, ew2, out):
    NBATCH, SEQ, D = x.shape
    NE = wgate.shape[1]
    H2 = eb1.shape[1] * eb1.shape[2]
    FE = H2 // 2
    FF = w1.shape[1]
    NF = FF // P
    HD = 8
    NH = D // HD
    TPB = SEQ // P
    NT = NBATCH * TPB
    TOKENS = NBATCH * SEQ
    GT = 4
    NG = NT // GT
    NXD = 6
    W = D + 4
    LT = TOKENS // P + NE - 1
    NM = 2 * LT
    UN = 14
    LP = (NM // UN + 1) * UN // 2
    EP = 4
    NB = 4 + NE
    assert D == P and TPB == 2 * GT and NG == 16 and NE == 8

    xs = [nc.dram_tensor(f"expert_rows_{k}", (LT * P, W), F32).ap() for k in range(2)]
    ye = [nc.dram_tensor(f"expert_out_{k}", (TOKENS, D), F32).ap() for k in range(2)]
    x_v = x.rearrange("b (p t) d -> p b t d", t=TPB)
    out_v = out.rearrange("b (p t) d -> p b t d", t=TPB)
    ye_v = [y.rearrange("(b p t) d -> p b t d", b=NBATCH, t=TPB) for y in ye]
    xs_v = [s.rearrange("(j p) w -> p j w", p=P) for s in xs]

    with ExitStack() as ctx:
        def sb(name, shape, dt=F32):
            return ctx.enter_context(nc.sbuf_tensor(name, shape, dt))

        def sem(name):
            return ctx.enter_context(nc.semaphore(name))

        x_all = sb("x_all", [P, NT, D])
        xn_rows = sb("xn_rows", [P, NT, W])
        wqkv_raw = sb("wqkv_raw", [P, 3 * D])
        wqkv_p = sb("wqkv_p", [P, 2, 3 * D], F32R)
        wo_s = sb("wo_s", [P, D])
        w1_raw = sb("w1_raw", [P, FF])
        w1_p = sb("w1_p", [P, 2, FF], F32R)
        w2_s = sb("w2_s", [P, NF, D])
        wg_s = sb("wg_s", [P, NE])
        ew2_s = sb("ew2_s", [P, NE, 2, D])
        bias_e = sb("bias_e", [P, NE, D], BF16)
        vec_raw = sb("vec_raw", [P, 9 + NF + NE])
        cols = sb("cols", [P, 3 + NF + NB])
        G1, BE1, G2, BE2 = range(4)
        BQ, B1, BK, NBQ, BQ1 = 0, 1, 1 + NF, 1 + NF + NB, 2 + NF + NB
        warm = sb("warm", [P, 2])
        brest = sb("brest", [P, NB])
        bhalf = sb("bhalf", [P, 2, NB], BF16)
        bparts = sb("bparts", [P, NB, 3])
        bias_kv = sb("bias_kv", [P, 2, 2 * D], BF16)
        bias_o = sb("bias_o", [P, GT, D], BF16)
        bias_2 = sb("bias_2", [P, GT, D], BF16)
        ones_b = sb("ones_b", [P, P], BF16)
        upper_b = sb("upper_b", [P, P], BF16)
        ident = sb("ident", [P, P])
        hmask = sb("hmask", [P, D])
        zmask = sb("zmask", [P, NH])
        pad_row = sb("pad_row", [P, W])
        pad_q = sb("pad_q", [P, NE - 1])
        pad_c = sb("pad_c", [P, NE - 1, NE])
        pad_s = sb("pad_s", [P, NE - 1])
        pad_idx = sb("pad_idx", [P, 2, NE - 1], U32)
        halfm = sb("halfm", [P, 2 * TPB])
        stats = sb("stats", [P, 2, TPB, 6])
        mv = sb("mv", [P, 2, TPB, 2])
        part = sb("part", [P, 4, TPB])
        varg = sb("varg", [P, 2, 2, TPB])
        rr = sb("rr", [P, 2, 2, TPB])
        nbias = sb("nbias", [P, 2, 2, TPB])
        inv_r2 = sb("inv_r2", [P, NT])
        aT_g = sb("aT_g", [P, 2, GT * P])
        rev8 = sb("rev8", [P, NE])
        top = sb("top", [P, 8, NT])
        slot_f = sb("slot_f", [P, NT])
        slot_u = sb("slot_u", [P, 2, NT], U32)
        cnt = sb("cnt", [P, 2, 9, NE])
        cnt_i = sb("cnt_i", [P, 2, NE], I32)
        jrow = sb("jrow", [P, LP])
        tile_e = sb("tile_e", [P, LP, NE])
        tile_s = sb("tile_s", [P, LP])
        tile_x = sb("tile_x", [P, EP + 2 * LP], U32)

        eq = sb("eq", [P, 2, 512])
        ek = sb("ek", [P, 2, GT, D])
        qf = sb("qf", [P, 2, GT * P])
        kf = sb("kf", [P, 2, GT, D])
        vv = sb("vv", [P, 2, GT, D + 1])
        kvz = sb("kvz", [P, D + NH])
        den = sb("den", [P, 2, GT, NH])
        rden = sb("rden", [P, 2, GT, NH])
        ysb = sb("ysb", [P, 2, GT, D])
        yTs = sb("yTs", [P, 2, GT * P])
        x1 = sb("x1", [P, 2, GT, D])
        newt = sb("newt", [P, 5, TPB])
        newt_i = sb("newt_i", [P, TPB], I32)
        bb = sb("bb", [P, 2, GT, D])
        bT_p = sb("bT_p", [P, 2, 2, GT * P], F32R)
        aT_p = sb("aT_p", [P, 2, 2, GT * P], F32R)
        hh = sb("hh", [P, NF, GT * P])

        with nc.sbuf_tensor("aT_all", [P, NT * P], F32) as aT_all:
            pass
        ew1_p = sb("ew1_p", [P, 2, NE, H2], F32R)
        E_LOW, E_HIGH = 0, 1

        banks = ctx.enter_context(nc.psum_tensor("banks", [P, 8, 512], F32))

        S = {}

        def s(name):
            if name not in S:
                S[name] = sem(name)
            return S[name]

        w_in = s("w_in")
        ew1_in = s("ew1_in")
        wide_in = s("wide_in")
        x_in = [s(f"x_in_{p}") for p in range(2)]
        aT_saved = [s(f"aT_saved_{p}") for p in range(2)]
        aT_in = [s(f"aT_in_{p}") for p in range(2)]
        rows_in = [s(f"rows_in_{u}") for u in range(UN)]
        list_dma = [s(f"list_dma_{k}") for k in range(2)]
        back_dma = [s(f"back_dma_{k}") for k in range(2)]
        y_in = [[s(f"y_in_{k}_{b}") for b in range(NBATCH)] for k in range(2)]

        a_t = bb
        small = [hh[:, i, :] for i in range(4)]
        oneh = [x1[:, k].rearrange("p t d -> p (t d)").rearrange("p (c e) -> p c e", e=NE) for k in range(2)]
        totals = ysb[:, 1].rearrange("p t d -> p (t d)")
        oneh_b = [yTs[:, k, 0:NT * NE // 2].bitcast(BF16).rearrange("p (c e) -> p c e", e=NE) for k in range(2)]
        gates = ysb[:, 0].rearrange("p t d -> p (t d)").rearrange("p (c e) -> p c e", e=NE)
        ew1_raw = aT_all[:, 0:NE * H2]
        XG = UN * W
        assert NE * 2 * H2 == NT * P and XG + NE * H2 <= NT * W
        eb1_s = xn_rows[:, :, :].rearrange("p c w -> p (c w)")[:, XG:XG + NE * H2].rearrange("p (e f) -> p e f", e=NE)
        xg = [xn_rows[:, u, :] for u in range(UN)]
        NX = UN // 2
        xT_p = [[bT_p[:, u // GT, part, (u % GT) * P:(u % GT + 1) * P] for part in range(2)] for u in range(NX)]
        hb = [ek[:, u].rearrange("p t d -> p (t d)") for u in range(2)]
        vm = [kf[:, u].rearrange("p t d -> p (t d)")[:, 0:FE] for u in range(2)]
        sg = [eq[:, u, 0:FE] for u in range(2)]
        hs = [ysb[:, u].rearrange("p t d -> p (t d)")[:, 0:FE] for u in range(2)]
        hTs = [yTs[:, u, 0:FE] for u in range(2)]
        yo = [(bb if u < 2 * GT else x1)[:, u // GT % 2, u % GT, :] for u in range(UN)]
        yc = [t_.rearrange("p (c d) -> p c d", d=D)
              for t_ in (aT_all[:, :], xn_rows[:, :, :].rearrange("p c w -> p (c w)")[:, 0:NT * D])]

        UP_BANKS = ((5, 7, 6, 7), (6, 7, 6, 7))

        block = ctx.enter_context(nc.Block())

        @block.sync
        def _(sp):
            def load_x(b, par):
                src = x_v[:, b] if isinstance(b, int) else \
                    x_v[:, bass.ds(b, 1)].rearrange("p b t d -> p (b t) d")
                dst = x_all[:, b * TPB:(b + 1) * TPB, :] if isinstance(b, int) else \
                    x_all[:, bass.ds(b * TPB, TPB), :]
                sp.dma_start(dst, src).then_inc(x_in[par], 16)

            for par in range(2):
                load_x(par, par)
            loads = [(wqkv_raw[:, :], wqkv), (wo_s[:, :], wo), (w1_raw[:, :], w1),
                     (w2_s[:, :, :], w2.rearrange("(f p) d -> p f d", p=P)), (wg_s[:, :], wgate),
                     (vec_raw[:, :], vecs)]
            for dst, src in loads:
                sp.dma_start(dst, src).then_inc(w_in, 16)
            with sp.Fori(1, NBATCH // 2) as i:
                for par in range(2):
                    sp.wait_ge(x_in[par], i * 16)
                    load_x(2 * i + par, par)
            with sp.Fori(0, NBATCH) as b:
                for h in range(2):
                    g_ = 2 * b + h
                    sp.wait_ge(s("aT_ready"), g_ + 1)
                    sp.dma_start(aT_all[:, bass.ds(g_ * (GT * P), GT * P)], aT_g[:, h, :]).then_inc(aT_saved[h], 16)
            for par in range(2):
                sp.wait_ge(aT_saved[par], 16 * NBATCH)
            sp.wait_ge(s("gate_done"), NG)

            def attn_in(b, h):
                free_wait(sp, s("aT_split"), 2 * b + h - 1)
                sp.dma_start(aT_g[:, h, :], aT_all[:, bass.ds(b * (TPB * P) + h * GT * P, GT * P)])\
                    .then_inc(aT_in[h], 16)
            for h in range(2):
                attn_in(0, h)
            with sp.Fori(1, NBATCH) as b:
                for h in range(2):
                    attn_in(b, h)

            for h in range(2):
                sp.wait_ge(aT_in[h], 16 * NBATCH)
            sp.dma_start(ew1_raw, ew1.rearrange("p e a f -> p (e a f)")).then_inc(ew1_in, 16)
            sp.dma_start(ew2_s[:, :, :, :], ew2.rearrange("p e (c d) -> p e c d", c=2)).then_inc(wide_in, 16)
            last_row = -(-(XG + NE * H2) // W)
            for k in range(2):
                sp.wait_ge(list_dma[k], 16 * last_row)
            sp.wait_ge(s("x1_ready"), -(-last_row // GT))
            sp.dma_start(eb1_s[:, :, :].rearrange("p e f -> p (e f)"),
                         eb1.rearrange("e a f -> (e a f)").partition_broadcast(P)).then_inc(wide_in, 16)

            for k in range(2):
                sp.wait_ge(list_dma[k], 16 * (NT + NE - 1))
            sp.wait_ge(s("x1_ready"), NG)

            def load_rows(i, u):
                free_wait(sp, back_dma[u % 2], 16 * (i * (UN // 2) + u // 2 - UN // 2 + 1))
                j = i * (UN // 2) + u // 2
                src = xs_v[u % 2][:, j, :] if isinstance(i, int) else \
                    xs_v[u % 2][:, bass.ds(j, 1), :].rearrange("p a w -> p (a w)")
                sp.dma_start(xg[u], src).then_inc(rows_in[u], 16)

            for u in range(UN):
                load_rows(0, u)
            with sp.Fori(1, NM // UN) as i:
                for u in range(UN):
                    load_rows(i, u)
            for u in range(NM % UN):
                load_rows(NM // UN, u)

            sp.wait_ge(s("d1_done"), NM)

            def load_y(k, b):
                sp.dma_start(yc[k][:, b * TPB:(b + 1) * TPB, :], ye_v[k][:, b]).then_inc(y_in[k][b], 16)
            sp.wait_ge(back_dma[0], 16 * LT)
            for b in range(2):
                load_y(0, b)
            sp.wait_ge(back_dma[1], 16 * LT)
            sp.wait_ge(s("hb_ready"), NM)
            for b in range(NBATCH):
                load_y(1, b)
                if b + 2 < NBATCH:
                    load_y(0, b + 2)
            for b in range(NBATCH):
                sp.wait_ge(s("comb_done"), b + 1)
                sp.dma_start(out_v[:, b], x_all[:, b * TPB:(b + 1) * TPB, :]).then_inc(s("out_dma"), 16)
            sp.wait_ge(s("out_dma"), 16 * NBATCH)

        @block.gpsimd
        def _(pool):
            g = nc.gpsimd
            g.memset(ones_b[:, :], 1.0).then_inc(s("c_ones"), 1)
            g.memset(upper_b[:, :], 1.0).then_inc(s("c_set"), 1)
            g.memset(ident[:, :], 0.0).then_inc(s("c_set"), 1)
            g.memset(hmask[:, :], 1.0).then_inc(s("c_set"), 1)
            g.memset(zmask[:, :], 1.0).then_inc(s("c_set"), 1)
            g.memset(halfm[:, :], -0.5).then_inc(s("c_set"), 1)
            g.memset(pad_row[:, :], 0.0).then_inc(s("c_set"), 1)
            g.memset(xn_rows[:, :, D:W], 0.0).then_inc(s("c_set"), 1)
            g.memset(vv[:, :, :, D:D + 1], 1.0).then_inc(s("c_vv"), 1)
            g.memset(tile_x[:, 0:EP], 0).then_inc(s("c_set"), 1)
            pool.wait_ge(s("c_set"), 8)
            g.affine_select(out=ident[:, :], in_=ident[:, :], compare_op=ALU.not_equal, fill=1.0, base=0,
                            pattern=[[-1, P]], channel_multiplier=1).then_inc(s("c_ident"), 1)
            g.iota(pad_row[:, D:D + 1].bitcast(I32), pattern=[[0, 1]], base=2 * TOKENS, channel_multiplier=0)\
                .then_inc(s("c_pad"), 1)
            g.iota(xn_rows[:, :, D:D + 1].bitcast(I32).rearrange("p (b t) a -> p b (t a)", t=TPB),
                   pattern=[[SEQ, NBATCH], [1, TPB]], base=0, channel_multiplier=TPB).then_inc(s("c_ids"), 1)
            g.affine_select(out=upper_b[:, :], in_=upper_b[:, :], compare_op=ALU.is_gt, fill=0.0, base=0,
                            pattern=[[1, P]], channel_multiplier=-1).then_inc(s("c_upper"), 1)
            hm = hmask[:, :].rearrange("p (h e) -> p h e", e=HD)
            g.affine_select(out=hm, in_=hm, compare_op=ALU.is_ge, fill=0.0, base=0,
                            pattern=[[-HD, NH], [0, HD]], channel_multiplier=1).then_inc(s("c_m1"), 1)
            g.affine_select(out=zmask[:, :], in_=zmask[:, :], compare_op=ALU.is_ge, fill=0.0, base=0,
                            pattern=[[-HD, NH]], channel_multiplier=1).then_inc(s("c_m1"), 1)
            pool.wait_ge(s("c_m1"), 2)
            g.affine_select(out=hm, in_=hm, compare_op=ALU.is_ge, fill=0.0, base=HD - 1,
                            pattern=[[HD, NH], [0, HD]], channel_multiplier=-1).then_inc(s("c_mask"), 1)
            g.affine_select(out=zmask[:, :], in_=zmask[:, :], compare_op=ALU.is_ge, fill=0.0, base=HD - 1,
                            pattern=[[HD, NH]], channel_multiplier=-1).then_inc(s("c_mask"), 1)
            g.iota(jrow[:, :], pattern=[[1, LP]], base=0, channel_multiplier=0,
                   allow_small_or_imprecise_dtypes=True).then_inc(s("c_j"), 1)
            g.iota(pad_q[:, :], pattern=[[P, NE - 1]], base=0, channel_multiplier=1,
                   allow_small_or_imprecise_dtypes=True).then_inc(s("c_j"), 1)
            g.memset(small[3], 0.0).then_inc(s("c_j"), 1)
            g.memset(cnt[:, :, 0, NE - 1:NE], float(TOKENS)).then_inc(s("c_j"), 1)
            g.memset(totals[:, 0:1], 0.0).then_inc(s("c_j"), 1)
            g.memset(cnt[:, :, 5, :], 0.0).then_inc(s("c_j"), 1)
            g.memset(cnt[:, :, 8, :], 0.0).then_inc(s("c_j"), 1)
            g.iota(rev8[:, :], pattern=[[-1, NE]], base=NE, channel_multiplier=0,
                   allow_small_or_imprecise_dtypes=True).then_inc(s("c_j"), 1)

            def roots(b, par):
                pool.wait_ge(s("varg_ready"), b + 1)
                free_wait(pool, s("xn_act"), b - 1)
                free_wait(pool, s("inv_done"), b - 1)
                g.tensor_tensor(rr[:, par].rearrange("p a t -> p (a t)"),
                                varg[:, par].rearrange("p a t -> p (a t)"), halfm[:, :], ALU.pow)\
                    .then_inc(s("rr_ready"), 1)
            for par in range(2):
                roots(par, par)
            with pool.Fori(1, NBATCH // 2) as i:
                for par in range(2):
                    roots(2 * i + par, par)

            pool.wait_ge(s("slots_ready"), 2)
            pool.wait_ge(s("weights_ready"), 1)
            pool.wait_ge(s("xn_act"), NBATCH)
            pool.wait_ge(s("inv_done"), NBATCH)
            for c in range(NT):
                for k in range(2):
                    free_wait(pool, list_dma[k], 16 * c)
                    g.indirect_dma_start(
                        xs[k], bass.IndirectOffsetOnAxis(ap=slot_u[:, k, c:c + 1], axis=0),
                        xn_rows[:, c, :], None).then_inc(list_dma[k], 16)
            pool.wait_ge(s("pads_ready"), 2)
            for i in range(NE - 1):
                for k in range(2):
                    pool.wait_ge(list_dma[k], 16 * (NT + i))
                    g.indirect_dma_start(
                        xs[k], bass.IndirectOffsetOnAxis(ap=pad_idx[:, k, i:i + 1], axis=0),
                        pad_row[:, :], None).then_inc(list_dma[k], 16)

            def scatter_back(i, u):
                n = i * UN + u
                pool.wait_ge(s("y_ready"), n + 1)
                free_wait(pool, back_dma[u % 2], 16 * (i * (UN // 2) + u // 2))
                g.indirect_dma_start(
                    ye[u % 2], bass.IndirectOffsetOnAxis(ap=xg[u][:, D:D + 1].bitcast(U32), axis=0),
                    yo[u], None, bounds_check=TOKENS - 1, oob_is_err=False).then_inc(back_dma[u % 2], 16)
            for n in range(NM):
                scatter_back(n // UN, n % UN)

        @block.scalar
        def _(act):
            a = nc.scalar
            def norm_a(b, h, par):
                act.wait_ge(s("nb_ready"), b + 1)
                free_wait(act, s("t_done"), 2 * b + h - 1)
                for t in range(GT):
                    c = b * TPB + h * GT + t
                    src = x_all[:, c, :] if isinstance(c, int) else \
                        x_all[:, bass.ds(c, 1), :].rearrange("p a d -> p (a d)")
                    i = h * GT + t
                    last = a.activation(a_t[:, h, t, :], src, ACT.Identity,
                                        bias=nbias[:, par, 1, i:i + 1], scale=rr[:, par, 1, i:i + 1])
                last.then_inc(s("a_ready"), 1)

            def evac_a(b, h):
                g_ = 2 * b + h
                act.wait_ge(s("t_done"), g_ + 1)
                free_wait(act, s("gate_done"), g_ - 1)
                free_wait(act, aT_saved[h], 16 * b)
                a.activation(aT_g[:, h, :], banks[:, h, :], ACT.Copy).then_inc(s("aT_ready"), 1)

            def act_norm(b, par):
                norm_a(b, 0, par)
                norm_a(b, 1, par)
                evac_a(b, 0)
                for i in range(NXD, TPB):
                    c = b * TPB + i
                    src = x_all[:, c, :] if isinstance(c, int) else \
                        x_all[:, bass.ds(c, 1), :].rearrange("p a d -> p (a d)")
                    dst = xn_rows[:, c, 0:D] if isinstance(c, int) else \
                        xn_rows[:, bass.ds(c, 1), 0:D].rearrange("p a d -> p (a d)")
                    last = a.activation(dst, src, ACT.Identity,
                                        bias=nbias[:, par, 0, i:i + 1], scale=rr[:, par, 0, i:i + 1])
                last.then_inc(s("xn_act"), 1)
                evac_a(b, 1)

            for par in range(2):
                act_norm(par, par)
            act.wait_ge(s("parts_done"), 1)
            for dst, lo, n, w_ in ((bias_kv, 0, 2, 2 * D), (bias_o, 2 * D, GT, D), (bias_2, 3 * D, GT, D)):
                a.activation(dst[0:3, :, :], banks[0:3, 6, lo:lo + w_].rearrange("p (a d) -> p a d", a=1)
                             .broadcast_to([3, n, w_]), ACT.Copy).then_inc(s("bias_ready"), 1)
            a.activation(bias_e[0:3, :, :].rearrange("p (a e) d -> p a (e d)", a=2), banks[0:3, 4:6, :], ACT.Copy)\
                .then_inc(s("bias_ready"), 1)
            with act.Fori(1, NBATCH // 2) as i:
                for par in range(2):
                    act_norm(2 * i + par, par)

            def high_a(b, h):
                act.wait_ge(aT_in[h], 16 * b + 16)
                free_wait(act, s("kv_done"), 2 * b + h - 1)
                a.activation(aT_p[:, h, 0, :], aT_g[:, h, :], ACT.Copy).then_inc(s("aTh_ready"), 1)

            for h in range(2):
                high_a(0, h)

            def best_copy(k):
                act.wait_ge(s("best_ready"), k + 1)
                a.activation(oneh_b[k][:, :, :], oneh[k][:, :, :], ACT.Copy).then_inc(s("oneh_ready"), 1)

            def totals_copy(k):
                act.wait_ge(s("rank_done"), k + 1)
                tot = banks[:, 7, :].rearrange("p (c e) -> p e c", e=NE)
                a.activation(totals[:, 1:1 + (NE - 1) * NT].rearrange("p (e c) -> p e c", c=NT), tot[:, 0:NE - 1, :],
                             ACT.Copy)
                a.activation(totals[:, 1 + (NE - 1) * NT:], tot[:, NE - 1, 0:NT - 1], ACT.Copy)\
                    .then_inc(s("totals_ready"), 1)
            best_copy(0)
            totals_copy(0)
            best_copy(1)
            act.wait_ge(s("gdiff_ready"), 1)
            a.activation(top[:, 4, :], top[:, 3, :], ACT.Exp).then_inc(s("gexp_ready"), 1)

            def elu_q(b, h):
                gi = 2 * b + h
                act.wait_ge(s("q_done"), gi + 1)
                free_wait(act, s("qf_ready"), gi - 1)
                a.activation(eq[:, h, :], banks[:, 4 + h, :], ACT.Relu, bias=cols[:, NBQ:NBQ + 1], scale=-1.0)\
                    .then_inc(s("qe1"), 1)
                act.wait_ge(s("qe1"), gi + 1)
                a.activation(eq[:, h, :], eq[:, h, :], ACT.Exp, scale=-1.0).then_inc(s("qe_ready"), 1)

            def elu_k(b, h):
                gi = 2 * b + h
                act.wait_ge(s("kv_done"), gi + 1)
                free_wait(act, s("kf_ready"), gi - 1)
                kv = banks[:, 2 * h:2 * h + 2, :].rearrange("p a (c n) -> p (a c) n", n=2 * D)
                a.activation(ek[:, h], kv[:, :, 0:D], ACT.Relu, scale=-1.0).then_inc(s("ke1"), 1)
                free_wait(act, s("kvacc_done"), b)
                a.activation(vv[:, h, :, 0:D], kv[:, :, D:2 * D], ACT.Copy).then_inc(s("v_ready"), 1)
                act.wait_ge(s("ke1"), gi + 1)
                a.activation(ek[:, h], ek[:, h], ACT.Exp, scale=-1.0).then_inc(s("ke_ready"), 1)

            def evac_y(b, h):
                act.wait_ge(s("yt_done"), 2 * b + h + 1)
                free_wait(act, s("o_done"), 2 * b + h - 1)
                a.activation(yTs[:, h, :], banks[:, 2 * h, :], ACT.Copy).then_inc(s("yT_ready"), 1)

            def evac_b(b, h):
                act.wait_ge(s("bt_done"), 2 * b + h + 1)
                free_wait(act, s("w1_done"), (2 * b + h - 1) * NF)
                a.activation(bT_p[:, h, 0, :], banks[:, 7 - h, :], ACT.Copy).then_inc(s("bT_ready"), 1)

            def gelus(b, h):
                gi = 2 * b + h
                free_wait(act, s("w2_done"), gi)
                for f in range(NF):
                    act.wait_ge(s("w1_done"), gi * NF + f + 1)
                    a.activation(hh[:, f, :], banks[:, UP_BANKS[h][f], :], ACT.Gelu,
                                 bias=cols[:, B1 + f:B1 + f + 1]).then_inc(s("gelu_done"), 1)

            def high_e(e):
                act.wait_ge(ew1_in, 16)
                a.activation(ew1_p[:, E_HIGH, e, :], ew1_raw[:, e * H2:(e + 1) * H2], ACT.Copy)\
                    .then_inc(s("eh_ready"), 1)

            def act_step3(b, ff, att, proj, experts=()):
                if ff:
                    gelus(b, 0)
                for e in experts:
                    high_e(e)
                if proj:
                    for h in range(2):
                        high_a(b + 2, h)
                if att:
                    for h in range(2):
                        evac_y(b + 1, h)
                if ff:
                    gelus(b, 1)
                if proj:
                    a.activation(warm[:, 0:1], cols[:, 0:1], ACT.Exp)
                    elu_q(b + 2, 0)
                    elu_k(b + 2, 0)
                    elu_q(b + 2, 1)
                if att:
                    evac_b(b + 1, 0)
                if proj:
                    elu_k(b + 2, 1)
                if att:
                    evac_b(b + 1, 1)

            act.wait_ge(s("cols_ready"), 1)
            for h in range(2):
                elu_q(0, h)
                elu_k(0, h)
            totals_copy(1)
            act_step3(-1, False, True, True)
            act_step3(0, True, True, True)
            with act.Fori(1, NBATCH - 2) as b:
                act_step3(b, True, True, True)
            act_step3(NBATCH - 2, True, True, False, range(NE // 2))
            act_step3(NBATCH - 1, True, False, False, range(NE // 2, NE))

            def high_x(n, u):
                act.wait_ge(s("xt_done"), n + 1)
                free_wait(act, s("d1_done"), n - NX + 1)
                a.activation(xT_p[u % NX][0], banks[:, u % 2, 0:P], ACT.Copy).then_inc(s("xT_ready"), 1)

            def evac_h(n, u):
                act.wait_ge(s("ht_done"), n + 1)
                free_wait(act, s("d2_done"), n - 1)
                a.activation(hTs[u % 2], banks[:, 4 + u % 2, 0:FE], ACT.Copy).then_inc(s("hT_ready"), 1)

            def swish(n, u):
                act.wait_ge(s("hb_ready"), n + 1)
                free_wait(act, s("hs_ready"), n - 1)
                a.activation(sg[u % 2], hb[u % 2][:, 0:FE], ACT.Gelu_apprx_sigmoid).then_inc(s("sg_ready"), 1)

            def out_rows(m, mu, half):
                act.wait_ge(s("d2_done"), m + 1)
                free_wait(act, back_dma[mu % 2], 16 * (half - 3))
                a.activation(yo[mu], banks[:, 6 + mu % 2, 0:D], ACT.Identity,
                             scale=xg[mu][:, D + 1 + mu % 2:D + 2 + mu % 2]).then_inc(s("y_ready"), 1)

            def act_step(i, u):
                n = i * UN + u
                known = isinstance(i, int)
                if not known or 3 <= n < NM + 3:
                    evac_h(n - 3, u - 3)
                if not known or n + 2 < NM:
                    high_x(n + 2, (u + 2) % UN)
                if not known or 1 <= n <= NM:
                    swish(n - 1, u - 1)
                if not known or n >= 4:
                    out_rows(n - 4, (u - 4) % UN, i * (UN // 2) + (u - 4 - u % 2) // 2)
            for u in range(2):
                high_x(u, u)
            a.activation(warm[:, 1:2], cols[:, 0:1], ACT.Gelu_apprx_sigmoid)
            for u in range(UN):
                act_step(0, u)
            with act.Fori(1, NM // UN) as i:
                for u in range(UN):
                    act_step(i, u)
            for n in range(NM // UN * UN, NM + 4):
                act_step(n // UN, n % UN)

        @block.vector
        def _(dve):
            v = nc.vector

            def mean_var(par, done, i):
                st = [stats[:, par, :, q] for q in range(6)]
                v.tensor_tensor(part[:, 0, :], st[1], st[4], ALU.subtract)
                v.tensor_tensor(part[:, 1, :], st[2], st[5], ALU.add)
                v.tensor_tensor(part[:, 2, :], st[1], st[4], ALU.add).then_inc(done, 1)
                dve.wait_ge(done, 3 * i + 1)
                v.scalar_tensor_tensor(part[:, 3, :], part[:, 0, :], 0.25, part[:, 0, :], ALU.mult, ALU.mult)
                v.tensor_scalar(mv[:, par, :, 0], part[:, 2, :], 0.5, None, ALU.mult).then_inc(done, 1)
                dve.wait_ge(done, 3 * i + 2)
                v.scalar_tensor_tensor(mv[:, par, :, 1], part[:, 1, :], 1.0 / D, part[:, 3, :],
                                       ALU.mult, ALU.add).then_inc(done, 1)
                dve.wait_ge(done, 3 * i + 3)

            def norm_batch(b, i, par):
                dve.wait_ge(x_in[par], 16 * i + 16)
                for t in range(TPB):
                    c = b * TPB + t
                    src = x_all[:, c, :] if isinstance(c, int) else \
                        x_all[:, bass.ds(c, 1), :].rearrange("p a d -> p (a d)")
                    last = v.bn_stats(stats[:, par, t, :], src)
                last.then_inc(s("st_ready"), 1)
                dve.wait_ge(s("st_ready"), b + 1)
                mean_var(par, s("mv_ready"), b)
                free_wait(dve, s("rr_ready"), b - 1)
                v.tensor_scalar(varg[:, par, 0, :], mv[:, par, :, 1], LN_EPS, None, ALU.add)\
                    .then_inc(s("u_ready"), 1)
                dve.wait_ge(s("u_ready"), b + 1)
                v.scalar_tensor_tensor(varg[:, par, 1, :], varg[:, par, 0, :], LN_EPS, mv[:, par, :, 1],
                                       ALU.mult, ALU.add).then_inc(s("varg_ready"), 1)

            def apply_batch(b, par):
                dve.wait_ge(s("rr_ready"), b + 1)
                free_wait(dve, s("xn_act"), b - 1)
                v.scalar_tensor_tensor(nbias[:, par], mv[:, par, :, 0].rearrange("p (a t) -> p a t", a=1)
                                       .broadcast_to([P, 2, TPB]), -1.0, rr[:, par],
                                       ALU.mult, ALU.mult).then_inc(s("nb_ready"), 1)
                v.tensor_tensor(newt[:, par, :], varg[:, par, 1, :], rr[:, par, 1, :], ALU.mult)\
                    .then_inc(s("inv1"), 1)
                for t in range(NXD):
                    c = b * TPB + t
                    src = x_all[:, c, :] if isinstance(c, int) else \
                        x_all[:, bass.ds(c, 1), :].rearrange("p a d -> p (a d)")
                    dst = xn_rows[:, c, 0:D] if isinstance(c, int) else \
                        xn_rows[:, bass.ds(c, 1), 0:D].rearrange("p a d -> p (a d)")
                    v.tensor_scalar(dst, src, mv[:, par, t, 0:1], rr[:, par, 0, t:t + 1],
                                    ALU.subtract, ALU.mult)
                dve.wait_ge(s("inv1"), b + 1)
                v.tensor_tensor(inv_r2[:, bass.ds(b * TPB, TPB)], newt[:, par, :], rr[:, par, 0, :], ALU.mult)\
                    .then_inc(s("inv_done"), 1)

            def take_gates(b):
                dve.wait_ge(s("gate_done"), 2 * b + 2)
                v.tensor_copy(gates[:, bass.ds(b * TPB, TPB), :].rearrange("p (a t) e -> p a t e", a=2),
                              banks[:, 2:4, 0:GT * NE].rearrange("p a (t e) -> p a t e", e=NE))\
                    .then_inc(s("gates_ready"), 1)

            norm_batch(0, 0, 0)
            norm_batch(1, 0, 1)
            dve.wait_ge(w_in, 16 * 6)
            for raw, dst, g_col in ((wqkv_raw, wqkv_p, G1), (w1_raw, w1_p, G2)):
                gain = vec_raw[:, g_col:g_col + 1]
                v.tensor_scalar(dst[:, 0, :], raw[:, :], gain, None, ALU.mult).then_inc(s("w_high"), 1)
                dve.wait_ge(s("w_high"), 1 if raw is wqkv_raw else 2)
                v.scalar_tensor_tensor(dst[:, 1, :], raw[:, :], gain, dst[:, 0, :], ALU.mult, ALU.subtract)\
                    .then_inc(s("ws_ready"), 1)

            def fold_biases():
                dve.wait_ge(s("fold_done"), 1)
                v.tensor_tensor(cols[:, 0:3 + NF], banks[:, 7, 0:3 + NF], vec_raw[:, 4:7 + NF], ALU.add)
                v.tensor_copy(cols[:, 3 + NF:1 + NF + NB], vec_raw[:, 7 + NF:5 + NF + NB]).then_inc(s("fold1"), 1)
                dve.wait_ge(s("fold1"), 1)
                v.tensor_scalar(cols[:, BQ1:BQ1 + 1], cols[:, BQ:BQ + 1], 1.0, None, ALU.add)
                v.tensor_scalar(cols[:, NBQ:NBQ + 1], cols[:, BQ:BQ + 1], -1.0, None, ALU.mult)\
                    .then_inc(s("cols_ready"), 1)
                row = cols[:, BK:BK + NB]
                v.tensor_copy(bhalf[:, 0, :], row).then_inc(s("sp"), 1)
                dve.wait_ge(s("sp"), 1)
                v.tensor_copy(bparts[:, :, 0], bhalf[:, 0, :])
                v.tensor_tensor(brest[:, :], row, bhalf[:, 0, :], ALU.subtract).then_inc(s("sp"), 1)
                dve.wait_ge(s("sp"), 2)
                v.tensor_copy(bhalf[:, 1, :], brest[:, :]).then_inc(s("sp"), 1)
                dve.wait_ge(s("sp"), 3)
                v.tensor_copy(bparts[:, :, 1], bhalf[:, 1, :])
                v.tensor_tensor(bparts[:, :, 2], brest[:, :], bhalf[:, 1, :], ALU.subtract)\
                    .then_inc(s("parts_ready"), 1)

            apply_batch(0, 0)
            fold_biases()
            norm_batch(2, 1, 0)
            apply_batch(1, 1)
            norm_batch(3, 1, 1)
            take_gates(0)
            with dve.Fori(1, NBATCH // 2 - 1) as i:
                for par in range(2):
                    apply_batch(2 * i + par, par)
                    norm_batch(2 * i + par + 2, i + 1, par)
                    take_gates(2 * i + par - 1)
            for par in range(2):
                apply_batch(NBATCH - 2 + par, par)
                take_gates(NBATCH - 3 + par)
            take_gates(NBATCH - 1)
            dve.wait_ge(s("xn_act"), NBATCH)

            def split_a(b, h):
                gi = 2 * b + h
                dve.wait_ge(s("aTh_ready"), gi + 1)
                free_wait(dve, s("kv_done"), gi - 1)
                v.tensor_tensor(aT_p[:, h, 1, :], aT_g[:, h, :], aT_p[:, h, 0, :], ALU.subtract)\
                    .then_inc(s("aT_split"), 1)

            def feature_q(b, h):
                gi = 2 * b + h
                dve.wait_ge(s("qe_ready"), gi + 1)
                free_wait(dve, s("y_mm_done"), gi - 1)
                v.scalar_tensor_tensor(qf[:, h, :], banks[:, 4 + h, :], cols[:, BQ1:BQ1 + 1],
                                       eq[:, h, :], ALU.add, ALU.max).then_inc(s("qf_ready"), 1)

            def feature_k(b, h):
                gi = 2 * b + h
                dve.wait_ge(s("ke_ready"), gi + 1)
                dve.wait_ge(s("v_ready"), gi + 1)
                free_wait(dve, s("kvacc_done"), b)
                kv = banks[:, 2 * h:2 * h + 2, :].rearrange("p a (c n) -> p (a c) n", n=2 * D)
                v.scalar_tensor_tensor(kf[:, h], kv[:, :, 0:D], 1.0, ek[:, h], ALU.add, ALU.max)\
                    .then_inc(s("kf_ready"), 1)

            def mask_kv(b):
                dve.wait_ge(s("kvacc_done"), b + 1)
                free_wait(dve, s("y_mm_done"), 2 * b)
                v.tensor_tensor(kvz[:, 0:D], banks[:, 4, 0:D], hmask[:, :], ALU.mult)
                v.tensor_scalar(kvz[:, D:D + NH], zmask[:, :], banks[:, 4, D:D + 1], None, ALU.mult)\
                    .then_inc(s("kvz_ready"), 1)

            rt = [0]

            def link(ins):
                rt[0] += 1
                ins.then_inc(s("route_step"), 1)
                dve.wait_ge(s("route_step"), rt[0])

            dve.wait_ge(s("gates_ready"), NBATCH)
            dve.wait_ge(s("c_j"), 8)
            V3 = [t_.rearrange("p (c e) -> p c e", e=NE) for t_ in small]
            ET = [t_.rearrange("p (e c) -> p e c", c=NT) for t_ in small]
            rev_b = rev8[:, :].rearrange("p (a e) -> p a e", a=1).broadcast_to([P, NT, NE])

            def wide(col):
                return col.rearrange("p (c a) -> p c a", a=1).broadcast_to([P, NT, NE])

            src = gates[:, :, :]
            for k in range(2):
                link(v.tensor_reduce(top[:, k, :], src, AX_X, ALU.max))
                link(v.tensor_tensor(V3[0], src, wide(top[:, k, :]), ALU.is_equal))
                link(v.tensor_tensor(V3[1], V3[0], rev_b, ALU.mult))
                link(v.tensor_reduce(top[:, 2, :], V3[1], AX_X, ALU.max))
                v.tensor_tensor(oneh[k][:, :, :], V3[1], wide(top[:, 2, :]), ALU.is_equal).then_inc(s("best_ready"), 1)
                split_a(0, k)
                if k == 0:
                    dve.wait_ge(s("best_ready"), 1)
                    link(v.scalar_tensor_tensor(V3[2], oneh[0][:, :, :], -BIG, gates[:, :, :], ALU.mult, ALU.add))
                    src = V3[2]
            link(v.tensor_tensor(top[:, 5, :], top[:, 1, :], top[:, 0, :], ALU.subtract))
            v.tensor_tensor(top[:, 3, :], top[:, 5, :], inv_r2[:, :], ALU.mult).then_inc(s("gdiff_ready"), 1)

            def rank_scan(k):
                dve.wait_ge(s("totals_ready"), k + 1)
                link(v.tensor_tensor_scan(small[1], totals, small[3], 0.0, ALU.add, ALU.add))
                link(v.tensor_copy(cnt[:, k, 0, 0:NE - 1], ET[1][:, 1:NE, 0]))
                link(v.tensor_copy(cnt[:, k, 1, 0:1], cnt[:, k, 0, 0:1]))
                link(v.tensor_tensor(cnt[:, k, 1, 1:NE], cnt[:, k, 0, 1:NE], cnt[:, k, 0, 0:NE - 1], ALU.subtract))
                link(v.tensor_scalar(cnt_i[:, 0, :], cnt[:, k, 1, :], float(P - 1), None, ALU.add))
                link(v.tensor_scalar(cnt_i[:, 1, :], cnt_i[:, 0, :], 7, None, ALU.arith_shift_right))
                link(v.tensor_copy(cnt[:, k, 2, :], cnt_i[:, 1, :]))
                link(v.tensor_tensor_scan(cnt[:, k, 3, :], cnt[:, k, 2, :], cnt[:, k, 5, :], 0.0, ALU.add, ALU.add))
                link(v.tensor_tensor(cnt[:, k, 6, :], cnt[:, k, 3, :], cnt[:, k, 2, :], ALU.subtract))
                link(v.tensor_tensor(cnt[:, k, 7, :], cnt[:, k, 1, :], cnt[:, k, 0, :], ALU.subtract))
                link(v.scalar_tensor_tensor(cnt[:, k, 4, :], cnt[:, k, 6, :], float(P), cnt[:, k, 7, :],
                                            ALU.mult, ALU.add))
                link(v.tensor_tensor(ET[1], ET[1],
                                     cnt[:, k, 4, :].rearrange("p (e a) -> p e a", a=1).broadcast_to([P, NE, NT]),
                                     ALU.add))

            def slots(k):
                link(v.tensor_tensor(V3[0], banks[:, 6, :].rearrange("p (c e) -> p c e", e=NE),
                                     small[1].rearrange("p (e c) -> p c e", c=NT), ALU.add))
                link(v.tensor_tensor(V3[2], V3[0], oneh[k][:, :, :], ALU.mult))
                link(v.tensor_reduce(slot_f[:, :], V3[2], AX_X, ALU.add))
                v.tensor_copy(slot_u[:, k, :], slot_f[:, :]).then_inc(s("slots_ready"), 1)

            def tables(k):
                NPAD = NE - 1
                link(v.scalar_tensor_tensor(cnt[:, k, 8, 1:NE], cnt[:, k, 3, 0:NPAD], float(P), cnt[:, k, 0, 0:NPAD],
                                            ALU.mult, ALU.subtract))
                link(v.tensor_tensor(pad_c[:, :, :],
                                     pad_q[:, :].rearrange("p (i a) -> p i a", a=1).broadcast_to([P, NPAD, NE]),
                                     cnt[:, k, 8, :].rearrange("p (a e) -> p a e", a=1).broadcast_to([P, NPAD, NE]),
                                     ALU.is_ge))
                link(v.tensor_tensor(pad_c[:, :, :], pad_c[:, :, :],
                                     cnt[:, k, 1, :].rearrange("p (a e) -> p a e", a=1).broadcast_to([P, NPAD, NE]),
                                     ALU.mult))
                link(v.tensor_reduce(pad_s[:, :], pad_c[:, :, :], AX_X, ALU.add))
                v.tensor_tensor(pad_idx[:, k, :], pad_s[:, :], pad_q[:, :], ALU.add).then_inc(s("pads_ready"), 1)
                link(v.tensor_tensor(
                    tile_e[:, :, :],
                    jrow[:, :].rearrange("p (j a) -> p j a", a=1).broadcast_to([P, LP, NE]),
                    cnt[:, k, 3, :].rearrange("p (a e) -> p a e", a=1).broadcast_to([P, LP, NE]), ALU.is_ge))
                link(v.tensor_reduce(tile_s[:, :], tile_e[:, :, :], AX_X, ALU.add))
                v.tensor_scalar(tile_x[:, EP:].rearrange("p (j k) -> p j k", k=2)[:, :, k], tile_s[:, :],
                                float(NE - 1), None, ALU.min).then_inc(s("tile_x_ready"), 1)

            rank_scan(0)
            slots(0)
            for h in range(2):
                feature_q(0, h)
                feature_k(0, h)
            dve.wait_ge(s("gexp_ready"), 1)
            link(v.tensor_scalar(top[:, 6, :], top[:, 4, :], 1.0, None, ALU.add))
            link(v.reciprocal(top[:, 7, :], top[:, 6, :]))
            v.tensor_copy(xn_rows[:, :, D + 1], top[:, 7, :])
            v.tensor_tensor(xn_rows[:, :, D + 2], top[:, 7, :], top[:, 4, :], ALU.mult).then_inc(s("weights_ready"), 1)
            rank_scan(1)
            dve.wait_ge(s("c_mask"), 2)
            mask_kv(0)
            slots(1)

            def divide(b, h):
                gi = 2 * b + h
                dve.wait_ge(s("y_mm_done"), gi + 1)
                Y = banks[:, 2 * h:2 * h + 2, :].rearrange("p a (c n) -> p (a c) n", n=256)
                v.tensor_scalar(den[:, h], Y[:, :, D:D + NH], DEN_EPS, None, ALU.max).then_inc(s("den1"), 1)
                dve.wait_ge(s("den1"), gi + 1)
                v.reciprocal(rden[:, h], den[:, h]).then_inc(s("den2"), 1)
                dve.wait_ge(s("den2"), gi + 1)
                free_wait(dve, s("yt_done"), gi - 1)
                v.tensor_tensor(
                    ysb[:, h].rearrange("p c (m e) -> p c m e", e=HD),
                    Y[:, :, 0:D].rearrange("p c (m e) -> p c m e", e=HD),
                    rden[:, h].rearrange("p c (m a) -> p c m a", a=1).broadcast_to([P, GT, NH, HD]),
                    ALU.mult).then_inc(s("ynorm_done"), 1)

            def after_attention(b):
                for h in range(2):
                    dve.wait_ge(s("o_done"), 2 * b + h + 1)
                    v.tensor_tensor(x1[:, h], banks[:, 2 * h + 1, :].rearrange("p (t d) -> p t d", d=D),
                                    xn_rows[:, bass.ds((2 * b + h) * GT, GT), 0:D], ALU.add)\
                        .then_inc(s("x1_ready"), 1)
                    dve.wait_ge(s("x1_ready"), 2 * b + h + 1)
                    for t in range(GT):
                        last = v.bn_stats(stats[:, 0, h * GT + t, :], x1[:, h, t, :])
                last.then_inc(s("st2"), 1)

            def add_ff(b, h):
                gi = 2 * b + h
                dve.wait_ge(s("w2_done"), gi + 1)
                dve.wait_ge(s("x1_added"), b + 1)
                xs_ = x_all[:, bass.ds(gi * GT, GT), :].rearrange("p t d -> p (t d)")
                v.tensor_tensor(xs_, xs_, banks[:, 5, :], ALU.add).then_inc(s("res_done"), 1)

            def second_norm(b, ff):
                N = 12
                dve.wait_ge(s("st2"), b + 1)
                mean_var(0, s("mv2"), b)
                step = s("newton")
                k = [0]

                def nl(ins):
                    k[0] += 1
                    ins.then_inc(step, 1)
                    dve.wait_ge(step, b * N + k[0])
                va = newt[:, 0, :]
                nl(v.tensor_scalar(va, mv[:, 0, :, 1], LN_EPS, None, ALU.add))
                nl(v.tensor_scalar(newt_i[:, :], va.bitcast(I32), 1, None, ALU.arith_shift_right))
                nl(v.tensor_scalar(newt[:, 1, :].bitcast(I32), newt_i[:, :], -1.0, float(0x5F3759DF),
                                   ALU.mult, ALU.add))
                cur = 1
                for it in range(3):
                    if it == 1 and ff:
                        add_ff(b - 1, 1)
                    y = newt[:, cur, :]
                    nxt = 3 - cur
                    nl(v.tensor_tensor(newt[:, 3, :], y, y, ALU.mult))
                    nl(v.scalar_tensor_tensor(newt[:, 4, :], newt[:, 3, :], -0.5, va, ALU.mult, ALU.mult))
                    nl(v.scalar_tensor_tensor(newt[:, nxt, :], newt[:, 4, :], 1.5, y, ALU.add, ALU.mult))
                    cur = nxt
                assert k[0] == N
                for h in range(2):
                    free_wait(dve, s("bt_done"), 2 * b + h - 1)
                    for t in range(GT):
                        i = h * GT + t
                        last = v.tensor_scalar(bb[:, h, t, :], x1[:, h, t, :], mv[:, 0, i, 0:1],
                                               newt[:, cur, i:i + 1], ALU.subtract, ALU.mult)
                    last.then_inc(s("bb_ready"), 1)

            def split_b(b, h):
                gi = 2 * b + h
                dve.wait_ge(s("bT_ready"), gi + 1)
                free_wait(dve, s("w1_done"), (gi - 1) * NF)
                v.tensor_tensor(bT_p[:, h, 1, :], banks[:, 7 - h, :], bT_p[:, h, 0, :], ALU.subtract)\
                    .then_inc(s("bT_split"), 1)

            def add_x1(b):
                xs_ = x_all[:, bass.ds(b * TPB, TPB), :].rearrange("p t d -> p (t d)")
                v.tensor_tensor(xs_, xs_, x1[:, :, :, :].rearrange("p h t d -> p (h t d)"), ALU.add)\
                    .then_inc(s("x1_added"), 1)

            def low_e(e):
                dve.wait_ge(s("eh_ready"), e + 1)
                v.tensor_tensor(ew1_p[:, E_LOW, e, :], ew1_raw[:, e * H2:(e + 1) * H2], ew1_p[:, E_HIGH, e, :],
                                ALU.subtract).then_inc(s("el_ready"), 1)

            def low_x(n, u):
                dve.wait_ge(s("xT_ready"), n + 1)
                free_wait(dve, s("d1_done"), n - NX + 1)
                v.tensor_tensor(xT_p[u % NX][1], banks[:, u % 2, 0:P], xT_p[u % NX][0], ALU.subtract)\
                    .then_inc(s("xT_split"), 1)

            def begin_experts():
                dve.wait_ge(wide_in, 32)
                v.tensor_scalar(eb1_s[:, :, FE:H2], eb1_s[:, :, FE:H2], 1.0, None, ALU.add).then_inc(s("plus_one"), 1)
                for u in range(2):
                    low_x(u, u)

            def dve_step3(b, ff, att, proj, more=None, experts=()):
                if att and ff:
                    mask_kv(b + 1)
                if att:
                    for h in range(2):
                        divide(b + 1, h)
                if ff:
                    add_ff(b, 0)
                if proj:
                    for h in range(2):
                        split_a(b + 2, h)
                for e in experts:
                    low_e(e)
                if more:
                    more()
                if att:
                    after_attention(b + 1)
                    second_norm(b + 1, ff)
                elif ff:
                    add_ff(b, 1)
                if proj:
                    feature_q(b + 2, 0)
                    feature_q(b + 2, 1)
                if att:
                    split_b(b + 1, 0)
                if proj:
                    for h in range(2):
                        feature_k(b + 2, h)
                if att:
                    split_b(b + 1, 1)
                    add_x1(b + 1)

            dve_step3(-1, False, True, True, lambda: tables(0))
            dve_step3(0, True, True, True, lambda: tables(1))
            with dve.Fori(1, NBATCH - 2) as b:
                dve_step3(b, True, True, True)
            dve_step3(NBATCH - 2, True, True, False, None, range(NE // 2))
            dve_step3(NBATCH - 1, True, False, False, begin_experts, range(NE // 2, NE))

            def add_bias(n, u, e):
                dve.wait_ge(s("d1_done"), n + 1)
                free_wait(dve, s("sg_ready"), n - 1)
                v.tensor_tensor(hb[u % 2], banks[:, 2 + u % 2, :],
                                eb1_s[:, bass.ds(e, 1), :].rearrange("p a f -> p (a f)"), ALU.add)\
                    .then_inc(s("hb_ready"), 1)

            def limit(n, u):
                dve.wait_ge(s("hb_ready"), n + 1)
                v.tensor_scalar(vm[u % 2], hb[u % 2][:, FE:H2], 1.0 + LIMIT, 1.0 - LIMIT, ALU.min, ALU.max)\
                    .then_inc(s("vm_ready"), 1)

            def gate_up(n, u):
                dve.wait_ge(s("sg_ready"), n + 1)
                dve.wait_ge(s("vm_ready"), n + 1)
                free_wait(dve, s("ht_done"), n - 1)
                v.scalar_tensor_tensor(hs[u % 2], sg[u % 2], GATED_LIMIT, vm[u % 2], ALU.min, ALU.mult)\
                    .then_inc(s("hs_ready"), 1)

            dve.wait_ge(s("tile_x_ready"), 2)
            dve.wait_ge(s("plus_one"), 1)

            def dve_block(i, steps):
                _, ev = nc.values_load_multi_w_load_instructions(
                    tile_x[0:1, bass.ds(i * UN + EP, UN)] if not isinstance(i, int)
                    else tile_x[0:1, i * UN + EP:i * UN + EP + UN],
                    engines=[DVE_E], min_val=0, max_val=NE - 1,
                    skip_runtime_bounds_check_because="written as min(count, NE - 1)")
                for u in steps:
                    n = i * UN + u
                    known = isinstance(i, int)
                    if not known or n < NM:
                        add_bias(n, u, ev[u])
                    if not known or n + 2 < NM:
                        low_x(n + 2, (u + 2) % UN)
                    if not known or n < NM:
                        limit(n, u)
                    if not known or 1 <= n < NM + 1:
                        gate_up(n - 1, (u - 1) % UN)

            dve_block(0, range(UN))
            with dve.Fori(1, NM // UN) as i:
                dve_block(i, range(UN))
            dve_block(NM // UN, range(NM % UN + 1))

            def combine(b):
                dve.wait_ge(y_in[0][b], 16)
                xb = x_all[:, b * TPB:(b + 1) * TPB, :]
                v.tensor_tensor(xb, xb, yc[0][:, b * TPB:(b + 1) * TPB, :], ALU.add).then_inc(s("comb_half"), 1)
                dve.wait_ge(s("comb_half"), b + 1)
                dve.wait_ge(y_in[1][b], 16)
                v.tensor_tensor(xb, xb, yc[1][:, b * TPB:(b + 1) * TPB, :], ALU.add).then_inc(s("comb_done"), 1)
            for b in range(NBATCH):
                combine(b)

        @block.tensor
        def _(pe):
            mm = nc.tensor.matmul
            tr = nc.tensor.transpose

            PARTS = ((0, 0), (1, 0), (0, 1))

            pe.wait_ge(w_in, 16 * 6)
            units = [(wqkv_raw, 0, BE1)] + [(w1_raw, f, BE2) for f in range(NF)] + \
                [(wqkv_raw, 1, BE1), (wqkv_raw, 2, BE1)]
            for i, (w_, c, be) in enumerate(units):
                last = mm(banks[:, 7, i:i + 1], w_[:, c * P:(c + 1) * P], vec_raw[:, be:be + 1],
                          start=True, stop=True)
            last.then_inc(s("fold_done"), 1)
            pe.wait_ge(s("c_ident"), 1)

            def trans_a(b, h):
                pe.wait_ge(s("a_ready"), 2 * b + h + 1)
                free_wait(pe, s("aT_ready"), 2 * b + h - 1)
                for t in range(GT):
                    last = tr(banks[:, h, t * P:(t + 1) * P], a_t[:, h, t, :], ident[:, :])
                last.then_inc(s("t_done"), 1)

            def gate(b, h):
                pe.wait_ge(s("aT_ready"), 2 * b + h + 1)
                free_wait(pe, s("gates_ready"), b)
                for t in range(GT):
                    last = mm(banks[:, 2 + h, t * NE:(t + 1) * NE], aT_g[:, h, t * P:(t + 1) * P], wg_s[:, :],
                              start=True, stop=True)
                last.then_inc(s("gate_done"), 1)

            def pe_norm(b):
                for h in range(2):
                    trans_a(b, h)
                for h in range(2):
                    gate(b, h)
            pe_norm(0)
            pe.wait_ge(s("parts_ready"), 1)
            for c in range(NB):
                bank = 6 if c < 4 else c // 4 + 3
                last = tr(banks[0:3, bank, c % 4 * P:(c % 4 + 1) * P], bparts[:, c, :], ident[:, :])
            last.then_inc(s("parts_done"), 1)
            with pe.Fori(1, NBATCH) as b:
                pe_norm(b)

            def project_q(b, h):
                gi = 2 * b + h
                pe.wait_ge(s("aT_split"), gi + 1)
                if h == 0:
                    free_wait(pe, s("kvz_ready"), b)
                else:
                    free_wait(pe, s("res_done"), 2 * (b - 1))
                for i, (w_, x_) in enumerate(PARTS):
                    last = mm(banks[:, 4 + h, :], wqkv_p[:, w_, 0:D], aT_p[:, h, x_, :], start=(i == 0), stop=(i == 2))
                last.then_inc(s("q_done"), 1)

            def project_kv(b, h, halves=(0, 1)):
                gi = 2 * b + h
                free_wait(pe, s("x1_ready"), gi - 1)
                for a_ in halves:
                    bank = 2 * h + a_
                    mm(banks[:, bank, :], ones_b[0:3, :], bias_kv[0:3, :, :].rearrange("p c n -> p (c n)"),
                       start=True, stop=False)
                    for c in range(2):
                        t = 2 * a_ + c
                        for i, (w_, x_) in enumerate(PARTS):
                            last = mm(banks[:, bank, c * 2 * D:(c + 1) * 2 * D], aT_p[:, h, x_, t * P:(t + 1) * P],
                                      wqkv_p[:, w_, D:3 * D], start=False, stop=(c == 1 and i == 2))
                if 1 in halves:
                    last.then_inc(s("kv_done"), 1)

            def kv_acc(b):
                pe.wait_ge(s("kf_ready"), 2 * b + 2)
                pe.wait_ge(s("v_ready"), 2 * b + 2)
                for h in range(2):
                    for t in range(GT):
                        last = mm(banks[:, 4, 0:D + 1], kf[:, h, t, :], vv[:, h, t, :],
                                  start=(h == 0 and t == 0), stop=(h == 1 and t == GT - 1))
                last.then_inc(s("kvacc_done"), 1)

            def attend(b, h):
                gi = 2 * b + h
                pe.wait_ge(s("kvz_ready"), b + 1)
                pe.wait_ge(s("qf_ready"), gi + 1)
                for t in range(GT):
                    last = mm(banks[:, 2 * h + t // 2, (t % 2) * 256:(t % 2) * 256 + D + NH],
                              qf[:, h, t * P:(t + 1) * P], kvz[:, :], start=True, stop=True)
                last.then_inc(s("y_mm_done"), 1)

            def trans_y(b, h):
                pe.wait_ge(s("ynorm_done"), 2 * b + h + 1)
                for t in range(GT):
                    last = tr(banks[:, 2 * h, t * P:(t + 1) * P], ysb[:, h, t, :], ident[:, :])
                last.then_inc(s("yt_done"), 1)

            def out_proj(b, h):
                pe.wait_ge(s("yT_ready"), 2 * b + h + 1)
                mm(banks[:, 2 * h + 1, :], ones_b[0:3, :], bias_o[0:3, :, :].rearrange("p c n -> p (c n)"),
                   start=True, stop=False)
                for t in range(GT):
                    last = mm(banks[:, 2 * h + 1, t * D:(t + 1) * D], yTs[:, h, t * P:(t + 1) * P], wo_s[:, :],
                              start=False, stop=(t == GT - 1))
                last.then_inc(s("o_done"), 1)

            def trans_b(b, h):
                pe.wait_ge(s("bb_ready"), 2 * b + h + 1)
                if isinstance(b, int) and b == 0:
                    pe.wait_ge(s("slots_ready"), 2)
                free_wait(pe, s("gelu_done"), 2 * b * NF)
                for t in range(GT):
                    last = tr(banks[:, 7 - h, t * P:(t + 1) * P], bb[:, h, t, :], ident[:, :])
                last.then_inc(s("bt_done"), 1)

            def ff_up(b, h, fs, att):
                gi = 2 * b + h
                for f in fs:
                    if h == 0 and f == 0:
                        if att:
                            pe.wait_ge(s("qf_ready"), 2 * b + 4)
                        else:
                            pe.wait_ge(s("res_done"), gi)
                        pe.wait_ge(s("bT_ready"), gi + 1)
                    else:
                        pe.wait_ge(s("bT_split"), 2 * b + (1 if h == 0 and f == 1 else 2))
                        free_wait(pe, s("gelu_done"), gi * NF + f - 1)
                    for i, (w_, x_) in enumerate(PARTS):
                        if h == 0 and f == 0 and i == 2:
                            pe.wait_ge(s("bT_split"), gi + 1)
                        last = mm(banks[:, UP_BANKS[h][f], :], w1_p[:, w_, f * P:(f + 1) * P], bT_p[:, h, x_, :],
                                  start=(i == 0), stop=(i == 2))
                    last.then_inc(s("w1_done"), 1)

            def ff_down(b, h):
                gi = 2 * b + h
                if h == 0:
                    pe.wait_ge(s("gelu_done"), gi * NF + 1)
                else:
                    pe.wait_ge(s("res_done"), gi)
                mm(banks[:, 5, :], ones_b[0:3, :], bias_2[0:3, :, :].rearrange("p c n -> p (c n)"),
                   start=True, stop=False)
                for f in range(NF):
                    pe.wait_ge(s("gelu_done"), gi * NF + f + 1)
                    for t in range(GT):
                        last = mm(banks[:, 5, t * D:(t + 1) * D], hh[:, f, t * P:(t + 1) * P], w2_s[:, f, :],
                                  start=False, stop=(f == NF - 1 and t == GT - 1))
                last.then_inc(s("w2_done"), 1)

            def pe_step3(b, ff, att, proj):
                last_step = not att
                if ff:
                    ff_up(b, 0, range(NF // 2), att)
                if ff and att:
                    kv_acc(b + 1)
                if ff:
                    ff_up(b, 0, range(NF // 2, NF), att)
                if att:
                    for h in range(2):
                        attend(b + 1, h)
                if ff:
                    ff_down(b, 0)
                if att:
                    for h in range(2):
                        trans_y(b + 1, h)
                if ff:
                    ff_up(b, 1, range(NF), att)
                if att:
                    for h in range(2):
                        out_proj(b + 1, h)
                if last_step:
                    for u in range(2):
                        pe.wait_ge(rows_in[u], 16)
                        tr(banks[:, u, 0:P], xg[u][:, 0:D], ident[:, :]).then_inc(s("xt_done"), 1)
                if ff:
                    ff_down(b, 1)
                if proj:
                    project_q(b + 2, 0)
                    project_kv(b + 2, 0)
                    project_q(b + 2, 1)
                    project_kv(b + 2, 1, (0,))
                if att:
                    trans_b(b + 1, 0)
                if proj:
                    project_kv(b + 2, 1, (1,))
                if att:
                    trans_b(b + 1, 1)

            def rank(k):
                pe.wait_ge(s("oneh_ready"), k + 1)
                free_wait(pe, s("slots_ready"), k)
                free_wait(pe, s("totals_ready"), k)
                oh = oneh_b[k][:, :, :].rearrange("p c e -> p (c e)")
                mm(banks[:, 6, :], upper_b[:, :], oh, start=True, stop=True)
                mm(banks[:, 7, :], ones_b[:, :], oh, start=True, stop=True).then_inc(s("rank_done"), 1)

            pe.wait_ge(s("c_upper"), 1)
            pe.wait_ge(s("c_ones"), 1)
            pe.wait_ge(s("ws_ready"), 2)
            pe.wait_ge(s("bias_ready"), 4)
            pe.wait_ge(s("gates_ready"), NBATCH)
            pe.wait_ge(s("c_vv"), 1)
            rank(0)
            project_q(0, 0)
            project_kv(0, 0)
            project_q(0, 1)
            project_kv(0, 1)
            rank(1)
            kv_acc(0)
            pe_step3(-1, False, True, True)
            pe_step3(0, True, True, True)
            with pe.Fori(1, NBATCH - 2) as b:
                pe_step3(b, True, True, True)
            pe_step3(NBATCH - 2, True, True, False)
            pe_step3(NBATCH - 1, True, False, False)

            pe.wait_ge(s("tile_x_ready"), 2)
            pe.wait_ge(wide_in, 32)
            pe.wait_ge(s("el_ready"), NE)

            def pe_block(i, steps):
                known = isinstance(i, int)
                _, ev = nc.values_load_multi_w_load_instructions(
                    tile_x[0:1, i * UN:i * UN + UN + EP] if known else tile_x[0:1, bass.ds(i * UN, UN + EP)],
                    engines=[PE_E], min_val=0, max_val=NE - 1,
                    skip_runtime_bounds_check_because="written as min(count, NE - 1)")
                for u in steps:
                    n = i * UN + u
                    m, mu = n - 3, (u - 3) % UN
                    if known and n == 3:
                        pe.wait_ge(s("res_done"), NG)
                    if not known or n >= 3:
                        pe.wait_ge(s("hs_ready"), m + 1)
                        free_wait(pe, s("hT_ready"), m - 1)
                        for c in range(2):
                            last = tr(banks[:, 4 + mu % 2, c * P:(c + 1) * P], hs[mu % 2][:, c * P:(c + 1) * P],
                                      ident[:, :])
                        last.then_inc(s("ht_done"), 1)
                    if not known or n + 2 < NM:
                        xu = (u + 2) % UN
                        pe.wait_ge(rows_in[xu], 16 * (i + (u + 2) // UN + 1))
                        free_wait(pe, s("xT_split"), n + 1)
                        tr(banks[:, xu % 2, 0:P], xg[xu][:, 0:D], ident[:, :]).then_inc(s("xt_done"), 1)
                    if not known or n < NM:
                        pe.wait_ge(s("xT_split"), n + 1)
                        free_wait(pe, s("hb_ready"), n - 1)
                        for q, (w_, x_) in enumerate(((E_HIGH, 0), (E_LOW, 0), (E_HIGH, 1))):
                            last = mm(banks[:, 2 + u % 2, :], xT_p[u % NX][x_],
                                      ew1_p[:, w_, bass.ds(ev[EP + u], 1), :].rearrange("p a f -> p (a f)"),
                                      start=(q == 0), stop=(q == 2))
                        last.then_inc(s("d1_done"), 1)
                    if not known or n >= 3:
                        pe.wait_ge(s("hT_ready"), m + 1)
                        free_wait(pe, s("y_ready"), m - 1)
                        e = ev[EP + u - 3]
                        for c in range(2):
                            last = mm(banks[:, 6 + mu % 2, 0:D], hTs[mu % 2][:, c * P:(c + 1) * P],
                                      ew2_s[:, bass.ds(e, 1), c, :].rearrange("p a d -> p (a d)"),
                                      start=(c == 0), stop=False)
                        last = mm(banks[:, 6 + mu % 2, 0:D], ones_b[0:3, :],
                                  bias_e[0:3, bass.ds(e, 1), :].rearrange("p a d -> p (a d)"), start=False, stop=True)
                        last.then_inc(s("d2_done"), 1)

            pe_block(0, range(UN))
            with pe.Fori(1, NM // UN) as i:
                pe_block(i, range(UN))
            pe_block(NM // UN, range(NM % UN + 3))


_OUT = ((8, 1024, 128), "float32")


def kernel(**inputs):
    import numpy as np
    import concourse.bacc as bacc
    from concourse.bass_utils import run_bass_kernel_spmd

    t = {k: np.asarray(v) for k, v in inputs.items()}
    E, H2, D = t["L0_ffn_dense_1_w"].shape
    F = H2 // 2
    ew1 = t["L0_ffn_dense_1_w"].reshape(E, F, 2, D).transpose(3, 0, 2, 1)
    eb1 = t["L0_ffn_dense_1_b"].reshape(E, F, 2).transpose(0, 2, 1)
    ew2 = t["L0_ffn_dense_2_w"].reshape(E, D, 2, F // 2).transpose(3, 0, 2, 1).reshape(F // 2, E, 2 * D)
    a = {k[len("L0_attn_"):]: v for k, v in t.items() if k.startswith("L0_attn_")}
    vecs = np.stack([a["g1"], a["be1"], a["g2"], a["be2"], a["qkv_b"][:D], *a["b1"].reshape(-1, D),
                     *a["qkv_b"][D:].reshape(2, D), a["out_b"], a["b2"], *t["L0_ffn_dense_2_b"]], axis=1)
    arrays = {"src": a["src"], "qkv_w": a["qkv_w"], "out_w": a["out_w"], "w1": a["w1"], "w2": a["w2"],
              "gate_w": t["L0_ffn_gate_w"], "vecs": vecs, "ew1": ew1, "eb1": eb1, "ew2": ew2}
    nc = bacc.Bacc("TRN2", target_bir_lowering=False, num_devices=1)
    args, feed = [], {}
    for n, v in arrays.items():
        v = np.ascontiguousarray(v)
        feed["in_" + n] = v
        args.append(nc.dram_tensor("in_" + n, v.shape, mybir.dt.from_np(v.dtype), kind="ExternalInput").ap())
    args.append(nc.dram_tensor("out_0", _OUT[0], F32, kind="ExternalOutput").ap())
    layer_kernel(nc, *args)
    r = run_bass_kernel_spmd(nc, [feed], core_ids=[0])
    return r.results[0]["out_0"]
```
